# Optimizing a Trainium2 kernel written in Bass

```python
import numpy as np
import jax
import jax.numpy as jnp

def _softmax(x, axis=-1):
    return jax.nn.softmax(x, axis=axis)

def _gelu(x):
    return jax.nn.gelu(x, approximate=True)

def _silu(x):
    return jax.nn.silu(x)

def _sigmoid(x):
    return jax.nn.sigmoid(x)

def _layernorm(x, axis=-1, eps=1e-05):
    m = jnp.mean(x, axis=axis, keepdims=True)
    v = jnp.var(x, axis=axis, keepdims=True)
    return (x - m) / jnp.sqrt(v + eps)

def _scatter_add(tgt, idx, src, axis=0):
    return tgt.at[idx].add(src)

def _segment_sum(src, seg, n):
    return jax.ops.segment_sum(src, seg, n)
kernel_name = 'mk_perceiver_d2_seqx_r8_ce5e40'

def setup_inputs(seed: int=0):
    np.random.seed(seed)
    _w = jnp.asarray

    def _rec_inputs():
        import jax
        import jax.numpy as jnp
        _rk = jax.random.key(seed)
        x = 7.22e-05 + 1 * jax.random.normal(jax.random.fold_in(_rk, 1), (8, 64, 256), jnp.float32)
        _lenS = 64 - jax.random.randint(jax.random.fold_in(_rk, 7), (8,), 0, max(1, 64 // 4) + 1, jnp.int32)
        _lenS2 = 128 - jax.random.randint(jax.random.fold_in(_rk, 8), (8,), 0, max(1, 128 // 4) + 1, jnp.int32)
        _ctx_2048P = jax.random.normal(jax.random.fold_in(_rk, 11), (8, 16, 256), jnp.float32)
        _ctx_2048c = jax.random.dirichlet(jax.random.fold_in(_rk, 511), 0.3 * jnp.ones((16,), jnp.float32), (8, 128))
        _ctx_2048t = jnp.einsum('bsk,bkd->bsd', _ctx_2048c, _ctx_2048P)
        _ctx_2048t = _ctx_2048t * jax.lax.rsqrt(jnp.mean(jnp.square(_ctx_2048t)) + 1e-12) * 0.953939
        ctx_2048 = -0.000514642 + 1.00011 * (_ctx_2048t + 0.3 * jax.random.normal(jax.random.fold_in(_rk, 611), (8, 128, 256), jnp.float32))
        return (x, ctx_2048)
    x, ctx_2048 = _rec_inputs()

    def _L0_xattn_setup():
        import jax, jax.numpy as jnp
        import numpy as np
        D_MODEL = 256
        NUM_HEADS = 16
        HEAD_DIM = D_MODEL // NUM_HEADS

        def _fq_sym(x, axis):
            s = jnp.max(jnp.abs(x), axis=axis, keepdims=True) / 127.0
            s = jnp.maximum(s, 1e-08)
            q = jnp.clip(jnp.round(x / s), -127.0, 127.0) * s
            return x + jax.lax.stop_gradient(q - x)

        def _fq_unsigned(x, axis):
            s = jnp.max(x, axis=axis, keepdims=True) / 255.0
            s = jnp.maximum(s, 1e-08)
            q = jnp.clip(jnp.round(x / s), 0.0, 255.0) * s
            return x + jax.lax.stop_gradient(q - x)
        key = jax.random.key(seed)
        ks = jax.random.split(key, 8)
        B, N, M, C = (2, 256, 64, D_MODEL)
        return {'x': jax.random.normal(ks[0], (B, N, C), jnp.float32), 'cond': jax.random.normal(ks[1], (B, M, C), jnp.float32), 'Wq': jax.random.normal(ks[2], (C, C), jnp.float32) * 0.02, 'bq': jnp.zeros((C,), jnp.float32), 'Wkv': jax.random.normal(ks[3], (C, 2 * C), jnp.float32) * 0.02, 'bkv': jnp.zeros((2 * C,), jnp.float32), 'Wp': jax.random.normal(ks[4], (C, C), jnp.float32) * 0.02, 'bp': jnp.zeros((C,), jnp.float32)}
    _L0_xattn_all = _L0_xattn_setup()
    _L0_xattn_in = {k: v for k, v in _L0_xattn_all.items() if k in ('Wq', 'bq', 'Wkv', 'bkv', 'Wp', 'bp')}
    del _L0_xattn_all

    def _L0_attn_setup():
        import jax, jax.numpy as jnp
        import numpy as np
        B, T, D = (2, 256, 256)
        H, HD = (16, 128)
        HHD = HD // 2
        SCALE = 1.0 / np.sqrt(HHD).astype(np.float32)
        key = jax.random.key(seed)
        ks = jax.random.split(key, 6)
        s = 1.0 / np.sqrt(D).astype(np.float32)
        return {'x': jax.random.normal(ks[0], (B, T, D), jnp.float32), 'Wq': jax.random.normal(ks[1], (D, H * HD), jnp.float32) * s, 'Wk': jax.random.normal(ks[2], (D, H * HD), jnp.float32) * s, 'Wv': jax.random.normal(ks[3], (D, H * HD), jnp.float32) * s, 'Wo': jax.random.normal(ks[4], (H * HD, D), jnp.float32) * s, 'lambda_init': jnp.full((H,), -0.2, jnp.float32)}
    _L0_attn_all = _L0_attn_setup()
    _L0_attn_in = {k: v for k, v in _L0_attn_all.items() if k in ('Wq', 'Wk', 'Wv', 'Wo', 'lambda_init')}
    del _L0_attn_all

    def _L0_ffn_setup():
        import jax, jax.numpy as jnp
        import numpy as np
        H = 256
        E = 8
        TOPK = 2
        I_MOE = 128
        I_SH = 512

        def _silu_and_mul(gu):
            g, u = jnp.split(gu, 2, axis=-1)
            return jax.nn.silu(g) * u
        key = jax.random.key(seed)
        ks = jax.random.split(key, 6)
        s = lambda *sh: 1.0 / np.sqrt(sh[-2])
        hidden_states = jax.random.normal(ks[0], (2, 128, H), dtype=jnp.float32)
        w_gate = jax.random.normal(ks[1], (H, E), dtype=jnp.float32) * (1.0 / np.sqrt(H))
        w_gate_up = jax.random.normal(ks[2], (E, H, 2 * I_MOE), dtype=jnp.float32) * (1.0 / np.sqrt(H))
        w_down = jax.random.normal(ks[3], (E, I_MOE, H), dtype=jnp.float32) * (1.0 / np.sqrt(I_MOE))
        w_sh_gate_up = jax.random.normal(ks[4], (H, 2 * I_SH), dtype=jnp.float32) * (1.0 / np.sqrt(H))
        w_sh_down = jax.random.normal(ks[5], (I_SH, H), dtype=jnp.float32) * (1.0 / np.sqrt(I_SH))
        return {'hidden_states': hidden_states, 'w_gate': w_gate, 'w_gate_up': w_gate_up, 'w_down': w_down, 'w_sh_gate_up': w_sh_gate_up, 'w_sh_down': w_sh_down}
    _L0_ffn_all = _L0_ffn_setup()
    _L0_ffn_in = {k: v for k, v in _L0_ffn_all.items() if k in ('w_gate', 'w_gate_up', 'w_down', 'w_sh_gate_up', 'w_sh_down')}
    del _L0_ffn_all

    def _L1_xattn_setup():
        import jax, jax.numpy as jnp
        import numpy as np
        DIM = 256
        H = 16
        D = 128
        INNER = H * D
        N_IMG = 257
        EPS = 1e-06

        def rms_norm(x, scale, eps=EPS):
            ms = jnp.mean(jnp.square(x), axis=-1, keepdims=True)
            return x * jax.lax.rsqrt(ms + eps) * scale

        def sdpa(q, k, v):
            scale = 1.0 / jnp.sqrt(jnp.asarray(D, q.dtype))
            scores = jnp.einsum('bshd,blhd->bhsl', q, k) * scale
            attn = jax.nn.softmax(scores, axis=-1)
            return jnp.einsum('bhsl,blhd->bshd', attn, v)
        key = jax.random.key(seed)
        ks = jax.random.split(key, 16)
        std = 1.0 / np.sqrt(DIM)
        inp = {'x': jax.random.normal(ks[0], (2, 512, DIM), jnp.float32), 'context': jax.random.normal(ks[1], (2, 769, DIM), jnp.float32), 'q_w': jax.random.normal(ks[2], (DIM, INNER), jnp.float32) * std, 'q_b': jnp.zeros((INNER,), jnp.float32), 'k_w': jax.random.normal(ks[3], (DIM, INNER), jnp.float32) * std, 'k_b': jnp.zeros((INNER,), jnp.float32), 'v_w': jax.random.normal(ks[4], (DIM, INNER), jnp.float32) * std, 'v_b': jnp.zeros((INNER,), jnp.float32), 'ki_w': jax.random.normal(ks[5], (DIM, INNER), jnp.float32) * std, 'ki_b': jnp.zeros((INNER,), jnp.float32), 'vi_w': jax.random.normal(ks[6], (DIM, INNER), jnp.float32) * std, 'vi_b': jnp.zeros((INNER,), jnp.float32), 'o_w': jax.random.normal(ks[7], (INNER, DIM), jnp.float32) * std, 'o_b': jnp.zeros((DIM,), jnp.float32), 'nq_s': jnp.ones((INNER,), jnp.float32), 'nkt_s': jnp.ones((INNER,), jnp.float32), 'nki_s': jnp.ones((INNER,), jnp.float32)}
        return inp
    _L1_xattn_all = _L1_xattn_setup()
    _L1_xattn_in = {k: v for k, v in _L1_xattn_all.items() if k in ('q_w', 'q_b', 'k_w', 'k_b', 'v_w', 'v_b', 'ki_w', 'ki_b', 'vi_w', 'vi_b', 'o_w', 'o_b', 'nq_s', 'nkt_s', 'nki_s')}
    del _L1_xattn_all

    def _L1_attn_setup():
        import jax, jax.numpy as jnp
        import numpy as np
        N_HEAD = 16
        LCOMP = 128
        ROPE_THETA = 10000.0

        def _apply_rope(x):
            d = x.shape[-1]
            T = x.shape[-2]
            half = d // 2
            pos = jnp.arange(T, dtype=jnp.float32)
            inv_freq = ROPE_THETA ** (-jnp.arange(half, dtype=jnp.float32) / half)
            ang = pos[:, None] * inv_freq[None, :]
            cos = jnp.repeat(jnp.cos(ang), 2, axis=-1).astype(x.dtype)
            sin = jnp.repeat(jnp.sin(ang), 2, axis=-1).astype(x.dtype)
            x_even = x[..., ::2]
            x_odd = x[..., 1::2]
            rot = jnp.stack((-x_odd, x_even), axis=-1).reshape(x.shape)
            return x * cos + rot * sin
        key = jax.random.key(seed)
        ks = jax.random.split(key, 4)
        B, T, C = (2, 256, 256)
        s = 0.02
        return {'x': jax.random.normal(ks[0], (B, T, C), dtype=jnp.float32), 'W_latent': jax.random.normal(ks[1], (C, LCOMP), dtype=jnp.float32) * s, 'b_latent': jnp.zeros((LCOMP,), dtype=jnp.float32), 'W_d': jax.random.normal(ks[2], (C, N_HEAD * LCOMP), dtype=jnp.float32) * s, 'b_d': jnp.zeros((N_HEAD * LCOMP,), dtype=jnp.float32), 'W_proj': jax.random.normal(ks[3], (N_HEAD * LCOMP, C), dtype=jnp.float32) * s, 'b_proj': jnp.zeros((C,), dtype=jnp.float32)}
    _L1_attn_all = _L1_attn_setup()
    _L1_attn_in = {k: v for k, v in _L1_attn_all.items() if k in ('W_latent', 'b_latent', 'W_d', 'b_d', 'W_proj', 'b_proj')}
    del _L1_attn_all

    def _L1_ffn_setup():
        import jax, jax.numpy as jnp
        import numpy as np
        NUM_EXPERTS = 8
        TOP_K = 2
        HIDDEN = 256
        INTER = 704
        B, S = (4, 256)
        key = jax.random.key(seed)
        ks = jax.random.split(key, 5)
        scale_h = 1.0 / np.sqrt(HIDDEN)
        scale_i = 1.0 / np.sqrt(INTER)
        return {'hidden_states': jax.random.normal(ks[0], (B, S, HIDDEN), dtype=jnp.float32), 'Wg': jax.random.normal(ks[1], (NUM_EXPERTS, HIDDEN), dtype=jnp.float32) * scale_h, 'w1': jax.random.normal(ks[2], (NUM_EXPERTS, INTER, HIDDEN), dtype=jnp.float32) * scale_h, 'w3': jax.random.normal(ks[3], (NUM_EXPERTS, INTER, HIDDEN), dtype=jnp.float32) * scale_h, 'w2': jax.random.normal(ks[4], (NUM_EXPERTS, HIDDEN, INTER), dtype=jnp.float32) * scale_i}
    _L1_ffn_all = _L1_ffn_setup()
    _L1_ffn_in = {k: v for k, v in _L1_ffn_all.items() if k in ('Wg', 'w1', 'w3', 'w2')}
    del _L1_ffn_all
    return {'x': x, 'ctx_2048': ctx_2048, 'L0_xattn_Wq': _L0_xattn_in['Wq'], 'L0_xattn_bq': _L0_xattn_in['bq'], 'L0_xattn_Wkv': _L0_xattn_in['Wkv'], 'L0_xattn_bkv': _L0_xattn_in['bkv'], 'L0_xattn_Wp': _L0_xattn_in['Wp'], 'L0_xattn_bp': _L0_xattn_in['bp'], 'L0_attn_Wq': _L0_attn_in['Wq'], 'L0_attn_Wk': _L0_attn_in['Wk'], 'L0_attn_Wv': _L0_attn_in['Wv'], 'L0_attn_Wo': _L0_attn_in['Wo'], 'L0_attn_lambda_init': _L0_attn_in['lambda_init'], 'L0_ffn_w_gate': _L0_ffn_in['w_gate'], 'L0_ffn_w_gate_up': _L0_ffn_in['w_gate_up'], 'L0_ffn_w_down': _L0_ffn_in['w_down'], 'L0_ffn_w_sh_gate_up': _L0_ffn_in['w_sh_gate_up'], 'L0_ffn_w_sh_down': _L0_ffn_in['w_sh_down'], 'L1_xattn_q_w': _L1_xattn_in['q_w'], 'L1_xattn_q_b': _L1_xattn_in['q_b'], 'L1_xattn_k_w': _L1_xattn_in['k_w'], 'L1_xattn_k_b': _L1_xattn_in['k_b'], 'L1_xattn_v_w': _L1_xattn_in['v_w'], 'L1_xattn_v_b': _L1_xattn_in['v_b'], 'L1_xattn_ki_w': _L1_xattn_in['ki_w'], 'L1_xattn_ki_b': _L1_xattn_in['ki_b'], 'L1_xattn_vi_w': _L1_xattn_in['vi_w'], 'L1_xattn_vi_b': _L1_xattn_in['vi_b'], 'L1_xattn_o_w': _L1_xattn_in['o_w'], 'L1_xattn_o_b': _L1_xattn_in['o_b'], 'L1_xattn_nq_s': _L1_xattn_in['nq_s'], 'L1_xattn_nkt_s': _L1_xattn_in['nkt_s'], 'L1_xattn_nki_s': _L1_xattn_in['nki_s'], 'L1_attn_W_latent': _L1_attn_in['W_latent'], 'L1_attn_b_latent': _L1_attn_in['b_latent'], 'L1_attn_W_d': _L1_attn_in['W_d'], 'L1_attn_b_d': _L1_attn_in['b_d'], 'L1_attn_W_proj': _L1_attn_in['W_proj'], 'L1_attn_b_proj': _L1_attn_in['b_proj'], 'L1_ffn_Wg': _L1_ffn_in['Wg'], 'L1_ffn_w1': _L1_ffn_in['w1'], 'L1_ffn_w3': _L1_ffn_in['w3'], 'L1_ffn_w2': _L1_ffn_in['w2']}

def reference(x, ctx_2048, L0_xattn_Wq, L0_xattn_bq, L0_xattn_Wkv, L0_xattn_bkv, L0_xattn_Wp, L0_xattn_bp, L0_attn_Wq, L0_attn_Wk, L0_attn_Wv, L0_attn_Wo, L0_attn_lambda_init, L0_ffn_w_gate, L0_ffn_w_gate_up, L0_ffn_w_down, L0_ffn_w_sh_gate_up, L0_ffn_w_sh_down, L1_xattn_q_w, L1_xattn_q_b, L1_xattn_k_w, L1_xattn_k_b, L1_xattn_v_w, L1_xattn_v_b, L1_xattn_ki_w, L1_xattn_ki_b, L1_xattn_vi_w, L1_xattn_vi_b, L1_xattn_o_w, L1_xattn_o_b, L1_xattn_nq_s, L1_xattn_nkt_s, L1_xattn_nki_s, L1_attn_W_latent, L1_attn_b_latent, L1_attn_W_d, L1_attn_b_d, L1_attn_W_proj, L1_attn_b_proj, L1_ffn_Wg, L1_ffn_w1, L1_ffn_w3, L1_ffn_w2):
    import jax
    import jax.numpy as jnp

    def _L0_xattn_ref(x, cond, Wq, bq, Wkv, bkv, Wp, bp):
        import jax, jax.numpy as jnp
        import numpy as np
        D_MODEL = 256
        NUM_HEADS = 16
        HEAD_DIM = D_MODEL // NUM_HEADS

        def _fq_sym(x, axis):
            s = jnp.max(jnp.abs(x), axis=axis, keepdims=True) / 127.0
            s = jnp.maximum(s, 1e-08)
            q = jnp.clip(jnp.round(x / s), -127.0, 127.0) * s
            return x + jax.lax.stop_gradient(q - x)

        def _fq_unsigned(x, axis):
            s = jnp.max(x, axis=axis, keepdims=True) / 255.0
            s = jnp.maximum(s, 1e-08)
            q = jnp.clip(jnp.round(x / s), 0.0, 255.0) * s
            return x + jax.lax.stop_gradient(q - x)
        B, N, C = x.shape
        H, hd = (NUM_HEADS, HEAD_DIM)
        q = (x @ Wq + bq).reshape(1, B * N, H, hd)
        kv = (cond @ Wkv + bkv).reshape(1, -1, 2, H, hd)
        k, v = (kv[:, :, 0], kv[:, :, 1])
        scale = 1.0 / np.sqrt(hd).astype(np.float32)
        q = jnp.transpose(q * scale, (0, 2, 1, 3))
        k = jnp.transpose(k, (0, 2, 1, 3))
        v = jnp.transpose(v, (0, 2, 1, 3))
        q = _fq_sym(q, axis=-1)
        k = _fq_sym(k, axis=-1)
        v = _fq_sym(v, axis=2)
        attn = jnp.einsum('bhqd,bhkd->bhqk', q, k)
        attn = jax.nn.softmax(attn.astype(jnp.float32), axis=-1)
        attn = _fq_unsigned(attn, axis=-1)
        out = jnp.einsum('bhqk,bhkd->bhqd', attn, v)
        out = jnp.transpose(out, (0, 2, 1, 3)).reshape(B, N, C)
        return out @ Wp + bp

    def _L0_attn_ref(x, Wq, Wk, Wv, Wo, lambda_init):
        import jax, jax.numpy as jnp
        import numpy as np
        B, T, D = (2, 256, 256)
        H, HD = (16, 128)
        HHD = HD // 2
        SCALE = 1.0 / np.sqrt(HHD).astype(np.float32)
        b, t, d = x.shape
        q = (x @ Wq).reshape(b, t, H, HD).transpose(0, 2, 1, 3)
        k = (x @ Wk).reshape(b, t, H, HD).transpose(0, 2, 1, 3)
        v = (x @ Wv).reshape(b, t, H, HD).transpose(0, 2, 1, 3)
        q1, q2 = (q[..., :HHD], q[..., HHD:])
        k1, k2 = (k[..., :HHD], k[..., HHD:])
        scores1 = jnp.einsum('bhtc,bhsc->bhts', q1, k1) * SCALE
        scores2 = jnp.einsum('bhtc,bhsc->bhts', q2, k2) * SCALE
        causal = jnp.tril(jnp.ones((t, t), bool))
        neg_inf = jnp.float32(-jnp.inf)
        scores1 = jnp.where(causal[None, None], scores1, neg_inf)
        scores2 = jnp.where(causal[None, None], scores2, neg_inf)
        attn1 = jax.nn.softmax(scores1, axis=-1)
        attn2 = jax.nn.softmax(scores2, axis=-1)
        lam = jax.nn.sigmoid(lambda_init)[None, :, None, None]
        diff_attn = attn1 - lam * attn2
        out = jnp.einsum('bhts,bhsd->bhtd', diff_attn, v)
        out = out.transpose(0, 2, 1, 3).reshape(b, t, H * HD)
        return out @ Wo

    def _L0_ffn_ref(hidden_states, w_gate, w_gate_up, w_down, w_sh_gate_up, w_sh_down):
        import jax, jax.numpy as jnp
        import numpy as np
        H = 256
        E = 8
        TOPK = 2
        I_MOE = 128
        I_SH = 512

        def _silu_and_mul(gu):
            g, u = jnp.split(gu, 2, axis=-1)
            return jax.nn.silu(g) * u
        orig_shape = hidden_states.shape
        x = hidden_states.reshape(-1, orig_shape[-1])
        router_logits = x @ w_gate
        probs = jax.nn.softmax(router_logits, axis=-1)
        topk_w, topk_ids = jax.lax.top_k(probs, TOPK)
        topk_w = topk_w / jnp.sum(topk_w, axis=-1, keepdims=True)
        combine = jnp.sum(topk_w[..., None] * jax.nn.one_hot(topk_ids, E, dtype=x.dtype), axis=1)
        gu = jnp.einsum('th,ehf->etf', x, w_gate_up)
        act = _silu_and_mul(gu)
        eo = jnp.einsum('eti,eih->eth', act, w_down)
        routed = jnp.einsum('te,eth->th', combine, eo)
        shared = _silu_and_mul(x @ w_sh_gate_up) @ w_sh_down
        return (routed + shared).reshape(orig_shape)

    def _L1_xattn_ref(x, context, q_w, q_b, k_w, k_b, v_w, v_b, ki_w, ki_b, vi_w, vi_b, o_w, o_b, nq_s, nkt_s, nki_s):
        import jax, jax.numpy as jnp
        import numpy as np
        DIM = 256
        H = 16
        D = 128
        INNER = H * D
        N_IMG = 257
        EPS = 1e-06

        def rms_norm(x, scale, eps=EPS):
            ms = jnp.mean(jnp.square(x), axis=-1, keepdims=True)
            return x * jax.lax.rsqrt(ms + eps) * scale

        def sdpa(q, k, v):
            scale = 1.0 / jnp.sqrt(jnp.asarray(D, q.dtype))
            scores = jnp.einsum('bshd,blhd->bhsl', q, k) * scale
            attn = jax.nn.softmax(scores, axis=-1)
            return jnp.einsum('bhsl,blhd->bshd', attn, v)
        B, S, _ = x.shape
        img_ctx = context[:, :N_IMG]
        txt_ctx = context[:, N_IMG:]
        q = rms_norm(x @ q_w + q_b, nq_s).reshape(B, S, H, D)
        k_txt = rms_norm(txt_ctx @ k_w + k_b, nkt_s).reshape(B, -1, H, D)
        v_txt = (txt_ctx @ v_w + v_b).reshape(B, -1, H, D)
        out_txt = sdpa(q, k_txt, v_txt)
        k_img = rms_norm(img_ctx @ ki_w + ki_b, nki_s).reshape(B, -1, H, D)
        v_img = (img_ctx @ vi_w + vi_b).reshape(B, -1, H, D)
        out_img = sdpa(q, k_img, v_img)
        out = (out_txt + out_img).reshape(B, S, INNER)
        return out @ o_w + o_b

    def _L1_attn_ref(x, W_latent, b_latent, W_d, b_d, W_proj, b_proj):
        import jax, jax.numpy as jnp
        import numpy as np
        N_HEAD = 16
        LCOMP = 128
        ROPE_THETA = 10000.0

        def _apply_rope(x):
            d = x.shape[-1]
            T = x.shape[-2]
            half = d // 2
            pos = jnp.arange(T, dtype=jnp.float32)
            inv_freq = ROPE_THETA ** (-jnp.arange(half, dtype=jnp.float32) / half)
            ang = pos[:, None] * inv_freq[None, :]
            cos = jnp.repeat(jnp.cos(ang), 2, axis=-1).astype(x.dtype)
            sin = jnp.repeat(jnp.sin(ang), 2, axis=-1).astype(x.dtype)
            x_even = x[..., ::2]
            x_odd = x[..., 1::2]
            rot = jnp.stack((-x_odd, x_even), axis=-1).reshape(x.shape)
            return x * cos + rot * sin
        B, T, C = x.shape
        kv = x @ W_latent + b_latent
        q = (x @ W_d + b_d).reshape(B, T, N_HEAD, LCOMP).transpose(0, 2, 1, 3)
        q_rot = _apply_rope(q)
        k_rot = _apply_rope(kv)
        scale = 1.0 / np.sqrt(LCOMP)
        att = jnp.einsum('bhtd,bsd->bhts', q_rot, k_rot) * scale
        causal = jnp.tril(jnp.ones((T, T), dtype=bool))
        att = jnp.where(causal[None, None], att, -jnp.inf)
        att = jax.nn.softmax(att, axis=-1)
        y = jnp.einsum('bhts,bsd->bhtd', att, kv)
        y = y.transpose(0, 2, 1, 3).reshape(B, T, N_HEAD * LCOMP)
        return y @ W_proj + b_proj

    def _L1_ffn_ref(hidden_states, Wg, w1, w3, w2):
        import jax, jax.numpy as jnp
        import numpy as np
        NUM_EXPERTS = 8
        TOP_K = 2
        HIDDEN = 256
        INTER = 704
        B, S = (4, 256)
        orig_shape = hidden_states.shape
        x = hidden_states.reshape(-1, HIDDEN)
        T = x.shape[0]
        router_logits = x @ Wg.T
        probs = jax.nn.softmax(router_logits, axis=-1)
        topk_vals, topk_idx = jax.lax.top_k(probs, TOP_K)
        topk_vals = topk_vals / jnp.sum(topk_vals, axis=-1, keepdims=True)
        combine = jnp.zeros((T, NUM_EXPERTS), dtype=x.dtype)
        combine = combine.at[jnp.arange(T)[:, None], topk_idx].add(topk_vals)
        out = jnp.zeros_like(x)
        for e in range(NUM_EXPERTS):
            h = jax.nn.silu(x @ w1[e].T) * (x @ w3[e].T)
            out = out + combine[:, e:e + 1] * (h @ w2[e].T)
        return out.reshape(orig_shape)
    x = x + _L0_xattn_ref(_layernorm(x, axis=-1), ctx_2048, L0_xattn_Wq, L0_xattn_bq, L0_xattn_Wkv, L0_xattn_bkv, L0_xattn_Wp, L0_xattn_bp)
    x = x + _L0_attn_ref(_layernorm(x, axis=-1), L0_attn_Wq, L0_attn_Wk, L0_attn_Wv, L0_attn_Wo, L0_attn_lambda_init)
    x = x + _L0_ffn_ref(_layernorm(x, axis=-1), L0_ffn_w_gate, L0_ffn_w_gate_up, L0_ffn_w_down, L0_ffn_w_sh_gate_up, L0_ffn_w_sh_down)
    x = x + _L1_xattn_ref(_layernorm(x, axis=-1), ctx_2048, L1_xattn_q_w, L1_xattn_q_b, L1_xattn_k_w, L1_xattn_k_b, L1_xattn_v_w, L1_xattn_v_b, L1_xattn_ki_w, L1_xattn_ki_b, L1_xattn_vi_w, L1_xattn_vi_b, L1_xattn_o_w, L1_xattn_o_b, L1_xattn_nq_s, L1_xattn_nkt_s, L1_xattn_nki_s)
    x = x + _L1_attn_ref(_layernorm(x, axis=-1), L1_attn_W_latent, L1_attn_b_latent, L1_attn_W_d, L1_attn_b_d, L1_attn_W_proj, L1_attn_b_proj)
    x = x + _L1_ffn_ref(_layernorm(x, axis=-1), L1_ffn_Wg, L1_ffn_w1, L1_ffn_w3, L1_ffn_w2)
    return x

_drawn_inputs = setup_inputs


def setup_inputs(seed=0):
    import zlib

    import numpy as np

    out = dict(_drawn_inputs(seed))
    spreads = {'L0_xattn_bq': (0.0, 0.8),
     'L0_xattn_bkv': (0.0, 0.1),
     'L0_xattn_bp': (0.0, 0.1),
     'L0_attn_lambda_init': (-0.20000000298023224, 0.6),
     'L1_xattn_q_b': (0.0, 0.1),
     'L1_xattn_k_b': (0.0, 0.1),
     'L1_xattn_v_b': (0.0, 0.1),
     'L1_xattn_ki_b': (0.0, 0.743),
     'L1_xattn_vi_b': (0.0, 0.1),
     'L1_xattn_o_b': (0.0, 0.1),
     'L1_xattn_nq_s': (1.0, 0.2),
     'L1_xattn_nkt_s': (1.0, 0.2),
     'L1_xattn_nki_s': (1.0, 0.2),
     'L1_attn_b_latent': (0.0, 0.1),
     'L1_attn_b_d': (0.0, 0.8),
     'L1_attn_b_proj': (0.0, 0.1)}
    factors = {'L0_xattn_Wq': 8.0, 'L1_attn_W_d': 8.0}
    for name, (base, spread) in spreads.items():
        noise = np.random.default_rng([zlib.crc32(name.encode()), seed]).standard_normal(out[name].shape)
        drawn = base * np.exp(spread * noise) if base else spread * noise
        out[name] = jnp.asarray(drawn.astype(out[name].dtype))
    for name, factor in factors.items():
        out[name] = (out[name] * factor).astype(out[name].dtype)
    return out
```

```python
from contextlib import ExitStack

import numpy as np

import concourse.bass as bass
from concourse import mybir

ALU = mybir.AluOpType
ACT = mybir.ActivationFunctionType
AX = mybir.AxisListType
F32 = mybir.dt.float32
F32R = mybir.dt.float32r
BF16 = mybir.dt.bfloat16

P = 128
D = 256
C2 = D // P
B, T = 8, 64
NT = B * T // P
NTOK = B * T
S = 128
NKT = B
H = 16
HD0 = 16
HW = 64
HD = 128
E0, E1 = 8, 8
CH0 = 12
CH1 = 11
ROUND = 12582912.0
LN255 = float(np.log(255.0))
SENT = -3.0e38
WA, WB = 768, 512

L0A = (0, 16, 768, 256)
L0F = (16, 12, 512, 256)
L1P = (28, 16, 256, 256)
L1X = (44, 16, 256, 256)
L1A = (60, 8, 512, 512)
L1F = (68, 44, 512, 256)

QB, KB, VB, NQ, NK, DB = 0, 16, 32, 48, 64, 80
LB, XVB = 96, 97
NVEC = 99
R_BQ, R_BK, R_BP, R_OB, R_PB, R_LB, R_LAM = 0, D, 2 * D, 3 * D, 4 * D, 5 * D, 5 * D + HD
NROW = R_LAM + H


def place(b):
    return (b // 2) % 2, 2 * (b // 4) + b % 2


class Count:

    def __init__(self, base):
        self.base, self.n = base, 0

    def up(self):
        self.n += 1
        return self.base + self.n


def build(nc, x_in, ctx_in, w_x0, w_l0a, w_l0f, w_l1p, w_l1x, w_l1a, w_l1f, gates, vecs, rows, ident_in, mask_in, rope_in, rotm_in, wl_in, out):
    with ExitStack() as top:
        def sem(name):
            return top.enter_context(nc.semaphore(name))

        def sb(name, shape, dt=F32, ctx=top):
            return ctx.enter_context(nc.sbuf_tensor(name, shape, dt))

        ps = top.enter_context(nc.psum_tensor("ps", [P, 8, 512], F32))

        x = sb("x", [P, NT, D])
        xn = sb("xn", [P, NT, D])
        xt_hi = sb("xt_hi", [P, C2, NTOK], F32R)
        xt_lo = sb("xt_lo", [P, C2, NTOK], F32R)
        stats = sb("stats", [P, NT, 6])
        mv = sb("mv", [P, NT, 2])
        vareps = sb("vareps", [P, NT])
        rstd = sb("rstd", [P, NT])
        neghalf = sb("neghalf", [P, NT])
        ident = sb("ident", [P, P])
        ident_bf = sb("ident_bf", [P, P], BF16)
        mask = sb("mask", [P, T])
        rope = sb("rope", [P, 2, T])
        vec = sb("vec", [P, NVEC])
        row = sb("row", [1, NROW])
        ones = sb("ones", [P, P])
        zero = sb("zero", [1, 1])
        rnd = sb("rnd", [P, 1])
        gate = sb("gate", [P, 2, C2, 8])
        gate_hi = sb("gate_hi", [P, 2, C2, 8], F32R)
        gate_lo = sb("gate_lo", [P, 2, C2, 8], F32R)
        raw = sb("raw", [P, 2, 1024])
        wa_hi = sb("wa_hi", [P, 2, WA], F32R)
        wa_lo = sb("wa_lo", [P, 2, WA], F32R)
        wb_hi = sb("wb_hi", [P, 2, WB], F32R)
        wb_lo = sb("wb_lo", [P, 2, WB], F32R)
        ctx = sb("ctx", [P, NKT, D])
        soft = sb("soft", [P, 3, 512])
        st, pr = soft[:, 0, :], soft[:, 1:3, :]
        mx = sb("mx", [P, 8])
        sm = sb("sm", [P, 8])
        rc = sb("rc", [P, 8])
        lam = sb("lam", [P, H])
        ot_hi = sb("ot_hi", [P, 2, 2, 512], F32R)
        ot_lo = sb("ot_lo", [P, 2, 2, 512], F32R)
        rotm = sb("rotm", [P, P])
        wl = sb("wl", [P, C2, HD])
        wl_hi = sb("wl_hi", [P, C2, HD], F32R)
        wl_lo = sb("wl_lo", [P, C2, HD], F32R)

        loaded = [sem("ctx_loaded"), sem("ident_loaded"), sem("x_loaded"), sem("wx_loaded")]
        set_up = sem("set_up")
        passed_pool, passed_pe = sem("passed_pool"), sem("passed_pe")
        ct_t, ct_hi_done, ct_lo_done, wx_split = sem("ct_t"), sem("ct_hi_done"), sem("ct_lo_done"), sem("wx_split")
        consts = sem("consts")
        raw_loaded = [sem("raw_loaded_0"), sem("raw_loaded_1")]
        hi_done = sem("hi_done")
        a_split, b_split = sem("a_split"), sem("b_split")
        a_used, b_used = sem("a_used"), sem("b_used")
        ln_step, ln_pow, ln_xn, ln_t, ln_hi, ln_lo = (sem(n) for n in ("ln_step", "ln_pow", "ln_xn", "ln_t", "ln_hi", "ln_lo"))
        x0 = {n: sem("x0_" + n) for n in (
            "wx_hi", "mm", "qe", "ke", "ve", "dve", "qrep", "kd", "k1", "kres", "k2", "krep", "idbf", "vti", "vi_t", "vi",
            "turn", "qt", "kt", "s", "nm", "nb", "e", "rnd_add", "rnd_pool", "rnd_dve", "t", "pt_dve", "pt_act", "pv", "rs", "out", "at_t", "at_hi", "at_lo")}
        l0 = {n: sem("l0_" + n) for n in ("lam", "q", "k", "qe", "ke", "ve", "s", "se", "dve", "sh", "e", "d", "t", "te", "pv", "ohi", "olo")}
        ff = {n: sem("ff_" + n) for n in ("lg", "dve", "shift", "e", "comb", "ghi", "glo", "g", "sg", "h", "hhi", "hlo", "ev")}
        l1 = {n: sem("l1_" + n) for n in ("acc0", "nqk", "sqq", "kst", "qst", "sqk", "acc", "ms", "sqrt", "rk", "qn", "s", "se", "dve", "sh", "e", "p", "t", "te", "u", "uhi", "ulo", "ohi", "olo")}
        la = {n: sem("la_" + n) for n in ("whi", "wlo", "lt", "lte", "late", "rot", "dve", "kr", "krot", "q", "qe", "s", "se", "sh", "e", "p", "t", "te", "pv", "ohi", "olo")}

        x_ready = sem("x_ready")
        y_done = sem("y_done")
        stored = sem("stored")

        def mm3(o, a, b, start, stop, **kw):
            nc.tensor.matmul(o, a[0], b[0], start=start, stop=False, **kw)
            nc.tensor.matmul(o, a[0], b[1], start=False, stop=False, **kw)
            return nc.tensor.matmul(o, a[1], b[0], start=False, stop=stop, **kw)

        def xt(c, lo, n):
            return xt_hi[:, c, lo:lo + n], xt_lo[:, c, lo:lo + n]

        def wa(u, lo, n):
            return wa_hi[:, u, lo:lo + n], wa_lo[:, u, lo:lo + n]

        def wb(u, lo, n, k0=0, k1=P):
            return wb_hi[k0:k1, u, lo:lo + n], wb_lo[k0:k1, u, lo:lo + n]

        SET_UP = 6

        def apart(eng):
            eng.sem_inc(passed_pool if eng is nc.gpsimd else passed_pe, 1)

        def load_block(sp, n, u, m, src, stage):
            cols = stage[2] + stage[3]
            if not isinstance(n, int) or n >= 2:
                sp.wait_ge(a_split, n - 1)
                sp.wait_ge(b_split, n - 1)
            sp.dma_start(raw[:, u, 0:cols], src[bass.ds(m, 1)].rearrange("a p m -> p (a m)")).then_inc(raw_loaded[u], 16)

        def load_stage(sp, src, stage):
            first, count = stage[0], stage[1]
            for u in range(2):
                load_block(sp, first + u, u, u, src, stage)
            with sp.Fori(1, count // 2) as i:
                for u in range(2):
                    load_block(sp, 2 * i + (first + u), u, 2 * i + u, src, stage)

        def split_block(pool, n, half, u, stage):
            a, b = stage[2], stage[3]
            old = not isinstance(n, int) or n >= 2
            pool.wait_ge(raw_loaded[u], 16 * half + 16)
            if old:
                pool.wait_ge(a_used, n - 1)
            apart(pool)
            nc.gpsimd.tensor_copy(wa_hi[:, u, 0:a], raw[:, u, 0:a]).then_inc(hi_done, 1)
            pool.wait_ge(hi_done, 2 * n + 1)
            nc.gpsimd.tensor_tensor(wa_lo[:, u, 0:a], raw[:, u, 0:a], wa_hi[:, u, 0:a].bitcast(F32), ALU.subtract).then_inc(a_split, 1)
            if old:
                pool.wait_ge(b_used, n - 1)
            apart(pool)
            nc.gpsimd.tensor_copy(wb_hi[:, u, 0:b], raw[:, u, a:a + b]).then_inc(hi_done, 1)
            pool.wait_ge(hi_done, 2 * n + 2)
            nc.gpsimd.tensor_tensor(wb_lo[:, u, 0:b], raw[:, u, a:a + b], wb_hi[:, u, 0:b].bitcast(F32), ALU.subtract).then_inc(b_split, 1)

        def split_first(pool, stage):
            for u in range(2):
                split_block(pool, stage[0] + u, stage[0] // 2, u, stage)

        def split_rest(pool, stage):
            first, count = stage[0], stage[1]
            with pool.Fori(1, count // 2) as i:
                for u in range(2):
                    split_block(pool, 2 * i + (first + u), i + first // 2, u, stage)

        LNS = 3

        def ln_dve_stats(dve, n):
            for t in range(NT):
                last = nc.vector.bn_stats(stats[:, t, :], x[:, t, :])
            last.then_inc(ln_step, 1)
            dve.wait_ge(ln_step, LNS * n + 1)
            for t in range(NT):
                last = nc.vector.bn_aggr(mv[:, t, :], stats[:, t, :])
            last.then_inc(ln_step, 1)
            dve.wait_ge(ln_step, LNS * n + 2)
            nc.vector.tensor_scalar(vareps[:], mv[:, :, 1], 1e-5, None, ALU.add).then_inc(ln_step, 1)
            dve.wait_ge(ln_pow, n + 1)
            for t in range(NT):
                last = nc.vector.tensor_scalar(xn[:, t, :], x[:, t, :], mv[:, t, 0:1], rstd[:, t:t + 1], ALU.subtract, ALU.mult)
            last.then_inc(ln_xn, 1)

        def ln_dve_split(dve, n):
            dve.wait_ge(ln_hi, n + 1)
            nc.vector.tensor_tensor(xt_lo[:].rearrange("p c n -> p (c n)"), ps[:, 0:2, :].rearrange("p c n -> p (c n)"),
                                    xt_hi[:].rearrange("p c n -> p (c n)").bitcast(F32), ALU.subtract).then_inc(ln_lo, 1)

        def ln_dve(dve, n):
            ln_dve_stats(dve, n)
            ln_dve_split(dve, n)

        def ln_pool(pool, n):
            pool.wait_ge(ln_step, LNS * n + 3)
            nc.gpsimd.tensor_tensor(rstd[:], vareps[:], neghalf[:], ALU.pow).then_inc(ln_pow, 1)

        def ln_pe(pe, n):
            pe.wait_ge(ln_xn, n + 1)
            for c in range(C2):
                for t in range(NT):
                    last = nc.tensor.transpose(ps[:, c, t * P:(t + 1) * P], xn[:, t, c * P:(c + 1) * P], ident[:])
            last.then_inc(ln_t, 1)

        def ln_act(act, n):
            act.wait_ge(ln_t, n + 1)
            nc.scalar.activation(xt_hi[:].rearrange("p c n -> p (c n)"), ps[:, 0:2, :].rearrange("p c n -> p (c n)"), ACT.Copy).then_inc(ln_hi, 1)

        def twice(off):
            return row[:, off:off + D].unsqueeze(1).broadcast_to([1, 2, D])

        def y_start(off):
            src = twice(off) if off is not None else zero[:, :].broadcast_to([1, 512])
            for k in range(2):
                nc.tensor.matmul(ps[:, 6 + k, :], ones[0:1, :], src, start=True, stop=False, skip_group_check=True)

        def y_add(o, w):
            for t in range(NT):
                last = mm3(ps[:, 6 + t // 2, (t % 2) * D:(t % 2 + 1) * D], o(t), w, False, False, skip_group_check=True)
            return last

        def y_stop():
            for k in range(2):
                last = nc.tensor.matmul(ps[:, 6 + k, :], ones[0:1, :], zero[:, :].broadcast_to([1, 512]), start=False, stop=True, skip_group_check=True)
            last.then_inc(y_done, 1)

        def add_y(dve, n):
            dve.wait_ge(y_done, n + 1)
            for k in range(2):
                v = x[:, 2 * k:2 * k + 2, :].rearrange("p t d -> p (t d)")
                last = nc.vector.tensor_tensor(v, ps[:, 6 + k, :], v, ALU.add)
            last.then_inc(x_ready, 1)
            dve.wait_ge(x_ready, n + 1)

        def flat(ap):
            return ap.rearrange("p a b -> p (a b)")

        mc = ExitStack()
        ct_hi = sb("ct_hi", [P, C2, B * S], F32R, mc)
        ct_lo = sb("ct_lo", [P, C2, B * S], F32R, mc)
        acc = sb("acc", [P, 1536], ctx=mc)
        m0 = ExitStack()
        wx = sb("wx", [P, C2, 1024], ctx=m0)
        wx_hi = sb("wx_hi", [P, C2, 1024], F32R, m0)
        wx_lo = sb("wx_lo", [P, C2, 1024], F32R, m0)
        qf = sb("qf", [P, NT, D], ctx=m0)
        kf = sb("kf", [P, NKT, D], ctx=m0)
        vf = sb("vf", [P, C2, B * S], ctx=m0)
        kres = sb("kres", [P, NKT, D], ctx=m0)
        qs = sb("qs", [P, NT * H], ctx=m0)
        qr = sb("qr", [P, NT * H], ctx=m0)
        ks = sb("ks", [P, NKT * H], ctx=m0)
        kr = sb("kr", [P, NKT * H], ctx=m0)
        vs = sb("vs", [P, C2], ctx=m0)
        vr = sb("vr", [P, C2], ctx=m0)
        q_rep = sb("q_rep", [P, NT, (H + 2) * HW], BF16, m0)
        k_rep = sb("k_rep", [P, NKT, (H + 2) * HW], BF16, m0)
        vti = sb("vti", [P, C2, B * S], BF16, m0)
        vi = sb("vi", [P, NKT, D], BF16, m0)
        qt = sb("qt", [P, 2, NTOK], BF16, m0)
        kt = sb("kt", [P, 2, B * S], BF16, m0)
        ex = kres[:].rearrange("p (u a) d -> p u (a d)", u=2)
        ei = vf[:, 0, :].bitcast(BF16).rearrange("p (u n) -> p u n", u=2)
        pt = vf[:, 1, :].bitcast(BF16).rearrange("p (u n) -> p u n", u=2)
        nm = sb("nm", [P, 2], ctx=m0)
        nb = sb("nb", [P, 2], ctx=m0)
        sums = sb("sums", [P, 2, 8], ctx=m0)
        rs = sb("rs", [P, 8], ctx=m0)
        m0.close()
        m1 = ExitStack()
        qh = sb("qh", [P, 512], ctx=m1)
        kh = sb("kh", [P, 512], ctx=m1)
        vh = sb("vh", [P, 2, NT, HD], ctx=m1)
        dd = sb("dd", [P, 2, 256], ctx=m1)
        ddt = sb("ddt", [P, 2, P], ctx=m1)
        m1.close()
        m2 = ExitStack()
        lg = sb("lg", [P, NT, 16], ctx=m2)
        top8 = sb("top8", [P, NT, 8], ctx=m2)
        rep = sb("rep", [P, NT, 16], ctx=m2)
        sel = sb("sel", [P, NT, 8], ctx=m2)
        sh = sb("sh", [P, NT, 8], ctx=m2)
        ssum = sb("ssum", [P, NT], ctx=m2)
        comb = sb("comb", [P, CH0, NT], ctx=m2)
        sg = sb("sg", [P, 2, 512], ctx=m2)
        hh = sb("hh", [P, 2, 512], ctx=m2)
        h_hi = sb("h_hi", [P, 2, 512], F32R, m2)
        h_lo = sb("h_lo", [P, 2, 512], F32R, m2)
        m2.close()
        m3 = ExitStack()
        kst = sb("kst", [P, H, B * S], ctx=m3)
        qst = sb("qst", [P, H, NTOK], ctx=m3)
        nqk = sb("nqk", [P, H], ctx=m3)
        epsc = sb("epsc", [P, 1], ctx=m3)
        m3.close()
        sq = flat(soft[:])
        rq = flat(xn[:, 0:2, :])
        rk = flat(xn[:, 2:4, :]).rearrange("p (g k) -> p g k", g=4)
        m4 = ExitStack()
        qc = sb("qc", [P, 2, 512], ctx=m4)
        qsn = sb("qsn", [P, 2, 512], ctx=m4)
        lt = sb("lt", [P, NTOK], ctx=m4)
        lat = sb("lat", [P, NT, HD], ctx=m4)
        krot = sb("krot", [P, 2, NTOK], ctx=m4)
        lcos = sb("lcos", [P, NTOK], ctx=m4)
        lsin = sb("lsin", [P, NTOK], ctx=m4)
        dtl = sb("dtl", [P, 2, 2, P], ctx=m4)
        m4.close()
        mc.close()
        mu = ExitStack()
        qn = sb("qn", [P, 2, NTOK], ctx=mu)
        kn = sb("kn", [P, 2, B * S], ctx=mu)
        ptx = sb("ptx", [P, 4, P], ctx=mu)
        u_hi = sb("u_hi", [P, C2, 512], F32R, mu)
        u_lo = sb("u_lo", [P, C2, 512], F32R, mu)
        mu.close()

        NLOAD, NCONST = 2, 8

        def setup_sync(sp):
            sp.dma_start(ctx[:], ctx_in).then_inc(loaded[0], 16)
            sp.dma_start(ident[:], ident_in).then_inc(loaded[1], 16)
            sp.dma_start(x[:], x_in).then_inc(loaded[2], 16)
            sp.dma_start(wx[:], w_x0).then_inc(loaded[3], 16)
            for dst, src in ((row, rows), (vec, vecs), (mask, mask_in), (rope, rope_in), (gate, gates), (rotm, rotm_in), (wl, wl_in)):
                sp.dma_start(dst[:], src).then_inc(consts, 16)

        CONSTS = 7 * 16

        def setup_pool(pool):
            nc.gpsimd.memset(ones[:], 1.0).then_inc(set_up, 1)
            nc.gpsimd.memset(zero[:], 0.0).then_inc(set_up, 1)
            nc.gpsimd.memset(neghalf[:], -0.5).then_inc(set_up, 1)
            nc.gpsimd.memset(rnd[:], ROUND).then_inc(set_up, 1)
            nc.gpsimd.memset(q_rep[:], 0.0).then_inc(set_up, 1)
            nc.gpsimd.memset(k_rep[:], 0.0).then_inc(set_up, 1)

        def bank_bf(b):
            return ps[:, b, :].bitcast(BF16)

        VBANK = ((6, 8), (0, 2))

        def l0x_pe_before(pe):
            pe.wait_ge(loaded[0], 16)
            pe.wait_ge(loaded[1], 16)
            for c in range(C2):
                for k in range(NKT):
                    last = nc.tensor.transpose(ps[:, 2 + 2 * c + k // 4, (k % 4) * P:(k % 4 + 1) * P], ctx[:, k, c * P:(c + 1) * P], ident[:])
            last.then_inc(ct_t, 1)
            ln_pe(pe, 0)
            pe.wait_ge(ln_lo, 1)
            pe.wait_ge(wx_split, 1)
            pe.wait_ge(consts, CONSTS)
            for k in range(2):
                nc.tensor.matmul(ps[:, k, :], ones[0:1, :], twice(R_BQ), start=True, stop=False, skip_group_check=True)
                for t in (2 * k, 2 * k + 1):
                    for c in range(C2):
                        last = mm3(ps[:, k, (t % 2) * D:(t % 2 + 1) * D], xt(c, t * P, P), (wx_hi[:, c, 0:D], wx_lo[:, c, 0:D]),
                                   False, t % 2 == 1 and c == 1, skip_group_check=True)
            last.then_inc(x0["mm"], 1)
            pe.wait_ge(ct_lo_done, 1)
            for k in range(4):
                nc.tensor.matmul(ps[:, 2 + k, :], ones[0:1, :], twice(R_BK), start=True, stop=False, skip_group_check=True)
                for t in (2 * k, 2 * k + 1):
                    for c in range(C2):
                        last = mm3(ps[:, 2 + k, (t % 2) * D:(t % 2 + 1) * D], (ct_hi[:, c, t * P:(t + 1) * P], ct_lo[:, c, t * P:(t + 1) * P]),
                                   (wx_hi[:, c, D:2 * D], wx_lo[:, c, D:2 * D]), False, t % 2 == 1 and c == 1, skip_group_check=True)
            last.then_inc(x0["mm"], 1)
            for m in range(C2):
                if m == 1:
                    pe.wait_ge(x0["qe"], 1)
                for j in range(2):
                    for c in range(C2):
                        cols = slice(2 * D + m * P, 2 * D + (m + 1) * P)
                        last = mm3(ps[:, VBANK[m][0] + j, :], (wx_hi[:, c, cols], wx_lo[:, c, cols]),
                                   (ct_hi[:, c, j * 512:(j + 1) * 512], ct_lo[:, c, j * 512:(j + 1) * 512]), c == 0, c == 1)
                last.then_inc(x0["mm"], 1)
            pe.wait_ge(x0["qrep"], 1)
            pe.wait_ge(x0["krep"], 1)
            pe.wait_ge(x0["ve"], 2)
            pe.wait_ge(x0["idbf"], 1)
            l0x_turn(pe, 0, 0)
            pe.wait_ge(x0["vti"], 1)
            for k in range(NKT):
                for c in range(C2):
                    last = nc.tensor.transpose(bank_bf(2 + k // 4)[:, (k % 4) * D + c * P:(k % 4) * D + (c + 1) * P], vti[:, c, k * P:(k + 1) * P], ident_bf[:])
            last.then_inc(x0["vi_t"], 1)
            pe.wait_ge(x0["vi"], 1)

        def l0x_turn(pe, pair, u):
            for t in range(NT):
                nc.tensor.transpose(bank_bf(0)[:, t * P:(t + 1) * P], q_rep[:, t, bass.ds(pair * 2 * HW, P)], ident_bf[:])
            for t in range(NKT):
                last = nc.tensor.transpose(bank_bf(1)[:, t * P:(t + 1) * P], k_rep[:, t, bass.ds(pair * 2 * HW, P)], ident_bf[:])
            last.then_inc(x0["turn"], 1)

        EV_ACT = (1, 4, 7, 10, 13)
        RND_POOL = (0, 3, 6, 9, 12)

        def shared(i, m, mine, sem_mine, sem_other):
            q, r = divmod(m, 16)
            if r in mine:
                return sem_mine, (i + q) * len(mine) + len([a for a in mine if a <= r])
            return sem_other, (i + q) * (16 - len(mine)) + len([a for a in range(r + 1) if a not in mine])

        def copied(i, m):
            return shared(i, m, EV_ACT, x0["pt_act"], x0["pt_dve"])

        def rounded(i, m):
            return shared(i, m, RND_POOL, x0["rnd_pool"], x0["rnd_dve"])

        def exists(i, n):
            return not isinstance(i, int) or n >= 0

        def l0x_pe_unit(pe, i, m, live=True):
            n, k, a, t = 16 * i + m, m % 8, (m % 8) // 4, m % 4
            pair, u = 2 * i + m // 8, (m // 8) % 2
            if live:
                if k == 0:
                    pe.wait_ge(x0["qt"], pair + 1)
                    pe.wait_ge(x0["kt"], pair + 1)
                if exists(i, n - 2):
                    pe.wait_ge(x0["e"], n - 1)
                for j in range(2):
                    last = nc.tensor.matmul(ps[:, 2 + 2 * (m % 2) + j, :], qt[64 * a:64 * a + 48, u, t * P:(t + 1) * P],
                                            kt[64 * a:64 * a + 48, u, j * 512:(j + 1) * 512], start=True, stop=True)
                last.then_inc(x0["s"], 1)
                if k == 5:
                    l0x_turn(pe, pair + 1, 1 - u)
            if exists(i, n - 3) and (live or m - 3 < 0):
                pe.wait_ge(*rounded(i, m - 3))
                if exists(i, n - 5):
                    pe.wait_ge(*copied(i, m - 5))
                for kk in range(NKT):
                    last = nc.tensor.transpose(bank_bf(6 + (m - 3) % 2)[:, kk * P:(kk + 1) * P], ei[:, (m - 3) % 2, kk * P:(kk + 1) * P], ident_bf[:])
                last.then_inc(x0["t"], 1)
            if exists(i, n - 4):
                q, kp = divmod(m - 4, 8)
                if kp == 0 and exists(i, n - 5):
                    pe.wait_ge(x0["out"], 2 * i + q)
                if live and k == 5:
                    pe.wait_ge(x0["qt"], pair + 2)
                pe.wait_ge(*copied(i, m - 4))
                for kk in range(NKT):
                    last = nc.tensor.matmul(ps[:, 0, 256 + 16 * kp:272 + 16 * kp], pt[:, (m - 4) % 2, kk * P:(kk + 1) * P],
                                            vi[:, kk, bass.ds((2 * i + q) * 32 + (kp // 4) * HD0, HD0)], start=kk == 0, stop=kk == NKT - 1)
                last.then_inc(x0["pv"], 1)

        def l0x_pe(pe):
            l0x_pe_before(pe)
            for m in range(16):
                l0x_pe_unit(pe, 0, m)
            with pe.Fori(1, 4) as i:
                for m in range(16):
                    l0x_pe_unit(pe, i, m)
            for m in range(4):
                l0x_pe_unit(pe, 4, m, live=False)
            pe.wait_ge(x0["out"], 8)
            for c in range(C2):
                for t in range(NT):
                    last = nc.tensor.transpose(ps[:, 2 + c, t * P:(t + 1) * P], xn[:, t, c * P:(c + 1) * P], ident[:])
            last.then_inc(x0["at_t"], 1)
            y_start(R_BP)
            pe.wait_ge(x0["at_lo"], 1)
            for c in range(C2):
                y_add(lambda t: xt(c, t * P, P), (wx_hi[:, c, 3 * D:], wx_lo[:, c, 3 * D:]))
            y_stop()

        def l0x_pool(pool):
            pool.wait_ge(x0["wx_hi"], 1)
            nc.gpsimd.tensor_tensor(flat(wx_lo[:]), flat(wx[:]), flat(wx_hi[:]).bitcast(F32), ALU.subtract).then_inc(wx_split, 1)

            def unit(i, m):
                n, r = 16 * i + m, rounded(i, m)[1]
                pool.wait_ge(x0["e"], n + 1)
                if exists(i, n - 2):
                    pool.wait_ge(x0["t"], n - 1)
                nc.gpsimd.tensor_tensor(ex[:, m % 2, :], ex[:, m % 2, :], rnd[:, :].broadcast_to([P, B * S]), ALU.add).then_inc(x0["rnd_add"], 1)
                pool.wait_ge(x0["rnd_add"], r)
                nc.gpsimd.tensor_tensor(ei[:, m % 2, :], ex[:, m % 2, :], rnd[:, :].broadcast_to([P, B * S]), ALU.subtract).then_inc(x0["rnd_pool"], 1)

            for m in RND_POOL:
                unit(0, m)
            with pool.Fori(1, 4) as i:
                for m in RND_POOL:
                    unit(i, m)

        def l0x_copy_pt(eng, i, m):
            n = 16 * i + m
            act = m % 16 in EV_ACT
            eng.wait_ge(x0["t"], n + 1)
            if exists(i, n - 2):
                eng.wait_ge(x0["pv"], n - 1)
            if act:
                nc.scalar.activation(pt[:, m % 2, :], bank_bf(6 + m % 2), ACT.Copy).then_inc(x0["pt_act"], 1)
            else:
                nc.vector.tensor_copy(pt[:, m % 2, :], bank_bf(6 + m % 2)).then_inc(x0["pt_dve"], 1)

        def l0x_act(act):
            act.wait_ge(loaded[3], 16)
            nc.scalar.activation(flat(wx_hi[:]), flat(wx[:]), ACT.Copy).then_inc(x0["wx_hi"], 1)
            act.wait_ge(ct_t, 1)
            for c in range(C2):
                last = nc.scalar.activation(ct_hi[:, c, :], flat(ps[:, 2 + 2 * c:4 + 2 * c, :]), ACT.Copy)
            last.then_inc(ct_hi_done, 1)
            ln_act(act, 0)
            act.wait_ge(x0["mm"], 1)
            nc.scalar.activation(flat(qf[:]), flat(ps[:, 0:2, :]), ACT.Copy, scale=0.25).then_inc(x0["qe"], 1)
            act.wait_ge(x0["mm"], 2)
            nc.scalar.activation(flat(kf[:]), flat(ps[:, 2:6, :]), ACT.Copy).then_inc(x0["ke"], 1)
            for c in range(C2):
                act.wait_ge(x0["mm"], 3 + c)
                nc.scalar.activation(vf[:, c, :], flat(ps[:, VBANK[c][0]:VBANK[c][1], :]), ACT.Identity, bias=vec[:, XVB + c:XVB + c + 1]).then_inc(x0["ve"], 1)
            act.wait_ge(x0["kd"], 1)
            kp = k_rep[:, :, 0:H * HW].rearrange("p t (h w) -> p t h w", w=HW)
            kv = kf[:].rearrange("p t (h e) -> p t h e", e=HD0)
            nc.scalar.activation(kp[:, :, :, 0:HD0], kv, ACT.Copy).then_inc(x0["k1"], 1)
            act.wait_ge(x0["kres"], 1)
            nc.scalar.activation(kp[:, :, :, HD0:2 * HD0], kres[:].rearrange("p t (h e) -> p t h e", e=HD0), ACT.Copy).then_inc(x0["k2"], 1)

            def turned(pair, u):
                act.wait_ge(x0["turn"], pair + 1)
                nc.scalar.activation(qt[:, u, :], bank_bf(0)[:, 0:NTOK], ACT.Copy).then_inc(x0["qt"], 1)

            def unit(i, m, live=True):
                n, k, pair, u = 16 * i + m, m % 8, 2 * i + m // 8, (m // 8) % 2
                if live:
                    act.wait_ge(x0["nb"], n + 1)
                    if exists(i, n - 2):
                        act.wait_ge(*rounded(i, m - 2))
                    if k == 0 and exists(i, n - 16):
                        act.wait_ge(x0["out"], pair - 1)
                    col = (m % 4) * H + (m % 8) // 4
                    nc.scalar.activation(ex[:, m % 2, :], flat(ps[:, 2 + 2 * (m % 2):4 + 2 * (m % 2), :]), ACT.Exp, bias=nb[:, m % 2:m % 2 + 1],
                                         scale=qs[:, bass.ds(2 * pair + col, 1)], accum_out=sums[:, u, k:k + 1]).then_inc(x0["e"], 1)
                if (m - 3) % 16 in EV_ACT and exists(i, n - 3) and (live or m < 3):
                    l0x_copy_pt(act, i, m - 3)
                if live and k == 5:
                    turned(pair + 1, 1 - u)

            turned(0, 0)
            for m in range(16):
                unit(0, m)
            with act.Fori(1, 4) as i:
                for m in range(16):
                    unit(i, m)
            for m in range(3):
                unit(4, m, live=False)
            act.wait_ge(x0["at_t"], 1)
            for c in range(C2):
                last = nc.scalar.activation(xt_hi[:, c, :], ps[:, 2 + c, :], ACT.Copy, scale=vs[:, c:c + 1])
            last.then_inc(x0["at_hi"], 1)

        def l0x_dve(dve):
            c = Count(0)
            step = x0["dve"]
            dve.wait_ge(loaded[1], 16)
            nc.vector.tensor_copy(ident_bf[:], ident[:]).then_inc(x0["idbf"], 1)
            dve.wait_ge(loaded[2], 16)
            dve.wait_ge(set_up, SET_UP)
            ln_dve_stats(dve, 0)
            dve.wait_ge(ct_hi_done, 1)
            for k in range(C2):
                last = nc.vector.tensor_tensor(ct_lo[:, k, :], flat(ps[:, 2 + 2 * k:4 + 2 * k, :]), ct_hi[:, k, :].bitcast(F32), ALU.subtract)
            last.then_inc(ct_lo_done, 1)
            ln_dve_split(dve, 0)

            def scale_of(src, s, r):
                nc.vector.tensor_reduce(s, src, AX.X, ALU.max, apply_absolute_value=True).then_inc(step, 1)
                dve.wait_ge(step, c.up())
                nc.vector.tensor_scalar(s, s, 1.0 / 127.0, 1e-8, ALU.mult, ALU.max).then_inc(step, 1)
                dve.wait_ge(step, c.up())
                nc.vector.reciprocal(r, s).then_inc(step, 1)
                dve.wait_ge(step, c.up())

            qv = qf[:].rearrange("p t (h e) -> p (t h) e", e=HD0)
            kv = kf[:].rearrange("p t (h e) -> p (t h) e", e=HD0)
            kp = k_rep[:, :, 0:H * HW].rearrange("p t (h w) -> p t h w", w=HW)
            kv4, krv = kf[:].rearrange("p t (h e) -> p t h e", e=HD0), kres[:].rearrange("p t (h e) -> p t h e", e=HD0)
            dve.wait_ge(x0["qe"], 1)
            scale_of(qv, qs[:], qr[:])
            nc.vector.tensor_tensor(qv, qv, qr[:].unsqueeze(2).broadcast_to([P, NT * H, HD0]), ALU.mult).then_inc(step, 1)
            dve.wait_ge(step, c.up())
            for r in range(3):
                for t in range(NT):
                    dst = q_rep[:, t, 0:H * HW].rearrange("p (h w) -> p h w", w=HW)[:, :, r * HD0:(r + 1) * HD0]
                    last = nc.vector.tensor_scalar(dst, qf[:, t, :].rearrange("p (h e) -> p h e", e=HD0), ROUND, ROUND, ALU.add, ALU.subtract)
            last.then_inc(x0["qrep"], 1)
            dve.wait_ge(x0["ke"], 1)
            scale_of(kv, ks[:], kr[:])
            nc.vector.tensor_tensor(kv, kv, kr[:].unsqueeze(2).broadcast_to([P, NKT * H, HD0]), ALU.mult).then_inc(step, 1)
            dve.wait_ge(step, c.up())
            nc.vector.tensor_scalar(flat(kf[:]), flat(kf[:]), ROUND, ROUND, ALU.add, ALU.subtract).then_inc(step, 1)
            dve.wait_ge(step, c.up())
            nc.vector.tensor_tensor(kv, kv, ks[:].unsqueeze(2).broadcast_to([P, NKT * H, HD0]), ALU.mult).then_inc(x0["kd"], 1)
            dve.wait_ge(x0["kd"], 1)
            dve.wait_ge(x0["k1"], 1)
            nc.vector.tensor_tensor(krv, kv4, kp[:, :, :, 0:HD0], ALU.subtract).then_inc(x0["kres"], 1)
            dve.wait_ge(x0["kres"], 1)
            dve.wait_ge(x0["k2"], 1)
            nc.vector.tensor_tensor(kp[:, :, :, 2 * HD0:3 * HD0], krv, kp[:, :, :, HD0:2 * HD0], ALU.subtract).then_inc(x0["krep"], 1)
            dve.wait_ge(x0["ve"], 2)
            scale_of(vf[:], vs[:], vr[:])
            for k in range(C2):
                last = nc.vector.tensor_scalar(vf[:, k, :], vf[:, k, :], vr[:, k:k + 1], ROUND, ALU.mult, ALU.add)
            last.then_inc(step, 1)
            dve.wait_ge(step, c.up())
            nc.vector.tensor_scalar(flat(vti[:]), flat(vf[:]), ROUND, None, ALU.subtract).then_inc(x0["vti"], 1)

            def turned(pair, u):
                dve.wait_ge(x0["turn"], pair + 1)
                nc.vector.tensor_copy(kt[:, u, :], bank_bf(1)).then_inc(x0["kt"], 1)

            def outputs(pair, u):
                dve.wait_ge(x0["pv"], 8 * pair + 8)
                nc.vector.reciprocal(rs[:], sums[:, u, :]).then_inc(x0["rs"], 1)
                dve.wait_ge(x0["rs"], pair + 1)
                for a in range(2):
                    last = nc.vector.tensor_tensor(xn[:, :, bass.ds(32 * pair + HD0 * a, HD0)], ps[:, 0, 256 + 64 * a:320 + 64 * a].rearrange("p (t e) -> p t e", t=NT),
                                                   rs[:, 4 * a:4 * a + 4].unsqueeze(2).broadcast_to([P, NT, HD0]), ALU.mult)
                last.then_inc(x0["out"], 1)

            def unit(i, m, live=True):
                n, k, pair, u = 16 * i + m, m % 8, 2 * i + m // 8, (m // 8) % 2
                if live:
                    dve.wait_ge(x0["s"], n + 1)
                    nc.vector.tensor_reduce(nm[:, m % 2:m % 2 + 1], flat(ps[:, 2 + 2 * (m % 2):4 + 2 * (m % 2), :]), AX.X, ALU.max, negate=True).then_inc(x0["nm"], 1)
                    dve.wait_ge(x0["nm"], n + 1)
                    if exists(i, n - 2):
                        dve.wait_ge(x0["e"], n - 1)
                    col = (m % 4) * H + (m % 8) // 4
                    nc.vector.tensor_scalar(nb[:, m % 2:m % 2 + 1], nm[:, m % 2:m % 2 + 1], qs[:, bass.ds(2 * pair + col, 1)], LN255, ALU.mult, ALU.add).then_inc(x0["nb"], 1)
                if (m - 1) % 16 not in RND_POOL and exists(i, n - 1) and (live or m < 1):
                    dve.wait_ge(x0["e"], n)
                    if exists(i, n - 3):
                        dve.wait_ge(x0["t"], n - 2)
                    nc.vector.tensor_scalar(ei[:, (m - 1) % 2, :], ex[:, (m - 1) % 2, :], ROUND, ROUND, ALU.add, ALU.subtract).then_inc(x0["rnd_dve"], 1)
                if (m - 3) % 16 not in EV_ACT and exists(i, n - 3) and (live or m < 3):
                    l0x_copy_pt(dve, i, m - 3)
                if k == 4 and exists(i, n - 8):
                    outputs(pair - 1, 1 - u)
                if live and k == 5:
                    turned(pair + 1, 1 - u)

            turned(0, 0)
            dve.wait_ge(x0["vi_t"], 1)
            nc.vector.tensor_copy(vi[:].rearrange("p k d -> p (k d)"), flat(ps[:, 2:4, :]).bitcast(BF16)).then_inc(x0["vi"], 1)
            for m in range(16):
                unit(0, m)
            with dve.Fori(1, 4) as i:
                for m in range(16):
                    unit(i, m)
            for m in range(5):
                unit(4, m, live=False)
            dve.wait_ge(x0["at_hi"], 1)
            for k in range(C2):
                last = nc.vector.scalar_tensor_tensor(xt_lo[:, k, :], ps[:, 2 + k, :], vs[:, k:k + 1], xt_hi[:, k, :].bitcast(F32), ALU.mult, ALU.subtract)
            last.then_inc(x0["at_lo"], 1)
            add_y(dve, 0)

        N1 = L0A[0]

        def by_batch(ap):
            return ap.rearrange("p (b e k) -> p e b k", e=2, k=T)

        def banks45():
            return ps[:, 4:6, 0:256].rearrange("p e (b k) -> p e b k", k=T)

        def l0a_project(pe, h, u):
            n = h + N1
            pe.wait_ge(a_split, n + 1)
            for k, name in enumerate(("q", "k")):
                if exists(h, h - 1):
                    pe.wait_ge(l0["se"], h)
                for c in range(C2):
                    last = mm3(ps[:, k, :], wa(u, 2 * P * k + c * P, P), (xt_hi[:, c, :], xt_lo[:, c, :]), c == 0, c == 1)
                last.then_inc(l0[name], 1)
            if exists(h, h - 1):
                pe.wait_ge(l0["ve"], h)
            for t in range(NT):
                for c in range(C2):
                    last = mm3(ps[:, 2, t * P:(t + 1) * P], xt(c, t * P, P), wa(u, 4 * P + c * P, P), c == 0, c == 1)
            last.then_inc(a_used, 1)

        def l0a_pv(pe, h, u):
            pe.wait_ge(l0["d"], h + 1)
            if exists(h, h - 1):
                pe.wait_ge(l0["te"], h)
            for g in range(2):
                last = nc.tensor.transpose(ps[:, 3, g * P:(g + 1) * P], dd[:, u, g * P:(g + 1) * P], ident[:])
            last.then_inc(l0["t"], 1)
            pe.wait_ge(l0["te"], h + 1)
            if exists(h, h - 1):
                pe.wait_ge(l0["olo"], h)
            apart(pe)
            for b in range(B):
                p, g = place(b)
                k0 = T * (b % 2)
                last = nc.tensor.matmul(ps[:, 4 + b % 2, (b // 2) * T:(b // 2 + 1) * T], vh[k0:k0 + T, u, b // 2, :], ddt[k0:k0 + T, g // 2, T * p:T * (p + 1)], start=True, stop=True)
            last.then_inc(l0["pv"], 1)

        def l0a_scores(pe, h, u):
            pe.wait_ge(l0["qe"], h + 1)
            pe.wait_ge(l0["ke"], h + 1)
            apart(pe)
            for b in range(B):
                p, g = place(b)
                for f in range(2):
                    r = slice(T * f, T * f + T)
                    last = nc.tensor.matmul(ps[T * p:T * (p + 1), f, g * T:(g + 1) * T], qh[r, b * T:(b + 1) * T], kh[r, b * T:(b + 1) * T], start=True, stop=True)
            last.then_inc(l0["s"], 1)

        def l0a_out(pe, h, u):
            pe.wait_ge(l0["olo"], h + 1)
            pe.wait_ge(b_split, h + N1 + 1)
            y_add(lambda t: (ot_hi[:, u, 0, t * P:(t + 1) * P], ot_lo[:, u, 0, t * P:(t + 1) * P]), wb(u, 0, D)).then_inc(b_used, 1)

        def l0a_pe_head(pe, h, u):
            l0a_project(pe, h, u)
            if exists(h, h - 1):
                l0a_pv(pe, h - 1, 1 - u)
            l0a_scores(pe, h, u)
            if exists(h, h - 1):
                l0a_out(pe, h - 1, 1 - u)

        def l0a_pe(pe):
            ln_pe(pe, 1)
            pe.wait_ge(x_ready, 1)
            y_start(None)
            pe.wait_ge(consts, CONSTS)
            lam_mm = nc.tensor.matmul(ps[:, 3, 0:H], ones[0:1, :], row[:, R_LAM:R_LAM + H], start=True, stop=True)
            lam_mm.then_inc(l0["lam"], 1)
            pe.wait_ge(l0["lam"], 2)
            pe.wait_ge(ln_lo, 2)
            for u in range(2):
                l0a_pe_head(pe, u, u)
            with pe.Fori(1, H // 2) as i:
                for u in range(2):
                    l0a_pe_head(pe, 2 * i + u, u)
            l0a_pv(pe, H - 1, 1)
            l0a_out(pe, H - 1, 1)
            y_stop()

        def l0a_pool(pool):
            split_first(pool, L0A)
            ln_pool(pool, 1)
            split_rest(pool, L0A)

        def l0a_act(act):
            ln_act(act, 1)
            act.wait_ge(l0["lam"], 1)
            nc.scalar.activation(lam[:], ps[:, 3, 0:H], ACT.Exp, scale=-1.0).then_inc(l0["lam"], 1)

            def after(h, u):
                act.wait_ge(l0["t"], h + 1)
                nc.scalar.activation(flat(ddt[:]), ps[:, 3, 0:2 * P], ACT.Copy).then_inc(l0["te"], 1)
                act.wait_ge(l0["pv"], h + 1)
                if exists(h, h - 2):
                    act.wait_ge(b_used, h + N1 - 1)
                nc.scalar.activation(by_batch(ot_hi[:, u, 0, :]), banks45(), ACT.Copy).then_inc(l0["ohi"], 1)

            def head(h, u):
                act.wait_ge(l0["q"], h + 1)
                if exists(h, h - 1):
                    act.wait_ge(l0["s"], h)
                nc.scalar.activation(qh[:], ps[:, 0, :], ACT.Copy).then_inc(l0["qe"], 1)
                act.wait_ge(l0["k"], h + 1)
                nc.scalar.activation(kh[:], ps[:, 1, :], ACT.Copy).then_inc(l0["ke"], 1)
                if exists(h, h - 1):
                    after(h - 1, 1 - u)
                act.wait_ge(l0["sh"], h + 1)
                nc.scalar.activation(pr[:, u, :], st, ACT.Exp, scale=T ** -0.5).then_inc(l0["e"], 1)

            for u in range(2):
                head(u, u)
            with act.Fori(1, H // 2) as i:
                for u in range(2):
                    head(2 * i + u, u)
            after(H - 1, 1)

        STEPS0 = 5

        def groups(ap, n=8):
            return ap.rearrange("p (g k) -> p g k", g=n)

        def wide(ap, n, k):
            return ap.unsqueeze(2).broadcast_to([P, n, k])

        def l0a_dve(dve):
            ln_dve(dve, 1)
            c = Count(0)
            dve.wait_ge(l0["lam"], 2)
            for k in range(3):
                if k == 0:
                    nc.vector.tensor_scalar(lam[:], lam[:], 1.0, None, ALU.add).then_inc(l0["dve"], 1)
                elif k == 1:
                    nc.vector.reciprocal(lam[:], lam[:]).then_inc(l0["dve"], 1)
                else:
                    nc.vector.tensor_scalar(lam[:], lam[:], -1.0, None, ALU.mult).then_inc(l0["dve"], 1)
                dve.wait_ge(l0["dve"], c.up())

            def after(h, u):
                dve.wait_ge(l0["ohi"], h + 1)
                nc.vector.tensor_tensor(by_batch(ot_lo[:, u, 0, :]), banks45(), by_batch(ot_hi[:, u, 0, :]).bitcast(F32), ALU.subtract).then_inc(l0["olo"], 1)

            def head(h, u):
                c = Count(3 + STEPS0 * h)
                dve.wait_ge(a_used, h + N1 + 1)
                if exists(h, h - 2):
                    dve.wait_ge(l0["pv"], h - 1)
                nc.vector.tensor_copy(vh[:, u, :, :].rearrange("p t d -> p (t d)"), ps[:, 2, :]).then_inc(l0["ve"], 1)
                if exists(h, h - 1):
                    after(h - 1, 1 - u)
                dve.wait_ge(l0["s"], h + 1)
                nc.vector.tensor_tensor(st.rearrange("p (f g k) -> p f g k", f=2, g=4), ps[:, 0:2, 0:256].rearrange("p f (g k) -> p f g k", g=4),
                                        mask[:].unsqueeze(1).unsqueeze(1).broadcast_to([P, 2, 4, T]), ALU.add).then_inc(l0["se"], 1)
                dve.wait_ge(l0["se"], h + 1)
                nc.vector.tensor_reduce(mx[:], groups(st), AX.X, ALU.max).then_inc(l0["dve"], 1)
                dve.wait_ge(l0["dve"], c.up())
                nc.vector.tensor_tensor(groups(st), groups(st), wide(mx[:], 8, T), ALU.subtract).then_inc(l0["sh"], 1)
                dve.wait_ge(l0["e"], h + 1)
                nc.vector.tensor_reduce(sm[:], groups(pr[:, u, :]), AX.X, ALU.add).then_inc(l0["dve"], 1)
                dve.wait_ge(l0["dve"], c.up())
                nc.vector.reciprocal(rc[:], sm[:]).then_inc(l0["dve"], 1)
                dve.wait_ge(l0["dve"], c.up())
                nc.vector.tensor_scalar(rc[:, 4:8], rc[:, 4:8], lam[:, bass.ds(h, 1)], None, ALU.mult).then_inc(l0["dve"], 1)
                dve.wait_ge(l0["dve"], c.up())
                nc.vector.tensor_tensor(groups(pr[:, u, :]), groups(pr[:, u, :]), wide(rc[:], 8, T), ALU.mult).then_inc(l0["dve"], 1)
                dve.wait_ge(l0["dve"], c.up())
                assert c.n == STEPS0
                nc.vector.tensor_tensor(dd[:, u, :], pr[:, u, 0:256], pr[:, u, 256:512], ALU.add).then_inc(l0["d"], 1)

            for u in range(2):
                head(u, u)
            with dve.Fori(1, H // 2) as i:
                for u in range(2):
                    head(2 * i + u, u)
            after(H - 1, 1)
            add_y(dve, 1)

        RSTEPS = 7

        def route_pe(pe, k):
            for t in range(NT):
                for c in range(C2):
                    last = mm3(ps[:, 2, 8 * t:8 * t + 8], xt(c, t * P, P), (gate_hi[:, k, c, :], gate_lo[:, k, c, :]), c == 0, c == 1)
            last.then_inc(ff["lg"], 1)

        def route_act(act, k):
            if k == 0:
                act.wait_ge(consts, CONSTS)
                nc.scalar.activation(gate_hi[:].rearrange("p a b e -> p (a b e)"), gate[:].rearrange("p a b e -> p (a b e)"), ACT.Copy).then_inc(ff["ghi"], 1)
            act.wait_ge(ff["shift"], k + 1)
            nc.scalar.activation(sh[:], sh[:], ACT.Exp).then_inc(ff["e"], 1)

        def route_dve(dve, k):
            c = Count(RSTEPS * k)
            step = ff["dve"]
            dve.wait_ge(ff["lg"], k + 1)
            nc.vector.memset(lg[:, :, 8:16], SENT)
            nc.vector.tensor_copy(lg[:, :, 0:8], ps[:, 2, 0:8 * NT].rearrange("p (t e) -> p t e", t=NT)).then_inc(step, 1)
            dve.wait_ge(step, c.up())
            for t in range(NT):
                last = nc.vector.max(top8[:, t, :], lg[:, t, :])
            last.then_inc(step, 1)
            dve.wait_ge(step, c.up())
            nc.vector.tensor_tensor(sh[:], lg[:, :, 0:8], top8[:, :, 0:1].broadcast_to([P, NT, 8]), ALU.subtract).then_inc(ff["shift"], 1)
            nc.vector.memset(top8[:, :, 2:8], SENT).then_inc(step, 1)
            dve.wait_ge(step, c.up())
            for t in range(NT):
                last = nc.vector.match_replace(rep[:, t, :], top8[:, t, :], lg[:, t, :], -SENT)
            last.then_inc(step, 1)
            dve.wait_ge(step, c.up())
            nc.vector.tensor_tensor(sel[:], rep[:, :, 0:8], lg[:, :, 0:8], ALU.not_equal).then_inc(step, 1)
            dve.wait_ge(step, c.up())
            dve.wait_ge(ff["e"], k + 1)
            nc.vector.tensor_tensor(sel[:], sel[:], sh[:], ALU.mult).then_inc(step, 1)
            dve.wait_ge(step, c.up())
            nc.vector.tensor_reduce(ssum[:], sel[:], AX.X, ALU.add).then_inc(step, 1)
            dve.wait_ge(step, c.up())
            assert c.n == RSTEPS
            nc.vector.reciprocal(ssum[:], ssum[:]).then_inc(ff["comb"], 1)
            dve.wait_ge(ff["comb"], 2 * k + 1)
            nc.vector.tensor_tensor(comb[:, 0:8, :].rearrange("p e t -> p t e"), sel[:], wide(ssum[:], NT, 8), ALU.mult).then_inc(ff["comb"], 1)

        def ffn_up(pe, n, m, u):
            pe.wait_ge(a_split, n + 1)
            if exists(m, m - 2):
                pe.wait_ge(ff["h"], m - 1)
            for k in range(2):
                for c in range(C2):
                    last = mm3(ps[:, 2 * u + k, :], wa(u, 2 * P * k + c * P, P), (xt_hi[:, c, :], xt_lo[:, c, :]), c == 0, c == 1)
                last.then_inc(ff["g"] if k == 0 else a_used, 1)

        def ffn_down(m, u, bank, r0, r1, first, final):
            for t in range(NT):
                o = (h_hi[r0:r1, u, t * P:(t + 1) * P], h_lo[r0:r1, u, t * P:(t + 1) * P])
                last = mm3(ps[:, bank + t // 2, (t % 2) * D:(t % 2 + 1) * D], o, wb(u, 0, D, r0, r1),
                           first and t % 2 == 0, final and t % 2 == 1, skip_group_check=True)
            return last

        def ffn_act(act, m, u):
            act.wait_ge(ff["g"], m + 1)
            if exists(m, m - 2):
                act.wait_ge(ff["h"], m - 1)
            nc.scalar.activation(sg[:, u, :], ps[:, 2 * u, :], ACT.Silu).then_inc(ff["sg"], 1)

        def ffn_act_hi(act, m, u, nb_used):
            act.wait_ge(ff["h"], m + 1)
            if nb_used is not None:
                act.wait_ge(b_used, nb_used)
            nc.scalar.activation(h_hi[:, u, :], hh[:, u, :], ACT.Copy).then_inc(ff["hhi"], 1)

        def ffn_dve(dve, n, m, u, old):
            dve.wait_ge(ff["sg"], m + 1)
            dve.wait_ge(a_used, n + 1)
            if exists(m, m - 2):
                dve.wait_ge(ff["hlo"], m - 1)
            nc.vector.tensor_tensor(hh[:, u, :], sg[:, u, :], ps[:, 2 * u + 1, :], ALU.mult).then_inc(ff["h"], 1)
            dve.wait_ge(ff["hhi"], m + 1)
            nc.vector.tensor_tensor(h_lo[:, u, :], hh[:, u, :], h_hi[:, u, :].bitcast(F32), ALU.subtract).then_inc(ff["hlo"], 1)

        def ffn_add(dve, bank, expert, used, xstep):
            dve.wait_ge(b_used, used)
            for t in range(NT):
                last = nc.vector.scalar_tensor_tensor(x[:, t, :], ps[:, bank + t // 2, (t % 2) * D:(t % 2 + 1) * D],
                                                      comb[:, bass.ds(expert, 1), t], x[:, t, :], ALU.mult, ALU.add)
            last.then_inc(ff["ev"], 1)
            dve.wait_ge(ff["ev"], xstep)

        N2 = L0F[0]

        def l0f_pe(pe):
            ln_pe(pe, 2)
            pe.wait_ge(ff["glo"], 1)
            pe.wait_ge(ln_lo, 3)
            route_pe(pe, 0)
            pe.wait_ge(ff["comb"], 1)

            def down(m, u):
                pe.wait_ge(ff["hlo"], m + 1)
                pe.wait_ge(b_split, m + N2 + 1)
                if exists(m, m - 2):
                    pe.wait_ge(ff["ev"], m - 1)
                ffn_down(m, u, 4 + 2 * u, 0, P, True, True).then_inc(b_used, 1)

            def chunk(m, u):
                ffn_up(pe, m + N2, m, u)
                if exists(m, m - 1):
                    down(m - 1, 1 - u)

            for u in range(2):
                chunk(u, u)
            with pe.Fori(1, CH0 // 2) as i:
                for u in range(2):
                    chunk(2 * i + u, u)
            down(CH0 - 1, 1)

        def l0f_pool(pool):
            split_first(pool, L0F)
            ln_pool(pool, 2)
            split_rest(pool, L0F)

        def l0f_act(act):
            ln_act(act, 2)
            route_act(act, 0)

            def chunk(m, u):
                ffn_act(act, m, u)
                ffn_act_hi(act, m, u, m + N2 - 1 if exists(m, m - 2) else None)

            for u in range(2):
                chunk(u, u)
            with act.Fori(1, CH0 // 2) as i:
                for u in range(2):
                    chunk(2 * i + u, u)

        def l0f_dve(dve):
            ln_dve_stats(dve, 2)
            dve.wait_ge(ff["ghi"], 1)
            nc.vector.tensor_tensor(gate_lo[:].rearrange("p a b e -> p (a b e)"), gate[:].rearrange("p a b e -> p (a b e)"),
                                    gate_hi[:].rearrange("p a b e -> p (a b e)").bitcast(F32), ALU.subtract).then_inc(ff["glo"], 1)
            ln_dve_split(dve, 2)
            nc.vector.memset(comb[:, 8:12, :], 1.0)
            route_dve(dve, 0)
            dve.wait_ge(ff["comb"], 2)

            def chunk(m, u):
                ffn_dve(dve, m + N2, m, u, None)
                if exists(m, m - 1):
                    ffn_add(dve, 4 + 2 * (1 - u), m - 1, m + N2, m)

            for u in range(2):
                chunk(u, u)
            with dve.Fori(1, CH0 // 2) as i:
                for u in range(2):
                    chunk(2 * i + u, u)
            ffn_add(dve, 6, CH0 - 1, CH0 + N2, CH0)

        NP, NX = L1P[0], L1X[0]

        def proj_pe(pe, m, u):
            n = m + NP
            pe.wait_ge(a_split, n + 1)
            if exists(m, m - 2):
                pe.wait_ge(l1["qst"], m - 1)
            for c in range(C2):
                last = mm3(ps[:, 4 + u, :], wa(u, c * P, P), (xt_hi[:, c, :], xt_lo[:, c, :]), c == 0, c == 1)
            last.then_inc(a_used, 1)
            pe.wait_ge(b_split, n + 1)
            if exists(m, m - 2):
                pe.wait_ge(l1["kst"], m - 1)
            for j in range(2):
                for c in range(C2):
                    last = mm3(ps[:, 2 * u + j, :], wb(u, c * P, P), (ct_hi[:, c, j * 512:(j + 1) * 512], ct_lo[:, c, j * 512:(j + 1) * 512]), c == 0, c == 1)
            last.then_inc(b_used, 1)

        def proj_act(act, m, u):
            act.wait_ge(a_used, m + NP + 1)
            if exists(m, m - 1):
                act.wait_ge(l1["acc"], m)
            nc.scalar.activation(sq[:, 1024:1536], ps[:, 4 + u, :], ACT.Square, bias=vec[:, bass.ds(m + QB, 1)]).then_inc(l1["sqq"], 1)
            act.wait_ge(l1["kst"], m + 1)
            nc.scalar.activation(sq[:, 0:1024], kst[:, bass.ds(m, 1), :].rearrange("p a n -> p (a n)"), ACT.Square).then_inc(l1["sqk"], 1)

        def proj_dve(dve, m, u):
            dve.wait_ge(b_used, m + NP + 1)
            nc.vector.tensor_scalar(kst[:, bass.ds(m, 1), :].rearrange("p a n -> p (a n)"), flat(ps[:, 2 * u:2 * u + 2, :]), vec[:, bass.ds(m + KB, 1)], None, ALU.add).then_inc(l1["kst"], 1)
            dve.wait_ge(l1["sqq"], m + 1)
            nc.vector.tensor_scalar(qst[:, bass.ds(m, 1), :].rearrange("p a n -> p (a n)"), ps[:, 4 + u, :], vec[:, bass.ds(m + QB, 1)], nqk[:, bass.ds(m, 1)],
                                    ALU.add, ALU.mult).then_inc(l1["qst"], 1)
            dve.wait_ge(l1["sqk"], m + 1)
            nc.vector.tensor_tensor(acc[:], acc[:], sq, ALU.add).then_inc(l1["acc"], 1)
            dve.wait_ge(l1["acc"], m + 1)

        def key_scores(pe, m, u):
            pe.wait_ge(l1["qn"], m + 1)
            if exists(m, m - 2):
                pe.wait_ge(l1["se"], m - 1)
            apart(pe)
            for b in range(B):
                p, g = place(b)
                last = nc.tensor.matmul(ps[T * p:T * (p + 1), u, g * S:(g + 1) * S], qn[:, u, b * T:(b + 1) * T], kn[:, u, b * S:(b + 1) * S], start=True, stop=True)
            last.then_inc(l1["s"], 1)

        def turn_x(pe, h, u):
            pe.wait_ge(l1["p"], h + 1)
            if exists(h, h - 1):
                pe.wait_ge(l1["te"], h)
            for g in range(4):
                last = nc.tensor.transpose(ps[:, 2, g * P:(g + 1) * P], pr[:, u, g * P:(g + 1) * P], ident[:])
            last.then_inc(l1["t"], 1)

        def mix_ctx(pe, h):
            pe.wait_ge(l1["te"], h + 1)
            if exists(h, h - 1):
                pe.wait_ge(l1["ulo"], h)
            apart(pe)
            for c in range(C2):
                for b in range(B):
                    p, g = place(b)
                    last = nc.tensor.matmul(ps[:, 3 + c, b * T:(b + 1) * T], ctx[:, b, c * P:(c + 1) * P], ptx[:, g, T * p:T * (p + 1)], start=True, stop=True)
            last.then_inc(l1["u"], 1)

        def values_x(pe, h, u):
            pe.wait_ge(l1["ulo"], h + 1)
            pe.wait_ge(a_split, h + NX + 1)
            if exists(h, h - 1):
                pe.wait_ge(l1["olo"], h)
            for c in range(C2):
                last = mm3(ps[:, 5, :], wa(u, c * P, P), (u_hi[:, c, :], u_lo[:, c, :]), c == 0, c == 1)
            last.then_inc(a_used, 1)

        def out_x(pe, h, u):
            pe.wait_ge(l1["olo"], h + 1)
            pe.wait_ge(b_split, h + NX + 1)
            y_add(lambda t: (ot_hi[:, u, 0, t * P:(t + 1) * P], ot_lo[:, u, 0, t * P:(t + 1) * P]), wb(u, 0, D)).then_inc(b_used, 1)

        def within(m):
            return not isinstance(m, int) or 0 <= m < H

        def l1x_pe(pe):
            ln_pe(pe, 3)
            pe.wait_ge(ln_lo, 4)
            for u in range(2):
                proj_pe(pe, u, u)
            with pe.Fori(1, H // 2) as i:
                for u in range(2):
                    proj_pe(pe, 2 * i + u, u)
            pe.wait_ge(l1["acc"], H)
            for k in range(3):
                last = nc.tensor.matmul(ps[:, k, :], ones[:, :], acc[:, k * 512:(k + 1) * 512], start=True, stop=True)
            last.then_inc(l1["ms"], 1)
            y_start(R_OB)
            pe.wait_ge(l1["sqrt"], 1)

            def turn(m, u):
                if within(m - 2):
                    turn_x(pe, m - 2, u)
                if within(m - 3):
                    out_x(pe, m - 3, 1 - u)
                if within(m - 2):
                    mix_ctx(pe, m - 2)
                if within(m):
                    key_scores(pe, m, u)
                if within(m - 2):
                    values_x(pe, m - 2, u)

            for m in range(4):
                turn(m, m % 2)
            with pe.Fori(2, H // 2) as i:
                for u in range(2):
                    turn(2 * i + u, u)
            for m in range(H, H + 3):
                turn(m, m % 2)
            y_stop()

        def l1x_pool(pool):
            split_first(pool, L1P)
            ln_pool(pool, 3)
            nc.gpsimd.memset(acc[:], 0.0).then_inc(l1["acc0"], 1)
            nc.gpsimd.memset(epsc[:], 1e-6).then_inc(l1["acc0"], 1)
            nc.gpsimd.tensor_tensor(nqk[:], vec[:, NQ:NQ + H], vec[:, NK:NK + H], ALU.mult).then_inc(l1["nqk"], 1)
            split_rest(pool, L1P)
            split_first(pool, L1X)
            pool.wait_ge(l1["rk"], 1)

            def head(m, u):
                if exists(m, m - 2):
                    pool.wait_ge(l1["s"], m - 1)
                nc.gpsimd.tensor_tensor(qn[:, u, :], qst[:, bass.ds(m, 1), :].rearrange("p a n -> p (a n)"), rq, ALU.mult)
                nc.gpsimd.tensor_copy(kn[:, u, :], kst[:, bass.ds(m, 1), :].rearrange("p a n -> p (a n)")).then_inc(l1["qn"], 1)

            for m in range(4):
                head(m, m % 2)
            with pool.Fori(2, H // 2) as i:
                for u in range(2):
                    head(2 * i + u, u)
                    split_block(pool, 2 * i + (u + NX - 2), i + (NX // 2 - 1), u, L1X)
            for u in range(2):
                split_block(pool, NX + H - 2 + u, (NX + H) // 2 - 1, u, L1X)

        def l1x_act(act):
            ln_act(act, 3)
            for u in range(2):
                proj_act(act, u, u)
            with act.Fori(1, H // 2) as i:
                for u in range(2):
                    proj_act(act, 2 * i + u, u)
            act.wait_ge(l1["ms"], 1)
            nc.scalar.activation(sq, ps[:, 0:3, :].rearrange("p a b -> p (a b)"), ACT.Sqrt, scale=1.0 / (H * HD), bias=epsc[:]).then_inc(l1["sqrt"], 1)

            def exps(m, u):
                act.wait_ge(l1["sh"], m + 1)
                if exists(m, m - 2):
                    act.wait_ge(l1["t"], m - 1)
                nc.scalar.activation(pr[:, u, :], st, ACT.Exp, scale=HD ** -0.5).then_inc(l1["e"], 1)

            def mixed(h):
                act.wait_ge(l1["t"], h + 1)
                nc.scalar.activation(flat(ptx[:]), ps[:, 2, :], ACT.Copy).then_inc(l1["te"], 1)
                act.wait_ge(l1["u"], h + 1)
                if exists(h, h - 1):
                    act.wait_ge(a_used, h + NX)
                nc.scalar.activation(flat(u_hi[:]), flat(ps[:, 3:5, :]), ACT.Copy).then_inc(l1["uhi"], 1)

            def outs(h, u):
                act.wait_ge(a_used, h + NX + 1)
                if exists(h, h - 2):
                    act.wait_ge(b_used, h + NX - 1)
                nc.scalar.activation(ot_hi[:, u, 0, :], ps[:, 5, :], ACT.Identity, bias=vec[:, bass.ds(h + VB, 1)]).then_inc(l1["ohi"], 1)

            def turn(m, u):
                if within(m - 2):
                    mixed(m - 2)
                    outs(m - 2, u)
                if within(m):
                    exps(m, u)

            for m in range(4):
                turn(m, m % 2)
            with act.Fori(2, H // 2) as i:
                for u in range(2):
                    turn(2 * i + u, u)
            for m in range(H, H + 2):
                turn(m, m % 2)

        STEPS1 = 3

        def l1x_dve(dve):
            ln_dve(dve, 3)
            dve.wait_ge(l1["acc0"], 2)
            dve.wait_ge(l1["nqk"], 1)
            for u in range(2):
                proj_dve(dve, u, u)
            with dve.Fori(1, H // 2) as i:
                for u in range(2):
                    proj_dve(dve, 2 * i + u, u)
            dve.wait_ge(l1["sqrt"], 1)
            dve.wait_ge(ln_t, 4)
            nc.vector.reciprocal(rq, sq[:, 1024:1536])
            for p in range(2):
                r = slice(T * p, T * (p + 1))
                last = nc.vector.reciprocal(rk[r].rearrange("p (G e) k -> p G e k", e=2), sq[r, 0:1024].rearrange("p (G q e k) -> p q G e k", G=2, q=2, e=2)[:, p])
            last.then_inc(l1["rk"], 1)
            dve.wait_ge(l1["rk"], 1)

            def scores(m, u):
                c = Count(STEPS1 * m)
                dve.wait_ge(l1["s"], m + 1)
                nc.vector.tensor_tensor(st, ps[:, u, :], rk.rearrange("p g k -> p (g k)"), ALU.mult).then_inc(l1["se"], 1)
                dve.wait_ge(l1["se"], m + 1)
                nc.vector.tensor_reduce(mx[:, 0:4], groups(st, 4), AX.X, ALU.max).then_inc(l1["dve"], 1)
                dve.wait_ge(l1["dve"], c.up())
                nc.vector.tensor_tensor(groups(st, 4), groups(st, 4), wide(mx[:, 0:4], 4, S), ALU.subtract).then_inc(l1["sh"], 1)

            def weights(m, u):
                c = Count(STEPS1 * m + 1)
                dve.wait_ge(l1["e"], m + 1)
                nc.vector.tensor_reduce(sm[:, 0:4], groups(pr[:, u, :], 4), AX.X, ALU.add).then_inc(l1["dve"], 1)
                dve.wait_ge(l1["dve"], c.up())
                nc.vector.reciprocal(rc[:, 0:4], sm[:, 0:4]).then_inc(l1["dve"], 1)
                dve.wait_ge(l1["dve"], c.up())
                nc.vector.tensor_tensor(groups(pr[:, u, :], 4), groups(pr[:, u, :], 4), wide(rc[:, 0:4], 4, S), ALU.mult).then_inc(l1["p"], 1)

            def mixed(h):
                dve.wait_ge(l1["uhi"], h + 1)
                nc.vector.tensor_tensor(flat(u_lo[:]), flat(ps[:, 3:5, :]), flat(u_hi[:]).bitcast(F32), ALU.subtract).then_inc(l1["ulo"], 1)

            def outs(h, u):
                dve.wait_ge(l1["ohi"], h + 1)
                nc.vector.scalar_tensor_tensor(ot_lo[:, u, 0, :], ps[:, 5, :], vec[:, bass.ds(h + VB, 1)], ot_hi[:, u, 0, :].bitcast(F32), ALU.add, ALU.subtract).then_inc(l1["olo"], 1)

            def turn(m, u):
                if within(m - 2):
                    mixed(m - 2)
                if within(m):
                    scores(m, u)
                if within(m - 2):
                    outs(m - 2, u)
                if within(m):
                    weights(m, u)

            for m in range(4):
                turn(m, m % 2)
            with dve.Fori(2, H // 2) as i:
                for u in range(2):
                    turn(2 * i + u, u)
            for m in range(H, H + 2):
                turn(m, m % 2)
            add_y(dve, 2)

        NA = L1A[0]

        def l1a_project(pe, j, u):
            pe.wait_ge(a_split, j + NA + 1)
            for a in range(2):
                if exists(j, j - 1):
                    pe.wait_ge(la["qe"], j)
                for c in range(C2):
                    last = mm3(ps[:, a, :], wa(u, 2 * P * a + c * P, P), (xt_hi[:, c, :], xt_lo[:, c, :]), c == 0, c == 1)
                last.then_inc(la["q"] if a == 0 else a_used, 1)

        def l1a_scores(pe, j):
            pe.wait_ge(la["qe"], j + 1)
            if exists(j, j - 1):
                pe.wait_ge(la["se"], j)
            apart(pe)
            for b in range(B):
                p, g = place(b)
                cols = slice(b * T, (b + 1) * T)
                for a in range(2):
                    o = ps[T * p:T * (p + 1), 3, (4 * a + g) * T:(4 * a + g + 1) * T]
                    nc.tensor.matmul(o, qc[:, a, cols], krot[:, 0, cols], start=True, stop=False)
                    last = nc.tensor.matmul(o, qsn[:, a, cols], krot[:, 1, cols], start=False, stop=True)
            last.then_inc(la["s"], 1)

        def l1a_pv(pe, j, u):
            pe.wait_ge(la["p"], j + 1)
            if exists(j, j - 1):
                pe.wait_ge(la["te"], j)
            for k in range(4):
                last = nc.tensor.transpose(ps[:, 2, k * P:(k + 1) * P], pr[:, u, k * P:(k + 1) * P], ident[:])
            last.then_inc(la["t"], 1)
            pe.wait_ge(la["te"], j + 1)
            if exists(j, j - 1):
                pe.wait_ge(la["olo"], j)
            apart(pe)
            for b in range(B):
                p, g = place(b)
                k0 = T * (b % 2)
                for a in range(2):
                    c0 = D * a + (b // 2) * T
                    last = nc.tensor.matmul(ps[:, 4 + b % 2, c0:c0 + T], lat[k0:k0 + T, b // 2, :], dtl[k0:k0 + T, a, g // 2, T * p:T * (p + 1)], start=True, stop=True)
            last.then_inc(la["pv"], 1)

        def l1a_out(pe, j, u):
            pe.wait_ge(la["olo"], j + 1)
            pe.wait_ge(b_split, j + NA + 1)
            for a in range(2):
                last = y_add(lambda t: (ot_hi[:, u, a, t * P:(t + 1) * P], ot_lo[:, u, a, t * P:(t + 1) * P]), wb(u, a * D, D))
            last.then_inc(b_used, 1)

        def l1a_step(pe, j, u):
            l1a_project(pe, j, u)
            if exists(j, j - 1):
                l1a_pv(pe, j - 1, 1 - u)
            l1a_scores(pe, j)
            if exists(j, j - 1):
                l1a_out(pe, j - 1, 1 - u)

        def l1a_pe(pe):
            ln_pe(pe, 4)
            y_start(R_PB)
            pe.wait_ge(ln_lo, 5)
            pe.wait_ge(la["wlo"], 1)
            for c in range(C2):
                last = mm3(ps[:, 0, :], (wl_hi[:, c, :], wl_lo[:, c, :]), (xt_hi[:, c, :], xt_lo[:, c, :]), c == 0, c == 1)
            last.then_inc(la["lt"], 1)
            nc.tensor.matmul(ps[:, 1, :], ones[0:1, :], row[:, R_LB:R_LB + HD].unsqueeze(1).broadcast_to([1, NT, HD]), start=True, stop=False, skip_group_check=True)
            for t in range(NT):
                for c in range(C2):
                    last = mm3(ps[:, 1, t * HD:(t + 1) * HD], xt(c, t * P, P), (wl_hi[:, c, :], wl_lo[:, c, :]), False, t == NT - 1 and c == 1, skip_group_check=True)
            last.then_inc(la["lt"], 1)
            pe.wait_ge(la["lte"], 1)
            nc.tensor.matmul(ps[:, 2, :], rotm[:], lt[:], start=True, stop=True).then_inc(la["rot"], 1)
            pe.wait_ge(la["kr"], 1)
            nc.tensor.matmul(ps[:, 2, :], rotm[:], krot[:, 0, :], start=True, stop=True).then_inc(la["rot"], 1)
            pe.wait_ge(la["late"], 1)
            pe.wait_ge(la["krot"], 1)
            for u in range(2):
                l1a_step(pe, u, u)
            with pe.Fori(1, H // 4) as i:
                for u in range(2):
                    l1a_step(pe, 2 * i + u, u)
            l1a_pv(pe, H // 2 - 1, 1)
            l1a_out(pe, H // 2 - 1, 1)
            y_stop()

        def l1a_pool(pool):
            split_first(pool, L1A)
            ln_pool(pool, 4)
            split_rest(pool, L1A)

        def banks45f():
            return ps[:, 4:6, :].rearrange("p e (a n) -> p e a n", a=2)

        def l1a_act(act):
            ln_act(act, 4)
            nc.scalar.activation(flat(wl_hi[:]), flat(wl[:]), ACT.Copy).then_inc(la["whi"], 1)
            act.wait_ge(la["lt"], 1)
            nc.scalar.activation(lt[:], ps[:, 0, :], ACT.Identity, bias=vec[:, LB:LB + 1]).then_inc(la["lte"], 1)
            act.wait_ge(la["lt"], 2)
            nc.scalar.activation(lat[:].rearrange("p t d -> p (t d)"), ps[:, 1, :], ACT.Copy).then_inc(la["late"], 1)

            def after(j, u):
                act.wait_ge(la["t"], j + 1)
                nc.scalar.activation(dtl[:].rearrange("p a g n -> p (a g n)"), ps[:, 2, :], ACT.Copy).then_inc(la["te"], 1)
                act.wait_ge(la["pv"], j + 1)
                if exists(j, j - 2):
                    act.wait_ge(b_used, j + NA - 1)
                for a in range(2):
                    last = nc.scalar.activation(by_batch(ot_hi[:, u, a, :]), banks45f()[:, :, a, :].rearrange("p e (b k) -> p e b k", k=T), ACT.Copy)
                last.then_inc(la["ohi"], 1)

            def step(j, u):
                if exists(j, j - 1):
                    after(j - 1, 1 - u)
                act.wait_ge(la["sh"], j + 1)
                nc.scalar.activation(pr[:, u, :], st, ACT.Exp, scale=HD ** -0.5).then_inc(la["e"], 1)

            for u in range(2):
                step(u, u)
            with act.Fori(1, H // 4) as i:
                for u in range(2):
                    step(2 * i + u, u)
            after(H // 2 - 1, 1)

        STEPSA = 3

        def l1a_dve(dve):
            ln_dve(dve, 4)
            dve.wait_ge(la["whi"], 1)
            nc.vector.tensor_tensor(flat(wl_lo[:]), flat(wl[:]), flat(wl_hi[:]).bitcast(F32), ALU.subtract).then_inc(la["wlo"], 1)
            rc_, rs_ = (rope[:, k, :].unsqueeze(1).broadcast_to([P, B, T]) for k in range(2))

            def by(ap):
                return ap.rearrange("p (b k) -> p b k", k=T)

            dve.wait_ge(la["lte"], 1)
            nc.vector.tensor_tensor(by(lcos[:]), by(lt[:]), rc_, ALU.mult).then_inc(la["dve"], 1)
            dve.wait_ge(la["rot"], 1)
            nc.vector.tensor_tensor(by(lsin[:]), by(ps[:, 2, :]), rs_, ALU.mult).then_inc(la["dve"], 1)
            dve.wait_ge(la["dve"], 2)
            nc.vector.tensor_tensor(krot[:, 0, :], lcos[:], lsin[:], ALU.subtract).then_inc(la["kr"], 1)
            dve.wait_ge(la["rot"], 2)
            nc.vector.tensor_copy(krot[:, 1, :], ps[:, 2, :]).then_inc(la["krot"], 1)

            def queries(j):
                if exists(j, j - 1):
                    dve.wait_ge(la["s"], j)
                for a in range(2):
                    dve.wait_ge(la["q"] if a == 0 else a_used, j + 1 if a == 0 else j + NA + 1)
                    bias = vec[:, bass.ds(2 * j + (DB + a), 1)]
                    nc.vector.scalar_tensor_tensor(by(qc[:, a, :]), by(ps[:, a, :]), bias, rc_, ALU.add, ALU.mult)
                    last = nc.vector.scalar_tensor_tensor(by(qsn[:, a, :]), by(ps[:, a, :]), bias, rs_, ALU.add, ALU.mult)
                last.then_inc(la["qe"], 1)

            def after(j, u):
                dve.wait_ge(la["ohi"], j + 1)
                for a in range(2):
                    last = nc.vector.tensor_tensor(by_batch(ot_lo[:, u, a, :]), banks45f()[:, :, a, :].rearrange("p e (b k) -> p e b k", k=T),
                                                   by_batch(ot_hi[:, u, a, :]).bitcast(F32), ALU.subtract)
                last.then_inc(la["olo"], 1)

            def step(j, u):
                c = Count(2 + STEPSA * j)
                queries(j)
                if exists(j, j - 1):
                    after(j - 1, 1 - u)
                dve.wait_ge(la["s"], j + 1)
                nc.vector.tensor_tensor(groups(st), groups(ps[:, 3, :]), mask[:].unsqueeze(1).broadcast_to([P, 8, T]), ALU.add).then_inc(la["se"], 1)
                dve.wait_ge(la["se"], j + 1)
                nc.vector.tensor_reduce(mx[:], groups(st), AX.X, ALU.max).then_inc(la["dve"], 1)
                dve.wait_ge(la["dve"], c.up())
                nc.vector.tensor_tensor(groups(st), groups(st), wide(mx[:], 8, T), ALU.subtract).then_inc(la["sh"], 1)
                dve.wait_ge(la["e"], j + 1)
                nc.vector.tensor_reduce(sm[:], groups(pr[:, u, :]), AX.X, ALU.add).then_inc(la["dve"], 1)
                dve.wait_ge(la["dve"], c.up())
                nc.vector.reciprocal(rc[:], sm[:]).then_inc(la["dve"], 1)
                dve.wait_ge(la["dve"], c.up())
                assert c.n == STEPSA
                nc.vector.tensor_tensor(groups(pr[:, u, :]), groups(pr[:, u, :]), wide(rc[:], 8, T), ALU.mult).then_inc(la["p"], 1)

            for u in range(2):
                step(u, u)
            with dve.Fori(1, H // 4) as i:
                for u in range(2):
                    step(2 * i + u, u)
            after(H // 2 - 1, 1)
            add_y(dve, 3)

        NF = L1F[0]
        HALF = 64

        def experts_of(m):
            mid = CH1 // 2
            if m == mid:
                return [(0, 0, HALF, False, True), (1, HALF, P, True, False)]
            return [(0, 0, P, m == 0, False)] if m < mid else [(1, 0, P, False, m == CH1 - 1)]

        def l1f_pe(pe):
            ln_pe(pe, 5)
            pe.wait_ge(ln_lo, 6)
            route_pe(pe, 1)
            pe.wait_ge(ff["comb"], 3)

            def down(i, k):
                m, u, pair = 2 * CH1 * i + CH0 + k, k % 2, k // CH1
                pe.wait_ge(ff["hlo"], m + 1)
                pe.wait_ge(b_split, m + (NF - CH0) + 1)
                for e, r0, r1, first, final in experts_of(k % CH1):
                    if first:
                        pe.wait_ge(ff["ev"], 4 * i + 2 * pair + e + (CH0 - 1))
                    last = ffn_down(m, u, 4 + 2 * e, r0, r1, first, final)
                last.then_inc(b_used, 1)

            with pe.Fori(0, 2) as i:
                for k in range(2 * CH1):
                    m = 2 * CH1 * i + CH0 + k
                    ffn_up(pe, m + (NF - CH0), m, k % 2)
                    if k:
                        down(i, k - 1)
                down(i, 2 * CH1 - 1)

        def l1f_pool(pool):
            split_first(pool, L1F)
            ln_pool(pool, 5)
            split_rest(pool, L1F)

        def l1f_act(act):
            ln_act(act, 5)
            route_act(act, 1)
            with act.Fori(0, 2) as i:
                for k in range(2 * CH1):
                    m = 2 * CH1 * i + CH0 + k
                    ffn_act(act, m, k % 2)
                    ffn_act_hi(act, m, k % 2, m + (NF - CH0) - 1)

        def l1f_dve(dve):
            ln_dve(dve, 5)
            route_dve(dve, 1)
            dve.wait_ge(ff["comb"], 4)
            with dve.Fori(0, 2) as i:
                for k in range(2 * CH1):
                    m = 2 * CH1 * i + CH0 + k
                    ffn_dve(dve, m + (NF - CH0), m, k % 2, None)
                    if (k - 1) % CH1 == CH1 // 2 or (k and k % CH1 == 0):
                        e = 2 * (k // CH1) if k % CH1 else 2 * (k // CH1) - 1
                        ffn_add(dve, 4 + 2 * (e % 2), 4 * i + e, m + (NF - CH0), 4 * i + e + (CH0 + 1))
                ffn_add(dve, 6, 4 * i + 3, 2 * CH1 * i + 2 * CH1 + NF, 4 * i + 3 + (CH0 + 1))

        block = top.enter_context(nc.Block())

        @block.sync
        def _(sp):
            setup_sync(sp)
            for src, stage in zip((w_l0a, w_l0f, w_l1p, w_l1x, w_l1a, w_l1f)[:6], (L0A, L0F, L1P, L1X, L1A, L1F)):
                load_stage(sp, src, stage)
            sp.wait_ge(ff["ev"], CH0 + E1)
            sp.dma_start(out, x[:]).then_inc(stored, 16)
            sp.wait_ge(stored, 16)

        @block.gpsimd
        def _(pool):
            setup_pool(pool)
            ln_pool(pool, 0)
            l0x_pool(pool)
            l0a_pool(pool)
            l0f_pool(pool)
            l1x_pool(pool)
            l1a_pool(pool)
            l1f_pool(pool)

        @block.scalar
        def _(act):
            l0x_act(act)
            l0a_act(act)
            l0f_act(act)
            l1x_act(act)
            l1a_act(act)
            l1f_act(act)

        @block.vector
        def _(dve):
            l0x_dve(dve)
            l0a_dve(dve)
            l0f_dve(dve)
            l1x_dve(dve)
            l1a_dve(dve)
            l1f_dve(dve)

        @block.tensor
        def _(pe):
            l0x_pe(pe)
            l0a_pe(pe)
            l0f_pe(pe)
            l1x_pe(pe)
            l1a_pe(pe)
            l1f_pe(pe)


def kernel(**inputs):
    import numpy as _np
    import concourse.bacc as _bacc
    from concourse import mybir as _mybir
    from concourse.bass_utils import run_bass_kernel_spmd as _run

    g = {k: _np.ascontiguousarray(v) for k, v in inputs.items()}
    cat = _np.concatenate

    def rows_to_partitions(w):
        return w.reshape(C2, P, -1).transpose(1, 0, 2)

    def by_head(w, width):
        n = w.shape[1] // width
        return w.reshape(C2, P, n, width).transpose(2, 1, 0, 3).reshape(n, P, C2 * width)

    def head_rows(w, n):
        return w.reshape(n, P, D)

    wkv = g["L0_xattn_Wkv"]
    w_x0 = rows_to_partitions(cat([g["L0_xattn_Wq"], wkv, g["L0_xattn_Wp"]], axis=1))
    w_l0a = cat([by_head(g["L0_attn_Wq"], HD), by_head(g["L0_attn_Wk"], HD), by_head(g["L0_attn_Wv"], HD), head_rows(g["L0_attn_Wo"], H)], axis=2)
    gu = g["L0_ffn_w_gate_up"].reshape(E0, C2, P, 2, P).transpose(0, 2, 3, 1, 4).reshape(E0, P, 512)
    sgu = g["L0_ffn_w_sh_gate_up"].reshape(C2, P, 2, 4, P).transpose(3, 1, 2, 0, 4).reshape(4, P, 512)
    w_l0f = cat([cat([gu, g["L0_ffn_w_down"]], axis=2), cat([sgu, head_rows(g["L0_ffn_w_sh_down"], 4)], axis=2)], axis=0)
    w_l1p = cat([by_head(g["L1_xattn_q_w"], HD), by_head(g["L1_xattn_ki_w"], HD)], axis=2)
    w_l1x = cat([by_head(g["L1_xattn_vi_w"], HD), head_rows(g["L1_xattn_o_w"], H)], axis=2)
    wd = g["L1_attn_W_d"].reshape(C2, P, H // 2, 2, HD).transpose(2, 1, 3, 0, 4).reshape(H // 2, P, 512)
    wpr = g["L1_attn_W_proj"].reshape(H // 2, 2, P, D).transpose(0, 2, 1, 3).reshape(H // 2, P, 512)
    w_l1a = cat([wd, wpr], axis=2)
    n1 = 4 * CH1

    def turned_rows(w):
        return w.reshape(n1, P, C2, P).transpose(0, 3, 2, 1).reshape(n1, P, 2 * P)

    w_l1f = cat([turned_rows(g["L1_ffn_w1"]), turned_rows(g["L1_ffn_w3"]), g["L1_ffn_w2"].transpose(0, 2, 1).reshape(n1, P, D)], axis=2)
    gates = _np.stack([rows_to_partitions(g["L0_ffn_w_gate"]), rows_to_partitions(g["L1_ffn_Wg"].T)], axis=1)
    cols = [g[k].reshape(H, P).T for k in ("L1_xattn_q_b", "L1_xattn_ki_b", "L1_xattn_vi_b", "L1_xattn_nq_s", "L1_xattn_nki_s", "L1_attn_b_d")]
    vecs = cat(cols + [g["L1_attn_b_latent"].reshape(1, P).T, g["L0_xattn_bkv"][D:].reshape(C2, P).T], axis=1)
    two = [g["L0_xattn_bq"], g["L0_xattn_bkv"][:D], g["L0_xattn_bp"], g["L1_xattn_o_b"], g["L1_attn_b_proj"], g["L1_attn_b_latent"], g["L0_attn_lambda_init"]]
    rows = cat(two).reshape(1, NROW)
    ident = _np.eye(P, dtype=_np.float32)
    key, query = _np.arange(T)[None, :], _np.arange(P)[:, None] % T
    mask = _np.where(key <= query, 0.0, -3.0e38).astype(_np.float32)
    half = HD // 2
    inv = (_np.float32(10000.0) ** (-_np.arange(half, dtype=_np.float32) / _np.float32(half))).astype(_np.float32)
    ang = (_np.arange(T, dtype=_np.float32)[:, None] * inv[None, :]).astype(_np.float32)
    rope = _np.stack([_np.repeat(_np.cos(ang), 2, axis=1).T, _np.repeat(_np.sin(ang), 2, axis=1).T], axis=1).astype(_np.float32)
    rotm = _np.zeros((P, P), _np.float32)
    rotm[_np.arange(0, P, 2), _np.arange(1, P, 2)] = -1.0
    rotm[_np.arange(1, P, 2), _np.arange(0, P, 2)] = 1.0

    named = {
        "x_in": g["x"].reshape(NT, P, D).transpose(1, 0, 2), "ctx_in": g["ctx_2048"].transpose(1, 0, 2), "w_x0": w_x0, "w_l0a": w_l0a, "w_l0f": w_l0f,
        "w_l1p": w_l1p, "w_l1x": w_l1x, "w_l1a": w_l1a, "w_l1f": w_l1f, "gates": gates, "vecs": vecs, "rows": rows,
        "ident_in": ident, "mask_in": mask, "rope_in": rope, "rotm_in": rotm, "wl_in": rows_to_partitions(g["L1_attn_W_latent"]),
    }
    nc = _bacc.Bacc("TRN2", target_bir_lowering=False, num_devices=1)
    arrays, args = {}, {}
    for name, a in named.items():
        arrays[name] = _np.ascontiguousarray(a)
        args[name] = nc.dram_tensor(name, arrays[name].shape, _mybir.dt.from_np(arrays[name].dtype), kind="ExternalInput").ap()
    out = nc.dram_tensor("x_out", (NT, P, D), F32, kind="ExternalOutput").ap()
    build(nc, out=out.rearrange("t p d -> p t d"), **args)
    r = _run(nc, [arrays], core_ids=[0])
    return r.results[0]["x_out"].reshape(B, T, D)
```

```python
from contextlib import ExitStack

import numpy as np

import concourse.bass as bass
from concourse import mybir

ALU = mybir.AluOpType
ACT = mybir.ActivationFunctionType
AX = mybir.AxisListType
F32 = mybir.dt.float32
F32R = mybir.dt.float32r
BF16 = mybir.dt.bfloat16

P = 128
D = 256
C2 = D // P
B, T = 8, 64
NT = B * T // P
NTOK = B * T
S = 128
NKT = B
H = 16
HD0 = 16
HW = 64
HD = 128
E0, E1 = 8, 8
CH0 = 12
CH1 = 11
ROUND = 12582912.0
LN255 = float(np.log(255.0))
RING = 4
SENT = -3.0e38
WA, WB = 768, 512

L0A = (0, 16, 768, 256)
L0F = (16, 12, 512, 256)
L1P = (28, 16, 256, 256)
L1X = (44, 16, 256, 256)
L1A = (60, 8, 512, 512)
L1F = (68, 44, 512, 256)

QB, KB, VB, NQ, NK, DB = 0, 16, 32, 48, 64, 80
LB, XVB = 96, 97
NVEC = 99
R_BQ, R_BK, R_BP, R_OB, R_PB, R_LB, R_LAM = 0, D, 2 * D, 3 * D, 4 * D, 5 * D, 5 * D + HD
NROW = R_LAM + H


def place(b):
    return (b // 2) % 2, 2 * (b // 4) + b % 2


class Count:

    def __init__(self, base):
        self.base, self.n = base, 0

    def up(self):
        self.n += 1
        return self.base + self.n


def build(nc, x_in, ctx_in, w_x0, w_l0a, w_l0f, w_l1p, w_l1x, w_l1a, w_l1f, gates, vecs, rows, ident_in, mask_in, rope_in, rotm_in, wl_in, out):
    with ExitStack() as top:
        def sem(name):
            return top.enter_context(nc.semaphore(name))

        def sb(name, shape, dt=F32, ctx=top):
            return ctx.enter_context(nc.sbuf_tensor(name, shape, dt))

        ps = top.enter_context(nc.psum_tensor("ps", [P, 8, 512], F32))

        x = sb("x", [P, NT, D])
        xn = sb("xn", [P, NT, D])
        xt_hi = sb("xt_hi", [P, C2, NTOK], F32R)
        xt_lo = sb("xt_lo", [P, C2, NTOK], F32R)
        stats = sb("stats", [P, NT, 6])
        mv = sb("mv", [P, NT, 2])
        vareps = sb("vareps", [P, NT])
        rstd = sb("rstd", [P, NT])
        neghalf = sb("neghalf", [P, NT])
        ident = sb("ident", [P, P])
        ident_bf = sb("ident_bf", [P, P], BF16)
        mask = sb("mask", [P, T])
        rope = sb("rope", [P, 2, T])
        vec = sb("vec", [P, NVEC])
        row = sb("row", [1, NROW])
        ones = sb("ones", [P, P])
        zero = sb("zero", [1, 1])
        rnd = sb("rnd", [P, 1])
        gate = sb("gate", [P, 2, C2, 8])
        gate_hi = sb("gate_hi", [P, 2, C2, 8], F32R)
        gate_lo = sb("gate_lo", [P, 2, C2, 8], F32R)
        raw = sb("raw", [P, 2, 1024])
        wa_hi = sb("wa_hi", [P, 2, WA], F32R)
        wa_lo = sb("wa_lo", [P, 2, WA], F32R)
        wb_hi = sb("wb_hi", [P, 2, WB], F32R)
        wb_lo = sb("wb_lo", [P, 2, WB], F32R)
        ctx = sb("ctx", [P, NKT, D])
        soft = sb("soft", [P, 3, 512])
        st, pr = soft[:, 0, :], soft[:, 1:3, :]
        mx = sb("mx", [P, 8])
        sm = sb("sm", [P, 8])
        rc = sb("rc", [P, 8])
        lam = sb("lam", [P, H])
        mo = ExitStack()
        ex = sb("ex", [P, RING, B * S], ctx=mo)
        mo.close()
        ot_hi = sb("ot_hi", [P, 2, 2, 512], F32R)
        ot_lo = sb("ot_lo", [P, 2, 2, 512], F32R)
        rotm = sb("rotm", [P, P])
        wl = sb("wl", [P, C2, HD])
        wl_hi = sb("wl_hi", [P, C2, HD], F32R)
        wl_lo = sb("wl_lo", [P, C2, HD], F32R)

        loaded = [sem("ctx_loaded"), sem("ident_loaded"), sem("x_loaded"), sem("wx_loaded")]
        set_up = sem("set_up")
        passed_pool, passed_pe = sem("passed_pool"), sem("passed_pe")
        ct_t, ct_hi_done, ct_lo_done, wx_split = sem("ct_t"), sem("ct_hi_done"), sem("ct_lo_done"), sem("wx_split")
        consts = sem("consts")
        a_loaded = [sem("a_loaded_0"), sem("a_loaded_1")]
        b_loaded = [sem("b_loaded_0"), sem("b_loaded_1")]
        a_hi, b_hi = sem("a_hi"), sem("b_hi")
        a_split, b_split = sem("a_split"), sem("b_split")
        a_used, b_used = sem("a_used"), sem("b_used")
        ln_step, ln_pow, ln_xn, ln_t, ln_hi, ln_lo = (sem(n) for n in ("ln_step", "ln_pow", "ln_xn", "ln_t", "ln_hi", "ln_lo"))
        x0 = {n: sem("x0_" + n) for n in (
            "wx_hi", "mm", "qe", "ke", "ve", "dve", "qrep", "kd", "k1", "kres", "k2", "krep", "idbf", "vti", "vi_t", "vi",
            "turn", "qt", "kt", "s", "nm", "nb", "e", "rnd_add", "rnd_pool", "rnd_dve", "t", "pt_dve", "pt_act", "pv", "rs", "out", "at_t", "at_hi", "at_lo")}
        l0 = {n: sem("l0_" + n) for n in ("lam", "q", "k", "qe", "ke", "ve", "s", "se", "dve", "sh", "e", "d", "t", "te", "pv", "ohi", "olo")}
        ff = {n: sem("ff_" + n) for n in ("lg", "dve", "shift", "e", "comb", "ghi", "glo", "g", "sg", "h", "hhi", "hlo", "ev")}
        l1 = {n: sem("l1_" + n) for n in ("acc0", "nqk", "sqq", "kst", "qst", "sqk", "acck", "accq", "ms", "sqrt", "rk", "qn", "kn", "s", "se", "dve", "sh", "e", "p", "t", "te", "u", "uhi", "ulo", "ohi", "olo")}
        la = {n: sem("la_" + n) for n in ("whi", "wlo", "lt", "lte", "late", "rot", "dve", "kr", "krot", "q", "qe", "s", "se", "sh", "e", "p", "t", "te", "pv", "ohi", "olo")}

        x_ready = sem("x_ready")
        y_done = sem("y_done")
        stored = sem("stored")

        def mm3(o, a, b, start, stop, **kw):
            nc.tensor.matmul(o, a[0], b[0], start=start, stop=False, **kw)
            nc.tensor.matmul(o, a[0], b[1], start=False, stop=False, **kw)
            return nc.tensor.matmul(o, a[1], b[0], start=False, stop=stop, **kw)

        def xt(c, lo, n):
            return xt_hi[:, c, lo:lo + n], xt_lo[:, c, lo:lo + n]

        def wa(u, lo, n):
            return wa_hi[:, u, lo:lo + n], wa_lo[:, u, lo:lo + n]

        def wb(u, lo, n, k0=0, k1=P):
            return wb_hi[k0:k1, u, lo:lo + n], wb_lo[k0:k1, u, lo:lo + n]

        SET_UP = 6

        def apart(eng):
            eng.sem_inc(passed_pool if eng is nc.gpsimd else passed_pe, 1)

        def load_block(sp, n, k, m, src, stage):
            u, a, cols = k % 2, stage[2], stage[2] + stage[3]
            old = not isinstance(n, int) or n >= 2
            if old:
                sp.wait_ge(a_split, n - 1)
                if isinstance(n, int):
                    sp.wait_ge(b_split, n - 1)
            block_of = src[bass.ds(m, 1)].rearrange("a p m -> p (a m)")
            sp.dma_start(raw[:, u, 0:a], block_of[:, 0:a]).then_inc(a_loaded[u], 16)
            if old:
                sp.wait_ge(b_split, n - 1)
            sp.dma_start(raw[:, u, a:cols], block_of[:, a:cols]).then_inc(b_loaded[u], 16)

        def load_stage(sp, src, stage):
            first, count = stage[0], stage[1]
            for u in range(2):
                load_block(sp, first + u, u, u, src, stage)
            with sp.Fori(1, count // 2) as i:
                for u in range(2):
                    load_block(sp, 2 * i + (first + u), u, 2 * i + u, src, stage)

        def hi_part(act, part, i, k, stage, stride=2):
            n, u = stride * i + k, k % 2
            old = not isinstance(n, int) or n >= 2
            cols = slice(0, stage[2]) if part == "a" else slice(stage[2], stage[2] + stage[3])
            dst, loaded_, done, used = (wa_hi, a_loaded, a_hi, a_used) if part == "a" else (wb_hi, b_loaded, b_hi, b_used)
            act.wait_ge(loaded_[u], 16 * ((stride // 2) * i + k // 2) + 16)
            if old:
                act.wait_ge(used, n - 1)
            nc.scalar.activation(dst[:, u, 0:cols.stop - cols.start], raw[:, u, cols], ACT.Copy).then_inc(done, 1)

        def lo_part(pool, part, i, k, stage, stride=2):
            n, u = stride * i + k, k % 2
            cols = slice(0, stage[2]) if part == "a" else slice(stage[2], stage[2] + stage[3])
            hi, lo, ready, done = (wa_hi, wa_lo, a_hi, a_split) if part == "a" else (wb_hi, wb_lo, b_hi, b_split)
            w = cols.stop - cols.start
            pool.wait_ge(ready, n + 1)
            nc.gpsimd.tensor_tensor(lo[:, u, 0:w], raw[:, u, cols], hi[:, u, 0:w].bitcast(F32), ALU.subtract).then_inc(done, 1)

        def next_part(f, eng, i, u, stage, following, lead=1):
            n = 2 * i + u + lead if isinstance(i, int) else 0
            if n < stage[1] or (n == stage[1] and following):
                f(eng, "a", i, stage[0] + u + lead, following if n == stage[1] else stage)

        def peeled(eng, count, step):
            for u in range(2):
                step(0, u)
            with eng.Fori(1, count // 2 - 1) as i:
                for u in range(2):
                    step(i, u)
            for u in range(2):
                step(count // 2 - 1, u)

        def lo_parts(pool, stage, following, lead=1):
            def step(i, u):
                lo_part(pool, "b", i, stage[0] + u, stage)
                next_part(lo_part, pool, i, u, stage, following, lead)

            peeled(pool, stage[1], step)

        LNS = 3

        def ln_dve_stats(dve, n):
            for t in range(NT):
                last = nc.vector.bn_stats(stats[:, t, :], x[:, t, :])
            last.then_inc(ln_step, 1)
            dve.wait_ge(ln_step, LNS * n + 1)
            for t in range(NT):
                last = nc.vector.bn_aggr(mv[:, t, :], stats[:, t, :])
            last.then_inc(ln_step, 1)
            dve.wait_ge(ln_step, LNS * n + 2)
            nc.vector.tensor_scalar(vareps[:], mv[:, :, 1], 1e-5, None, ALU.add).then_inc(ln_step, 1)
            dve.wait_ge(ln_pow, n + 1)
            for t in range(NT):
                last = nc.vector.tensor_scalar(xn[:, t, :], x[:, t, :], mv[:, t, 0:1], rstd[:, t:t + 1], ALU.subtract, ALU.mult)
            last.then_inc(ln_xn, 1)

        def ln_dve_split(dve, n):
            dve.wait_ge(ln_hi, n + 1)
            nc.vector.tensor_tensor(xt_lo[:].rearrange("p c n -> p (c n)"), ps[:, 0:2, :].rearrange("p c n -> p (c n)"),
                                    xt_hi[:].rearrange("p c n -> p (c n)").bitcast(F32), ALU.subtract).then_inc(ln_lo, 1)

        def ln_dve(dve, n):
            ln_dve_stats(dve, n)
            ln_dve_split(dve, n)

        def ln_pool(pool, n):
            pool.wait_ge(ln_step, LNS * n + 3)
            nc.gpsimd.tensor_tensor(rstd[:], vareps[:], neghalf[:], ALU.pow).then_inc(ln_pow, 1)

        def ln_pe(pe, n):
            pe.wait_ge(ln_xn, n + 1)
            for c in range(C2):
                for t in range(NT):
                    last = nc.tensor.transpose(ps[:, c, t * P:(t + 1) * P], xn[:, t, c * P:(c + 1) * P], ident[:])
            last.then_inc(ln_t, 1)

        def ln_act(act, n):
            act.wait_ge(ln_t, n + 1)
            nc.scalar.activation(xt_hi[:].rearrange("p c n -> p (c n)"), ps[:, 0:2, :].rearrange("p c n -> p (c n)"), ACT.Copy).then_inc(ln_hi, 1)

        def twice(off):
            return row[:, off:off + D].unsqueeze(1).broadcast_to([1, 2, D])

        def y_start(off):
            src = twice(off) if off is not None else zero[:, :].broadcast_to([1, 512])
            for k in range(2):
                nc.tensor.matmul(ps[:, 6 + k, :], ones[0:1, :], src, start=True, stop=False, skip_group_check=True)

        def y_add(o, w):
            for t in range(NT):
                last = mm3(ps[:, 6 + t // 2, (t % 2) * D:(t % 2 + 1) * D], o(t), w, False, False, skip_group_check=True)
            return last

        def y_stop():
            for k in range(2):
                last = nc.tensor.matmul(ps[:, 6 + k, :], ones[0:1, :], zero[:, :].broadcast_to([1, 512]), start=False, stop=True, skip_group_check=True)
            last.then_inc(y_done, 1)

        def add_y(dve, n):
            dve.wait_ge(y_done, n + 1)
            for k in range(2):
                v = x[:, 2 * k:2 * k + 2, :].rearrange("p t d -> p (t d)")
                last = nc.vector.tensor_tensor(v, ps[:, 6 + k, :], v, ALU.add)
            last.then_inc(x_ready, 1)
            dve.wait_ge(x_ready, n + 1)

        def flat(ap):
            return ap.rearrange("p a b -> p (a b)")

        mc = ExitStack()
        ct_hi = sb("ct_hi", [P, C2, B * S], F32R, mc)
        ct_lo = sb("ct_lo", [P, C2, B * S], F32R, mc)
        acc = sb("acc", [P, 1536], ctx=mc)
        m0 = ExitStack()
        wx = sb("wx", [P, C2, 1024], ctx=m0)
        wx_hi = sb("wx_hi", [P, C2, 1024], F32R, m0)
        wx_lo = sb("wx_lo", [P, C2, 1024], F32R, m0)
        qf = sb("qf", [P, NT, D], ctx=m0)
        kf = sb("kf", [P, NKT, D], ctx=m0)
        vf = sb("vf", [P, C2, B * S], ctx=m0)
        kres = sb("kres", [P, NKT, D], ctx=m0)
        qs = sb("qs", [P, NT * H], ctx=m0)
        qr = sb("qr", [P, NT * H], ctx=m0)
        ks = sb("ks", [P, NKT * H], ctx=m0)
        kr = sb("kr", [P, NKT * H], ctx=m0)
        vs = sb("vs", [P, C2], ctx=m0)
        vr = sb("vr", [P, C2], ctx=m0)
        q_rep = sb("q_rep", [P, NT, (H + 2) * HW], BF16, m0)
        k_rep = sb("k_rep", [P, NKT, (H + 2) * HW], BF16, m0)
        vti = sb("vti", [P, C2, B * S], BF16, m0)
        vi = sb("vi", [P, NKT, D], BF16, m0)
        qt = sb("qt", [P, 2, NTOK], BF16, m0)
        kt = sb("kt", [P, 2, B * S], BF16, m0)
        ei = flat(kres[:]).bitcast(BF16).rearrange("p (r n) -> p r n", r=RING)
        pt = flat(vf[:]).bitcast(BF16).rearrange("p (r n) -> p r n", r=RING)
        nm = sb("nm", [P, 2], ctx=m0)
        nb = sb("nb", [P, 2], ctx=m0)
        sums = sb("sums", [P, 2, 8], ctx=m0)
        rs = sb("rs", [P, 8], ctx=m0)
        m0.close()
        m1 = ExitStack()
        qh = sb("qh", [P, 512], ctx=m1)
        kh = sb("kh", [P, 512], ctx=m1)
        vh = sb("vh", [P, 2, NT, HD], ctx=m1)
        dd = sb("dd", [P, 2, 256], ctx=m1)
        ddt = sb("ddt", [P, 2, P], ctx=m1)
        m1.close()
        m2 = ExitStack()
        lg = sb("lg", [P, NT, 16], ctx=m2)
        top8 = sb("top8", [P, NT, 8], ctx=m2)
        rep = sb("rep", [P, NT, 16], ctx=m2)
        sel = sb("sel", [P, NT, 8], ctx=m2)
        sh = sb("sh", [P, NT, 8], ctx=m2)
        ssum = sb("ssum", [P, NT], ctx=m2)
        comb = sb("comb", [P, CH0, NT], ctx=m2)
        sg = sb("sg", [P, 2, 512], ctx=m2)
        hh = sb("hh", [P, 2, 512], ctx=m2)
        h_hi = sb("h_hi", [P, 2, 512], F32R, m2)
        h_lo = sb("h_lo", [P, 2, 512], F32R, m2)
        m2.close()
        m3 = ExitStack()
        kst = sb("kst", [P, H, B * S], ctx=m3)
        qst = sb("qst", [P, H, NTOK], ctx=m3)
        nqk = sb("nqk", [P, H], ctx=m3)
        epsc = sb("epsc", [P, 1], ctx=m3)
        m3.close()
        sq = flat(soft[:])
        rq = flat(xn[:, 0:2, :])
        rk = flat(xn[:, 2:4, :]).rearrange("p (g k) -> p g k", g=4)
        m4 = ExitStack()
        qc = sb("qc", [P, 2, 512], ctx=m4)
        qsn = sb("qsn", [P, 2, 512], ctx=m4)
        lt = sb("lt", [P, NTOK], ctx=m4)
        lat = sb("lat", [P, NT, HD], ctx=m4)
        krot = sb("krot", [P, 2, NTOK], ctx=m4)
        lcos = sb("lcos", [P, NTOK], ctx=m4)
        lsin = sb("lsin", [P, NTOK], ctx=m4)
        dtl = sb("dtl", [P, 2, 2, P], ctx=m4)
        m4.close()
        mc.close()
        mu = ExitStack()
        qn = sb("qn", [P, 2, NTOK], ctx=mu)
        kn = sb("kn", [P, 2, B * S], ctx=mu)
        ptx = sb("ptx", [P, 4, P], ctx=mu)
        u_hi = sb("u_hi", [P, C2, 512], F32R, mu)
        u_lo = sb("u_lo", [P, C2, 512], F32R, mu)
        mu.close()

        NLOAD, NCONST = 2, 8

        def setup_sync(sp):
            sp.dma_start(ctx[:], ctx_in).then_inc(loaded[0], 16)
            sp.dma_start(ident[:], ident_in).then_inc(loaded[1], 16)
            sp.dma_start(x[:], x_in).then_inc(loaded[2], 16)
            sp.dma_start(wx[:], w_x0).then_inc(loaded[3], 16)
            for dst, src in ((row, rows), (vec, vecs), (mask, mask_in), (rope, rope_in), (gate, gates), (rotm, rotm_in), (wl, wl_in)):
                sp.dma_start(dst[:], src).then_inc(consts, 16)

        CONSTS = 7 * 16

        def setup_pool(pool):
            nc.gpsimd.memset(ones[:], 1.0).then_inc(set_up, 1)
            nc.gpsimd.memset(zero[:], 0.0).then_inc(set_up, 1)
            nc.gpsimd.memset(neghalf[:], -0.5).then_inc(set_up, 1)
            nc.gpsimd.memset(rnd[:], ROUND).then_inc(set_up, 1)
            nc.gpsimd.memset(q_rep[:], 0.0).then_inc(set_up, 1)
            nc.gpsimd.memset(k_rep[:], 0.0).then_inc(set_up, 1)

        def bank_bf(b):
            return ps[:, b, :].bitcast(BF16)

        VBANK = ((6, 8), (0, 2))

        def l0x_pe_before(pe):
            pe.wait_ge(loaded[0], 16)
            pe.wait_ge(loaded[1], 16)
            for c in range(C2):
                for k in range(NKT):
                    last = nc.tensor.transpose(ps[:, 2 + 2 * c + k // 4, (k % 4) * P:(k % 4 + 1) * P], ctx[:, k, c * P:(c + 1) * P], ident[:])
            last.then_inc(ct_t, 1)
            ln_pe(pe, 0)
            pe.wait_ge(ln_lo, 1)
            pe.wait_ge(wx_split, 1)
            pe.wait_ge(consts, CONSTS)
            for k in range(2):
                nc.tensor.matmul(ps[:, k, :], ones[0:1, :], twice(R_BQ), start=True, stop=False, skip_group_check=True)
                for t in (2 * k, 2 * k + 1):
                    for c in range(C2):
                        last = mm3(ps[:, k, (t % 2) * D:(t % 2 + 1) * D], xt(c, t * P, P), (wx_hi[:, c, 0:D], wx_lo[:, c, 0:D]),
                                   False, t % 2 == 1 and c == 1, skip_group_check=True)
            last.then_inc(x0["mm"], 1)
            pe.wait_ge(ct_lo_done, 1)
            for k in range(4):
                nc.tensor.matmul(ps[:, 2 + k, :], ones[0:1, :], twice(R_BK), start=True, stop=False, skip_group_check=True)
                for t in (2 * k, 2 * k + 1):
                    for c in range(C2):
                        last = mm3(ps[:, 2 + k, (t % 2) * D:(t % 2 + 1) * D], (ct_hi[:, c, t * P:(t + 1) * P], ct_lo[:, c, t * P:(t + 1) * P]),
                                   (wx_hi[:, c, D:2 * D], wx_lo[:, c, D:2 * D]), False, t % 2 == 1 and c == 1, skip_group_check=True)
            last.then_inc(x0["mm"], 1)
            for m in range(C2):
                if m == 1:
                    pe.wait_ge(x0["qe"], 1)
                for j in range(2):
                    for c in range(C2):
                        cols = slice(2 * D + m * P, 2 * D + (m + 1) * P)
                        last = mm3(ps[:, VBANK[m][0] + j, :], (wx_hi[:, c, cols], wx_lo[:, c, cols]),
                                   (ct_hi[:, c, j * 512:(j + 1) * 512], ct_lo[:, c, j * 512:(j + 1) * 512]), c == 0, c == 1)
                last.then_inc(x0["mm"], 1)
            pe.wait_ge(x0["qrep"], 1)
            pe.wait_ge(x0["krep"], 1)
            pe.wait_ge(x0["ve"], 2)
            pe.wait_ge(x0["idbf"], 1)
            l0x_turn(pe, 0, 0)
            pe.wait_ge(x0["vti"], 1)
            for k in range(NKT):
                for c in range(C2):
                    last = nc.tensor.transpose(bank_bf(2 + k // 4)[:, (k % 4) * D + c * P:(k % 4) * D + (c + 1) * P], vti[:, c, k * P:(k + 1) * P], ident_bf[:])
            last.then_inc(x0["vi_t"], 1)
            pe.wait_ge(x0["vi"], 1)

        def l0x_turn(pe, pair, u):
            for t in range(NT):
                nc.tensor.transpose(bank_bf(0)[:, t * P:(t + 1) * P], q_rep[:, t, bass.ds(pair * 2 * HW, P)], ident_bf[:])
            for t in range(NKT):
                last = nc.tensor.transpose(bank_bf(1)[:, t * P:(t + 1) * P], k_rep[:, t, bass.ds(pair * 2 * HW, P)], ident_bf[:])
            last.then_inc(x0["turn"], 1)

        TL, VL, TURN, OUT = 4, 6, 2, 5
        EV_ACT = tuple(r for r in range(16) if r % 8 != 6)
        RND_POOL = (1, 4, 9, 12)

        def shared(i, m, mine, sem_mine, sem_other):
            q, r = divmod(m, 16)
            if r in mine:
                return sem_mine, (i + q) * len(mine) + len([a for a in mine if a <= r])
            return sem_other, (i + q) * (16 - len(mine)) + len([a for a in range(r + 1) if a not in mine])

        def copied(i, m):
            return shared(i, m, EV_ACT, x0["pt_act"], x0["pt_dve"])

        def rounded(i, m):
            return shared(i, m, RND_POOL, x0["rnd_pool"], x0["rnd_dve"])

        def exists(i, n):
            return not isinstance(i, int) or n >= 0

        def l0x_pe_unit(pe, i, m, live=True):
            n, k, a, t = 16 * i + m, m % 8, (m % 8) // 4, m % 4
            pair, u = 2 * i + m // 8, (m // 8) % 2
            if live:
                if k == 0:
                    pe.wait_ge(x0["qt"], pair + 1)
                    pe.wait_ge(x0["kt"], pair + 1)
                if exists(i, n - 2):
                    pe.wait_ge(x0["e"], n - 1)
                for j in range(2):
                    last = nc.tensor.matmul(ps[:, 2 + 2 * (m % 2) + j, :], qt[64 * a:64 * a + 48, u, t * P:(t + 1) * P],
                                            kt[64 * a:64 * a + 48, u, j * 512:(j + 1) * 512], start=True, stop=True)
                last.then_inc(x0["s"], 1)
            if exists(i, n - TL) and (live or m < TL):
                pe.wait_ge(*rounded(i, m - TL))
                if exists(i, n - TL - 2):
                    pe.wait_ge(*copied(i, m - TL - 2))
                for kk in range(NKT):
                    last = nc.tensor.transpose(bank_bf(6 + (m - TL) % 2)[:, kk * P:(kk + 1) * P], ei[:, (m - TL) % RING, kk * P:(kk + 1) * P], ident_bf[:])
                last.then_inc(x0["t"], 1)
            if exists(i, n - VL):
                q, kp = divmod(m - VL, 8)
                if kp == 0 and exists(i, n - VL - 1):
                    pe.wait_ge(x0["out"], 2 * i + q)
                if live and k == TURN + 1:
                    pe.wait_ge(x0["qt"], pair + 2)
                pe.wait_ge(*copied(i, m - VL))
                for kk in range(NKT):
                    last = nc.tensor.matmul(ps[:, 0, 256 + 16 * kp:272 + 16 * kp], pt[:, (m - VL) % RING, kk * P:(kk + 1) * P],
                                            vi[:, kk, bass.ds((2 * i + q) * 32 + (kp // 4) * HD0, HD0)], start=kk == 0, stop=kk == NKT - 1)
                last.then_inc(x0["pv"], 1)
            if live and k == TURN:
                l0x_turn(pe, pair + 1, 1 - u)

        def l0x_pe(pe):
            l0x_pe_before(pe)
            for m in range(16):
                l0x_pe_unit(pe, 0, m)
            with pe.Fori(1, 4) as i:
                for m in range(16):
                    l0x_pe_unit(pe, i, m)
            for m in range(VL):
                l0x_pe_unit(pe, 4, m, live=False)
            pe.wait_ge(x0["out"], 8)
            for c in range(C2):
                for t in range(NT):
                    last = nc.tensor.transpose(ps[:, 2 + c, t * P:(t + 1) * P], xn[:, t, c * P:(c + 1) * P], ident[:])
            last.then_inc(x0["at_t"], 1)
            y_start(R_BP)
            pe.wait_ge(x0["at_lo"], 1)
            for c in range(C2):
                y_add(lambda t: xt(c, t * P, P), (wx_hi[:, c, 3 * D:], wx_lo[:, c, 3 * D:]))
            y_stop()

        def l0x_pool(pool):
            pool.wait_ge(x0["wx_hi"], 1)
            nc.gpsimd.tensor_tensor(flat(wx_lo[:]), flat(wx[:]), flat(wx_hi[:]).bitcast(F32), ALU.subtract).then_inc(wx_split, 1)

            def unit(i, m):
                n, r = 16 * i + m, rounded(i, m)[1]
                pool.wait_ge(x0["e"], n + 1)
                if exists(i, n - RING):
                    pool.wait_ge(x0["t"], n - RING + 1)
                nc.gpsimd.tensor_tensor(ex[:, m % RING, :], ex[:, m % RING, :], rnd[:, :].broadcast_to([P, B * S]), ALU.add).then_inc(x0["rnd_add"], 1)
                pool.wait_ge(x0["rnd_add"], r)
                nc.gpsimd.tensor_tensor(ei[:, m % RING, :], ex[:, m % RING, :], rnd[:, :].broadcast_to([P, B * S]), ALU.subtract).then_inc(x0["rnd_pool"], 1)

            for m in RND_POOL:
                unit(0, m)
            with pool.Fori(1, 4) as i:
                for m in RND_POOL:
                    unit(i, m)

        def l0x_copy_pt(eng, i, m):
            n = 16 * i + m
            act = m % 16 in EV_ACT
            eng.wait_ge(x0["t"], n + 1)
            if exists(i, n - RING):
                eng.wait_ge(x0["pv"], n - RING + 1)
            if act:
                nc.scalar.activation(pt[:, m % RING, :], bank_bf(6 + m % 2), ACT.Copy).then_inc(x0["pt_act"], 1)
            else:
                nc.vector.tensor_copy(pt[:, m % RING, :], bank_bf(6 + m % 2)).then_inc(x0["pt_dve"], 1)

        def l0x_act(act):
            act.wait_ge(loaded[3], 16)
            nc.scalar.activation(flat(wx_hi[:]), flat(wx[:]), ACT.Copy).then_inc(x0["wx_hi"], 1)
            act.wait_ge(ct_t, 1)
            for c in range(C2):
                last = nc.scalar.activation(ct_hi[:, c, :], flat(ps[:, 2 + 2 * c:4 + 2 * c, :]), ACT.Copy)
            last.then_inc(ct_hi_done, 1)
            ln_act(act, 0)
            act.wait_ge(x0["mm"], 1)
            nc.scalar.activation(flat(qf[:]), flat(ps[:, 0:2, :]), ACT.Copy, scale=0.25).then_inc(x0["qe"], 1)
            act.wait_ge(x0["mm"], 2)
            nc.scalar.activation(flat(kf[:]), flat(ps[:, 2:6, :]), ACT.Copy).then_inc(x0["ke"], 1)
            for c in range(C2):
                act.wait_ge(x0["mm"], 3 + c)
                nc.scalar.activation(vf[:, c, :], flat(ps[:, VBANK[c][0]:VBANK[c][1], :]), ACT.Identity, bias=vec[:, XVB + c:XVB + c + 1]).then_inc(x0["ve"], 1)
            act.wait_ge(x0["kd"], 1)
            kp = k_rep[:, :, 0:H * HW].rearrange("p t (h w) -> p t h w", w=HW)
            kv = kf[:].rearrange("p t (h e) -> p t h e", e=HD0)
            nc.scalar.activation(kp[:, :, :, 0:HD0], kv, ACT.Copy).then_inc(x0["k1"], 1)
            act.wait_ge(x0["kres"], 1)
            nc.scalar.activation(kp[:, :, :, HD0:2 * HD0], kres[:].rearrange("p t (h e) -> p t h e", e=HD0), ACT.Copy).then_inc(x0["k2"], 1)

            def turned(pair, u):
                act.wait_ge(x0["turn"], pair + 1)
                nc.scalar.activation(qt[:, u, :], bank_bf(0)[:, 0:NTOK], ACT.Copy).then_inc(x0["qt"], 1)

            def unit(i, m, live=True):
                n, k, pair, u = 16 * i + m, m % 8, 2 * i + m // 8, (m // 8) % 2
                if live:
                    act.wait_ge(x0["nb"], n + 1)
                    if exists(i, n - RING):
                        act.wait_ge(*rounded(i, m - RING))
                    if k == 0 and exists(i, n - 16):
                        act.wait_ge(x0["out"], pair - 1)
                    col = (m % 4) * H + (m % 8) // 4
                    nc.scalar.activation(ex[:, m % RING, :], flat(ps[:, 2 + 2 * (m % 2):4 + 2 * (m % 2), :]), ACT.Exp, bias=nb[:, m % 2:m % 2 + 1],
                                         scale=qs[:, bass.ds(2 * pair + col, 1)], accum_out=sums[:, u, k:k + 1]).then_inc(x0["e"], 1)
                if live and k == TURN:
                    turned(pair + 1, 1 - u)
                if (m - TL) % 16 in EV_ACT and exists(i, n - TL) and (live or m < TL):
                    l0x_copy_pt(act, i, m - TL)

            turned(0, 0)
            for m in range(16):
                unit(0, m)
            with act.Fori(1, 4) as i:
                for m in range(16):
                    unit(i, m)
            for m in range(TL):
                unit(4, m, live=False)
            act.wait_ge(x0["at_t"], 1)
            for c in range(C2):
                last = nc.scalar.activation(xt_hi[:, c, :], ps[:, 2 + c, :], ACT.Copy, scale=vs[:, c:c + 1])
            last.then_inc(x0["at_hi"], 1)

        def l0x_dve(dve):
            c = Count(0)
            step = x0["dve"]
            dve.wait_ge(loaded[1], 16)
            nc.vector.tensor_copy(ident_bf[:], ident[:]).then_inc(x0["idbf"], 1)
            dve.wait_ge(loaded[2], 16)
            dve.wait_ge(set_up, SET_UP)
            ln_dve_stats(dve, 0)
            dve.wait_ge(ct_hi_done, 1)
            for k in range(C2):
                last = nc.vector.tensor_tensor(ct_lo[:, k, :], flat(ps[:, 2 + 2 * k:4 + 2 * k, :]), ct_hi[:, k, :].bitcast(F32), ALU.subtract)
            last.then_inc(ct_lo_done, 1)
            ln_dve_split(dve, 0)

            def scale_of(src, s, r):
                nc.vector.tensor_reduce(s, src, AX.X, ALU.max, apply_absolute_value=True).then_inc(step, 1)
                dve.wait_ge(step, c.up())
                nc.vector.tensor_scalar(s, s, 1.0 / 127.0, 1e-8, ALU.mult, ALU.max).then_inc(step, 1)
                dve.wait_ge(step, c.up())
                nc.vector.reciprocal(r, s).then_inc(step, 1)
                dve.wait_ge(step, c.up())

            qv = qf[:].rearrange("p t (h e) -> p (t h) e", e=HD0)
            kv = kf[:].rearrange("p t (h e) -> p (t h) e", e=HD0)
            kp = k_rep[:, :, 0:H * HW].rearrange("p t (h w) -> p t h w", w=HW)
            kv4, krv = kf[:].rearrange("p t (h e) -> p t h e", e=HD0), kres[:].rearrange("p t (h e) -> p t h e", e=HD0)
            dve.wait_ge(x0["qe"], 1)
            scale_of(qv, qs[:], qr[:])
            nc.vector.tensor_tensor(qv, qv, qr[:].unsqueeze(2).broadcast_to([P, NT * H, HD0]), ALU.mult).then_inc(step, 1)
            dve.wait_ge(step, c.up())
            for r in range(3):
                for t in range(NT):
                    dst = q_rep[:, t, 0:H * HW].rearrange("p (h w) -> p h w", w=HW)[:, :, r * HD0:(r + 1) * HD0]
                    last = nc.vector.tensor_scalar(dst, qf[:, t, :].rearrange("p (h e) -> p h e", e=HD0), ROUND, ROUND, ALU.add, ALU.subtract)
            last.then_inc(x0["qrep"], 1)
            dve.wait_ge(x0["ke"], 1)
            scale_of(kv, ks[:], kr[:])
            nc.vector.tensor_tensor(kv, kv, kr[:].unsqueeze(2).broadcast_to([P, NKT * H, HD0]), ALU.mult).then_inc(step, 1)
            dve.wait_ge(step, c.up())
            nc.vector.tensor_scalar(flat(kf[:]), flat(kf[:]), ROUND, ROUND, ALU.add, ALU.subtract).then_inc(step, 1)
            dve.wait_ge(step, c.up())
            nc.vector.tensor_tensor(kv, kv, ks[:].unsqueeze(2).broadcast_to([P, NKT * H, HD0]), ALU.mult).then_inc(x0["kd"], 1)
            dve.wait_ge(x0["kd"], 1)
            dve.wait_ge(x0["k1"], 1)
            nc.vector.tensor_tensor(krv, kv4, kp[:, :, :, 0:HD0], ALU.subtract).then_inc(x0["kres"], 1)
            dve.wait_ge(x0["kres"], 1)
            dve.wait_ge(x0["k2"], 1)
            nc.vector.tensor_tensor(kp[:, :, :, 2 * HD0:3 * HD0], krv, kp[:, :, :, HD0:2 * HD0], ALU.subtract).then_inc(x0["krep"], 1)
            dve.wait_ge(x0["ve"], 2)
            scale_of(vf[:], vs[:], vr[:])
            for k in range(C2):
                last = nc.vector.tensor_scalar(vf[:, k, :], vf[:, k, :], vr[:, k:k + 1], ROUND, ALU.mult, ALU.add)
            last.then_inc(step, 1)
            dve.wait_ge(step, c.up())
            nc.vector.tensor_scalar(flat(vti[:]), flat(vf[:]), ROUND, None, ALU.subtract).then_inc(x0["vti"], 1)

            def turned(pair, u):
                dve.wait_ge(x0["turn"], pair + 1)
                nc.vector.tensor_copy(kt[:, u, :], bank_bf(1)).then_inc(x0["kt"], 1)

            def outputs(pair, u):
                dve.wait_ge(x0["pv"], 8 * pair + 8)
                nc.vector.reciprocal(rs[:], sums[:, u, :]).then_inc(x0["rs"], 1)
                dve.wait_ge(x0["rs"], pair + 1)
                for a in range(2):
                    last = nc.vector.tensor_tensor(xn[:, :, bass.ds(32 * pair + HD0 * a, HD0)], ps[:, 0, 256 + 64 * a:320 + 64 * a].rearrange("p (t e) -> p t e", t=NT),
                                                   rs[:, 4 * a:4 * a + 4].unsqueeze(2).broadcast_to([P, NT, HD0]), ALU.mult)
                last.then_inc(x0["out"], 1)

            def unit(i, m, live=True):
                n, k, pair, u = 16 * i + m, m % 8, 2 * i + m // 8, (m // 8) % 2
                if live:
                    dve.wait_ge(x0["s"], n + 1)
                    nc.vector.tensor_reduce(nm[:, m % 2:m % 2 + 1], flat(ps[:, 2 + 2 * (m % 2):4 + 2 * (m % 2), :]), AX.X, ALU.max, negate=True).then_inc(x0["nm"], 1)
                    dve.wait_ge(x0["nm"], n + 1)
                    if exists(i, n - 2):
                        dve.wait_ge(x0["e"], n - 1)
                    col = (m % 4) * H + (m % 8) // 4
                    nc.vector.tensor_scalar(nb[:, m % 2:m % 2 + 1], nm[:, m % 2:m % 2 + 1], qs[:, bass.ds(2 * pair + col, 1)], LN255, ALU.mult, ALU.add).then_inc(x0["nb"], 1)
                if k == OUT and exists(i, n - 8):
                    outputs(pair - 1, 1 - u)
                if (m - 1) % 16 not in RND_POOL and exists(i, n - 1) and (live or m < 1):
                    dve.wait_ge(x0["e"], n)
                    if exists(i, n - 1 - RING):
                        dve.wait_ge(x0["t"], n - RING)
                    nc.vector.tensor_scalar(ei[:, (m - 1) % RING, :], ex[:, (m - 1) % RING, :], ROUND, ROUND, ALU.add, ALU.subtract).then_inc(x0["rnd_dve"], 1)
                if (m - TL) % 16 not in EV_ACT and exists(i, n - TL) and (live or m < TL):
                    l0x_copy_pt(dve, i, m - TL)
                if live and k == TURN:
                    turned(pair + 1, 1 - u)

            turned(0, 0)
            dve.wait_ge(x0["vi_t"], 1)
            nc.vector.tensor_copy(vi[:].rearrange("p k d -> p (k d)"), flat(ps[:, 2:4, :]).bitcast(BF16)).then_inc(x0["vi"], 1)
            for m in range(16):
                unit(0, m)
            with dve.Fori(1, 4) as i:
                for m in range(16):
                    unit(i, m)
            for m in range(OUT + 1):
                unit(4, m, live=False)
            dve.wait_ge(x0["at_hi"], 1)
            for k in range(C2):
                last = nc.vector.scalar_tensor_tensor(xt_lo[:, k, :], ps[:, 2 + k, :], vs[:, k:k + 1], xt_hi[:, k, :].bitcast(F32), ALU.mult, ALU.subtract)
            last.then_inc(x0["at_lo"], 1)
            add_y(dve, 0)

        N1 = L0A[0]

        def by_batch(ap):
            return ap.rearrange("p (b e k) -> p e b k", e=2, k=T)

        def banks45():
            return ps[:, 4:6, 0:256].rearrange("p e (b k) -> p e b k", k=T)

        def l0a_project(pe, h, u):
            n = h + N1
            pe.wait_ge(a_split, n + 1)
            for k, name in enumerate(("q", "k")):
                if exists(h, h - 1):
                    pe.wait_ge(l0["se"], h)
                for c in range(C2):
                    last = mm3(ps[:, k, :], wa(u, 2 * P * k + c * P, P), (xt_hi[:, c, :], xt_lo[:, c, :]), c == 0, c == 1)
                last.then_inc(l0[name], 1)
            if exists(h, h - 1):
                pe.wait_ge(l0["ve"], h)
            for t in range(NT):
                for c in range(C2):
                    last = mm3(ps[:, 2, t * P:(t + 1) * P], xt(c, t * P, P), wa(u, 4 * P + c * P, P), c == 0, c == 1)
            last.then_inc(a_used, 1)

        def l0a_turn(pe, h, u):
            pe.wait_ge(l0["d"], h + 1)
            if exists(h, h - 1):
                pe.wait_ge(l0["te"], h)
            for g in range(2):
                last = nc.tensor.transpose(ps[:, 3, g * P:(g + 1) * P], dd[:, u, g * P:(g + 1) * P], ident[:])
            last.then_inc(l0["t"], 1)

        def l0a_pv(pe, h, u):
            pe.wait_ge(l0["te"], h + 1)
            if exists(h, h - 1):
                pe.wait_ge(l0["olo"], h)
            apart(pe)
            for b in range(B):
                p, g = place(b)
                k0 = T * (b % 2)
                last = nc.tensor.matmul(ps[:, 4 + b % 2, (b // 2) * T:(b // 2 + 1) * T], vh[k0:k0 + T, u, b // 2, :], ddt[k0:k0 + T, g // 2, T * p:T * (p + 1)], start=True, stop=True)
            last.then_inc(l0["pv"], 1)

        def l0a_scores(pe, h, u):
            pe.wait_ge(l0["qe"], h + 1)
            pe.wait_ge(l0["ke"], h + 1)
            apart(pe)
            for b in range(B):
                p, g = place(b)
                for f in range(2):
                    r = slice(T * f, T * f + T)
                    last = nc.tensor.matmul(ps[T * p:T * (p + 1), f, g * T:(g + 1) * T], qh[r, b * T:(b + 1) * T], kh[r, b * T:(b + 1) * T], start=True, stop=True)
            last.then_inc(l0["s"], 1)

        def l0a_out(pe, h, u):
            pe.wait_ge(l0["olo"], h + 1)
            pe.wait_ge(b_split, h + N1 + 1)
            y_add(lambda t: (ot_hi[:, u, 0, t * P:(t + 1) * P], ot_lo[:, u, 0, t * P:(t + 1) * P]), wb(u, 0, D)).then_inc(b_used, 1)

        def l0a_pe_head(pe, h, u):
            l0a_project(pe, h, u)
            if exists(h, h - 1):
                l0a_turn(pe, h - 1, 1 - u)
            l0a_scores(pe, h, u)
            if exists(h, h - 2):
                l0a_out(pe, h - 2, u)
            if exists(h, h - 1):
                l0a_pv(pe, h - 1, 1 - u)

        def l0a_pe(pe):
            ln_pe(pe, 1)
            pe.wait_ge(x_ready, 1)
            y_start(None)
            pe.wait_ge(consts, CONSTS)
            lam_mm = nc.tensor.matmul(ps[:, 3, 0:H], ones[0:1, :], row[:, R_LAM:R_LAM + H], start=True, stop=True)
            lam_mm.then_inc(l0["lam"], 1)
            pe.wait_ge(l0["lam"], 2)
            pe.wait_ge(ln_lo, 2)
            for u in range(2):
                l0a_pe_head(pe, u, u)
            with pe.Fori(1, H // 2) as i:
                for u in range(2):
                    l0a_pe_head(pe, 2 * i + u, u)
            l0a_turn(pe, H - 1, 1)
            l0a_out(pe, H - 2, 0)
            l0a_pv(pe, H - 1, 1)
            l0a_out(pe, H - 1, 1)
            y_stop()

        def l0a_pool(pool):
            lo_part(pool, "a", 0, L0A[0], L0A)
            ln_pool(pool, 1)
            lo_part(pool, "a", 0, L0A[0] + 1, L0A)
            lo_parts(pool, L0A, L0F, 2)

        def l0a_act(act):
            hi_part(act, "a", 0, L0A[0], L0A)
            ln_act(act, 1)
            act.wait_ge(l0["lam"], 1)
            nc.scalar.activation(lam[:], ps[:, 3, 0:H], ACT.Exp, scale=-1.0).then_inc(l0["lam"], 1)

            def turned(h):
                act.wait_ge(l0["t"], h + 1)
                nc.scalar.activation(flat(ddt[:]), ps[:, 3, 0:2 * P], ACT.Copy).then_inc(l0["te"], 1)

            def after(h, u):
                act.wait_ge(l0["pv"], h + 1)
                if exists(h, h - 2):
                    act.wait_ge(b_used, h + N1 - 1)
                nc.scalar.activation(by_batch(ot_hi[:, u, 0, :]), banks45(), ACT.Copy).then_inc(l0["ohi"], 1)

            def head(i, u):
                h = 2 * i + u
                act.wait_ge(l0["q"], h + 1)
                if exists(h, h - 1):
                    act.wait_ge(l0["s"], h)
                nc.scalar.activation(qh[:], ps[:, 0, :], ACT.Copy).then_inc(l0["qe"], 1)
                act.wait_ge(l0["k"], h + 1)
                nc.scalar.activation(kh[:], ps[:, 1, :], ACT.Copy).then_inc(l0["ke"], 1)
                if exists(h, h - 1):
                    hi_part(act, "b", i, N1 + u - 1, L0A)
                next_part(hi_part, act, i, u, L0A, None)
                if exists(h, h - 1):
                    turned(h - 1)
                act.wait_ge(l0["sh"], h + 1)
                nc.scalar.activation(pr[:, u, :], st, ACT.Exp, scale=T ** -0.5).then_inc(l0["e"], 1)
                if exists(h, h - 1):
                    after(h - 1, 1 - u)

            for u in range(2):
                head(0, u)
            with act.Fori(1, H // 2 - 1) as i:
                for u in range(2):
                    head(i, u)
            for u in range(2):
                head(H // 2 - 1, u)
            if 6 > 1:
                hi_part(act, "a", 0, N1 + H, L0F)
            hi_part(act, "b", 0, N1 + H - 1, L0A)
            turned(H - 1)
            after(H - 1, 1)

        STEPS0 = 5

        def groups(ap, n=8):
            return ap.rearrange("p (g k) -> p g k", g=n)

        def wide(ap, n, k):
            return ap.unsqueeze(2).broadcast_to([P, n, k])

        def l0a_dve(dve):
            ln_dve(dve, 1)
            c = Count(0)
            dve.wait_ge(l0["lam"], 2)
            for k in range(3):
                if k == 0:
                    nc.vector.tensor_scalar(lam[:], lam[:], 1.0, None, ALU.add).then_inc(l0["dve"], 1)
                elif k == 1:
                    nc.vector.reciprocal(lam[:], lam[:]).then_inc(l0["dve"], 1)
                else:
                    nc.vector.tensor_scalar(lam[:], lam[:], -1.0, None, ALU.mult).then_inc(l0["dve"], 1)
                dve.wait_ge(l0["dve"], c.up())

            def after(h, u):
                dve.wait_ge(l0["ohi"], h + 1)
                nc.vector.tensor_tensor(by_batch(ot_lo[:, u, 0, :]), banks45(), by_batch(ot_hi[:, u, 0, :]).bitcast(F32), ALU.subtract).then_inc(l0["olo"], 1)

            def head(h, u):
                c = Count(3 + STEPS0 * h)
                dve.wait_ge(a_used, h + N1 + 1)
                if exists(h, h - 2):
                    dve.wait_ge(l0["pv"], h - 1)
                nc.vector.tensor_copy(vh[:, u, :, :].rearrange("p t d -> p (t d)"), ps[:, 2, :]).then_inc(l0["ve"], 1)
                dve.wait_ge(l0["s"], h + 1)
                nc.vector.tensor_tensor(st.rearrange("p (f g k) -> p f g k", f=2, g=4), ps[:, 0:2, 0:256].rearrange("p f (g k) -> p f g k", g=4),
                                        mask[:].unsqueeze(1).unsqueeze(1).broadcast_to([P, 2, 4, T]), ALU.add).then_inc(l0["se"], 1)
                dve.wait_ge(l0["se"], h + 1)
                nc.vector.tensor_reduce(mx[:], groups(st), AX.X, ALU.max).then_inc(l0["dve"], 1)
                dve.wait_ge(l0["dve"], c.up())
                nc.vector.tensor_tensor(groups(st), groups(st), wide(mx[:], 8, T), ALU.subtract).then_inc(l0["sh"], 1)
                dve.wait_ge(l0["e"], h + 1)
                nc.vector.tensor_reduce(sm[:], groups(pr[:, u, :]), AX.X, ALU.add).then_inc(l0["dve"], 1)
                dve.wait_ge(l0["dve"], c.up())
                nc.vector.reciprocal(rc[:], sm[:]).then_inc(l0["dve"], 1)
                dve.wait_ge(l0["dve"], c.up())
                nc.vector.tensor_scalar(rc[:, 4:8], rc[:, 4:8], lam[:, bass.ds(h, 1)], None, ALU.mult).then_inc(l0["dve"], 1)
                dve.wait_ge(l0["dve"], c.up())
                nc.vector.tensor_tensor(groups(pr[:, u, :]), groups(pr[:, u, :]), wide(rc[:], 8, T), ALU.mult).then_inc(l0["dve"], 1)
                dve.wait_ge(l0["dve"], c.up())
                assert c.n == STEPS0
                nc.vector.tensor_tensor(dd[:, u, :], pr[:, u, 0:256], pr[:, u, 256:512], ALU.add).then_inc(l0["d"], 1)
                if exists(h, h - 1):
                    after(h - 1, 1 - u)

            for u in range(2):
                head(u, u)
            with dve.Fori(1, H // 2) as i:
                for u in range(2):
                    head(2 * i + u, u)
            after(H - 1, 1)
            add_y(dve, 1)

        RSTEPS = 7

        def route_pe(pe, k):
            for t in range(NT):
                for c in range(C2):
                    last = mm3(ps[:, 2, 8 * t:8 * t + 8], xt(c, t * P, P), (gate_hi[:, k, c, :], gate_lo[:, k, c, :]), c == 0, c == 1)
            last.then_inc(ff["lg"], 1)

        def route_act(act, k):
            if k == 0:
                act.wait_ge(consts, CONSTS)
                nc.scalar.activation(gate_hi[:].rearrange("p a b e -> p (a b e)"), gate[:].rearrange("p a b e -> p (a b e)"), ACT.Copy).then_inc(ff["ghi"], 1)
            act.wait_ge(ff["shift"], k + 1)
            nc.scalar.activation(sh[:], sh[:], ACT.Exp).then_inc(ff["e"], 1)

        def route_dve(dve, k):
            c = Count(RSTEPS * k)
            step = ff["dve"]
            dve.wait_ge(ff["lg"], k + 1)
            nc.vector.memset(lg[:, :, 8:16], SENT)
            nc.vector.tensor_copy(lg[:, :, 0:8], ps[:, 2, 0:8 * NT].rearrange("p (t e) -> p t e", t=NT)).then_inc(step, 1)
            dve.wait_ge(step, c.up())
            for t in range(NT):
                last = nc.vector.max(top8[:, t, :], lg[:, t, :])
            last.then_inc(step, 1)
            dve.wait_ge(step, c.up())
            nc.vector.tensor_tensor(sh[:], lg[:, :, 0:8], top8[:, :, 0:1].broadcast_to([P, NT, 8]), ALU.subtract).then_inc(ff["shift"], 1)
            nc.vector.memset(top8[:, :, 2:8], SENT).then_inc(step, 1)
            dve.wait_ge(step, c.up())
            for t in range(NT):
                last = nc.vector.match_replace(rep[:, t, :], top8[:, t, :], lg[:, t, :], -SENT)
            last.then_inc(step, 1)
            dve.wait_ge(step, c.up())
            nc.vector.tensor_tensor(sel[:], rep[:, :, 0:8], lg[:, :, 0:8], ALU.not_equal).then_inc(step, 1)
            dve.wait_ge(step, c.up())
            dve.wait_ge(ff["e"], k + 1)
            nc.vector.tensor_tensor(sel[:], sel[:], sh[:], ALU.mult).then_inc(step, 1)
            dve.wait_ge(step, c.up())
            nc.vector.tensor_reduce(ssum[:], sel[:], AX.X, ALU.add).then_inc(step, 1)
            dve.wait_ge(step, c.up())
            assert c.n == RSTEPS
            nc.vector.reciprocal(ssum[:], ssum[:]).then_inc(ff["comb"], 1)
            dve.wait_ge(ff["comb"], 2 * k + 1)
            nc.vector.tensor_tensor(comb[:, 0:8, :].rearrange("p e t -> p t e"), sel[:], wide(ssum[:], NT, 8), ALU.mult).then_inc(ff["comb"], 1)

        def ffn_up(pe, n, m, u):
            pe.wait_ge(a_split, n + 1)
            if exists(m, m - 2):
                pe.wait_ge(ff["h"], m - 1)
            for k in range(2):
                for c in range(C2):
                    last = mm3(ps[:, 2 * u + k, :], wa(u, 2 * P * k + c * P, P), (xt_hi[:, c, :], xt_lo[:, c, :]), c == 0, c == 1)
                last.then_inc(ff["g"] if k == 0 else a_used, 1)

        def ffn_down(m, u, bank, r0, r1, first, final):
            for t in range(NT):
                o = (h_hi[r0:r1, u, t * P:(t + 1) * P], h_lo[r0:r1, u, t * P:(t + 1) * P])
                last = mm3(ps[:, bank + t // 2, (t % 2) * D:(t % 2 + 1) * D], o, wb(u, 0, D, r0, r1),
                           first and t % 2 == 0, final and t % 2 == 1, skip_group_check=True)
            return last

        def ffn_act(act, m, u):
            act.wait_ge(ff["g"], m + 1)
            if exists(m, m - 2):
                act.wait_ge(ff["h"], m - 1)
            nc.scalar.activation(sg[:, u, :], ps[:, 2 * u, :], ACT.Silu).then_inc(ff["sg"], 1)

        def ffn_act_hi(act, m, u, nb_used):
            act.wait_ge(ff["h"], m + 1)
            if nb_used is not None:
                act.wait_ge(b_used, nb_used)
            nc.scalar.activation(h_hi[:, u, :], hh[:, u, :], ACT.Copy).then_inc(ff["hhi"], 1)

        def ffn_dve(dve, n, m, u, old):
            dve.wait_ge(ff["sg"], m + 1)
            dve.wait_ge(a_used, n + 1)
            if exists(m, m - 2):
                dve.wait_ge(ff["hlo"], m - 1)
            nc.vector.tensor_tensor(hh[:, u, :], sg[:, u, :], ps[:, 2 * u + 1, :], ALU.mult).then_inc(ff["h"], 1)
            dve.wait_ge(ff["hhi"], m + 1)
            nc.vector.tensor_tensor(h_lo[:, u, :], hh[:, u, :], h_hi[:, u, :].bitcast(F32), ALU.subtract).then_inc(ff["hlo"], 1)

        def ffn_add(dve, bank, expert, used, xstep):
            dve.wait_ge(b_used, used)
            for t in range(NT):
                last = nc.vector.scalar_tensor_tensor(x[:, t, :], ps[:, bank + t // 2, (t % 2) * D:(t % 2 + 1) * D],
                                                      comb[:, bass.ds(expert, 1), t], x[:, t, :], ALU.mult, ALU.add)
            last.then_inc(ff["ev"], 1)
            dve.wait_ge(ff["ev"], xstep)

        N2 = L0F[0]

        def l0f_pe(pe):
            ln_pe(pe, 2)
            pe.wait_ge(ff["glo"], 1)
            pe.wait_ge(ln_lo, 3)
            route_pe(pe, 0)
            pe.wait_ge(ff["comb"], 1)

            def down(m, u):
                pe.wait_ge(ff["hlo"], m + 1)
                pe.wait_ge(b_split, m + N2 + 1)
                if exists(m, m - 2):
                    pe.wait_ge(ff["ev"], m - 1)
                ffn_down(m, u, 4 + 2 * u, 0, P, True, True).then_inc(b_used, 1)

            def chunk(m, u):
                ffn_up(pe, m + N2, m, u)
                if exists(m, m - 1):
                    down(m - 1, 1 - u)

            for u in range(2):
                chunk(u, u)
            with pe.Fori(1, CH0 // 2) as i:
                for u in range(2):
                    chunk(2 * i + u, u)
            down(CH0 - 1, 1)

        def l0f_pool(pool):
            ln_pool(pool, 2)
            lo_part(pool, "a", 0, N2 + 1, L0F)
            lo_parts(pool, L0F, L1P, 2)

        def l0f_act(act):
            hi_part(act, "a", 0, N2 + 1, L0F)
            ln_act(act, 2)
            route_act(act, 0)

            def chunk(i, u):
                m = 2 * i + u
                ffn_act(act, m, u)
                hi_part(act, "b", i, N2 + u, L0F)
                next_part(hi_part, act, i, u, L0F, L1P, 2)
                ffn_act_hi(act, m, u, m + N2 - 1 if exists(m, m - 2) else None)

            peeled(act, CH0, chunk)

        def l0f_dve(dve):
            ln_dve_stats(dve, 2)
            dve.wait_ge(ff["ghi"], 1)
            nc.vector.tensor_tensor(gate_lo[:].rearrange("p a b e -> p (a b e)"), gate[:].rearrange("p a b e -> p (a b e)"),
                                    gate_hi[:].rearrange("p a b e -> p (a b e)").bitcast(F32), ALU.subtract).then_inc(ff["glo"], 1)
            ln_dve_split(dve, 2)
            nc.vector.memset(comb[:, 8:12, :], 1.0)
            route_dve(dve, 0)
            dve.wait_ge(ff["comb"], 2)

            def chunk(m, u):
                ffn_dve(dve, m + N2, m, u, None)
                if exists(m, m - 1):
                    ffn_add(dve, 4 + 2 * (1 - u), m - 1, m + N2, m)

            for u in range(2):
                chunk(u, u)
            with dve.Fori(1, CH0 // 2) as i:
                for u in range(2):
                    chunk(2 * i + u, u)
            ffn_add(dve, 6, CH0 - 1, CH0 + N2, CH0)

        NP, NX = L1P[0], L1X[0]

        def proj_pe(pe, m, u):
            n = m + NP
            pe.wait_ge(a_split, n + 1)
            if exists(m, m - 2):
                pe.wait_ge(l1["qst"], m - 1)
            for c in range(C2):
                last = mm3(ps[:, 4 + u, :], wa(u, c * P, P), (xt_hi[:, c, :], xt_lo[:, c, :]), c == 0, c == 1)
            last.then_inc(a_used, 1)
            pe.wait_ge(b_split, n + 1)
            if exists(m, m - 2):
                pe.wait_ge(l1["kst"], m - 1)
            for j in range(2):
                for c in range(C2):
                    last = mm3(ps[:, 2 * u + j, :], wb(u, c * P, P), (ct_hi[:, c, j * 512:(j + 1) * 512], ct_lo[:, c, j * 512:(j + 1) * 512]), c == 0, c == 1)
            last.then_inc(b_used, 1)

        def proj_act(act, i, u):
            m = 2 * i + u
            for part in "ab":
                hi_part(act, part, i, NP + u + 1, L1P)
            act.wait_ge(a_used, m + NP + 1)
            if exists(m, m - 1):
                act.wait_ge(l1["acck"], m)
                act.wait_ge(l1["accq"], m)
            nc.scalar.activation(sq[:, 1024:1536], ps[:, 4 + u, :], ACT.Square, bias=vec[:, bass.ds(m + QB, 1)]).then_inc(l1["sqq"], 1)
            act.wait_ge(l1["kst"], m + 1)
            nc.scalar.activation(sq[:, 0:1024], kst[:, bass.ds(m, 1), :].rearrange("p a n -> p (a n)"), ACT.Square).then_inc(l1["sqk"], 1)

        def proj_dve(dve, m, u):
            dve.wait_ge(b_used, m + NP + 1)
            nc.vector.tensor_scalar(kst[:, bass.ds(m, 1), :].rearrange("p a n -> p (a n)"), flat(ps[:, 2 * u:2 * u + 2, :]), vec[:, bass.ds(m + KB, 1)], None, ALU.add).then_inc(l1["kst"], 1)
            dve.wait_ge(l1["sqq"], m + 1)
            nc.vector.tensor_scalar(qst[:, bass.ds(m, 1), :].rearrange("p a n -> p (a n)"), ps[:, 4 + u, :], vec[:, bass.ds(m + QB, 1)], nqk[:, bass.ds(m, 1)],
                                    ALU.add, ALU.mult).then_inc(l1["qst"], 1)
            dve.wait_ge(l1["sqk"], m + 1)
            nc.vector.tensor_tensor(acc[:, 0:1024], acc[:, 0:1024], sq[:, 0:1024], ALU.add).then_inc(l1["acck"], 1)
            dve.wait_ge(l1["acck"], m + 1)

        def key_scores(pe, m, u):
            pe.wait_ge(l1["qn"], m + 1)
            pe.wait_ge(l1["kn"], m + 1)
            if exists(m, m - 2):
                pe.wait_ge(l1["se"], m - 1)
            apart(pe)
            for b in range(B):
                p, g = place(b)
                last = nc.tensor.matmul(ps[T * p:T * (p + 1), u, g * S:(g + 1) * S], qn[:, u, b * T:(b + 1) * T], kn[:, u, b * S:(b + 1) * S], start=True, stop=True)
            last.then_inc(l1["s"], 1)

        def turn_x(pe, h, u):
            pe.wait_ge(l1["p"], h + 1)
            if exists(h, h - 1):
                pe.wait_ge(l1["te"], h)
            for g in range(4):
                last = nc.tensor.transpose(ps[:, 2, g * P:(g + 1) * P], pr[:, u, g * P:(g + 1) * P], ident[:])
            last.then_inc(l1["t"], 1)

        def mix_ctx(pe, h):
            pe.wait_ge(l1["te"], h + 1)
            if exists(h, h - 1):
                pe.wait_ge(l1["ulo"], h)
            apart(pe)
            for c in range(C2):
                for b in range(B):
                    p, g = place(b)
                    last = nc.tensor.matmul(ps[:, 3 + c, b * T:(b + 1) * T], ctx[:, b, c * P:(c + 1) * P], ptx[:, g, T * p:T * (p + 1)], start=True, stop=True)
            last.then_inc(l1["u"], 1)

        def values_x(pe, h, u):
            pe.wait_ge(l1["ulo"], h + 1)
            pe.wait_ge(a_split, h + NX + 1)
            if exists(h, h - 1):
                pe.wait_ge(l1["olo"], h)
            for c in range(C2):
                last = mm3(ps[:, 5, :], wa(u, c * P, P), (u_hi[:, c, :], u_lo[:, c, :]), c == 0, c == 1)
            last.then_inc(a_used, 1)

        def out_x(pe, h, u):
            pe.wait_ge(l1["olo"], h + 1)
            pe.wait_ge(b_split, h + NX + 1)
            y_add(lambda t: (ot_hi[:, u, 0, t * P:(t + 1) * P], ot_lo[:, u, 0, t * P:(t + 1) * P]), wb(u, 0, D)).then_inc(b_used, 1)

        def within(m):
            return not isinstance(m, int) or 0 <= m < H

        def l1x_pe(pe):
            ln_pe(pe, 3)
            pe.wait_ge(ln_lo, 4)
            for u in range(2):
                proj_pe(pe, u, u)
            with pe.Fori(1, H // 2) as i:
                for u in range(2):
                    proj_pe(pe, 2 * i + u, u)
            pe.wait_ge(l1["acck"], H)
            pe.wait_ge(l1["accq"], H)
            for k in range(3):
                last = nc.tensor.matmul(ps[:, k, :], ones[:, :], acc[:, k * 512:(k + 1) * 512], start=True, stop=True)
            last.then_inc(l1["ms"], 1)
            y_start(R_OB)
            pe.wait_ge(l1["sqrt"], 1)

            def turn(m, u):
                if within(m - 2):
                    turn_x(pe, m - 2, u)
                if within(m):
                    key_scores(pe, m, u)
                if within(m - 2):
                    mix_ctx(pe, m - 2)
                if within(m - 3):
                    out_x(pe, m - 3, 1 - u)
                if within(m - 2):
                    values_x(pe, m - 2, u)

            for m in range(4):
                turn(m, m % 2)
            with pe.Fori(2, H // 2) as i:
                for u in range(2):
                    turn(2 * i + u, u)
            for m in range(H, H + 3):
                turn(m, m % 2)
            y_stop()

        def l1x_pool(pool):
            ln_pool(pool, 3)
            lo_part(pool, "b", 0, NP, L1P)
            nc.gpsimd.memset(acc[:], 0.0).then_inc(l1["acc0"], 1)
            nc.gpsimd.memset(epsc[:], 1e-6).then_inc(l1["acc0"], 1)
            nc.gpsimd.tensor_tensor(nqk[:], vec[:, NQ:NQ + H], vec[:, NK:NK + H], ALU.mult).then_inc(l1["nqk"], 1)

            def proj(i, u):
                m = 2 * i + u
                for part in "ab":
                    lo_part(pool, part, i, NP + u + 1, L1P)
                pool.wait_ge(l1["sqq"], m + 1)
                nc.gpsimd.tensor_tensor(acc[:, 1024:1536], acc[:, 1024:1536], sq[:, 1024:1536], ALU.add).then_inc(l1["accq"], 1)
                pool.wait_ge(l1["accq"], m + 1)

            pool.wait_ge(l1["acc0"], 2)
            for u in range(2):
                proj(0, u)
            with pool.Fori(1, H // 2) as i:
                for u in range(2):
                    proj(i, u)
            pool.wait_ge(l1["rk"], 1)

            def head(m, u):
                if exists(m, m - 2):
                    pool.wait_ge(l1["s"], m - 1)
                nc.gpsimd.tensor_tensor(qn[:, u, :], qst[:, bass.ds(m, 1), :].rearrange("p a n -> p (a n)"), rq, ALU.mult).then_inc(l1["qn"], 1)

            def turn(i, u):
                head(2 * i + u, u)
                for part in "ab":
                    lo_part(pool, part, i, NX + u - 1, L1X)

            for m in range(2):
                head(m, m)
            for u in range(2):
                turn(1, u)
            with pool.Fori(2, H // 2) as i:
                for u in range(2):
                    turn(i, u)
            for part in "ab":
                lo_part(pool, part, 0, NX + H - 1, L1X)
            if 6 > 4:
                lo_part(pool, "a", 0, NX + H, L1A)

        def l1x_act(act):
            ln_act(act, 3)
            hi_part(act, "b", 0, NP, L1P)
            for u in range(2):
                proj_act(act, 0, u)
            with act.Fori(1, H // 2) as i:
                for u in range(2):
                    proj_act(act, i, u)
            act.wait_ge(l1["ms"], 1)
            nc.scalar.activation(sq, ps[:, 0:3, :].rearrange("p a b -> p (a b)"), ACT.Sqrt, scale=1.0 / (H * HD), bias=epsc[:]).then_inc(l1["sqrt"], 1)

            def exps(m, u):
                act.wait_ge(l1["sh"], m + 1)
                if exists(m, m - 2):
                    act.wait_ge(l1["t"], m - 1)
                nc.scalar.activation(pr[:, u, :], st, ACT.Exp, scale=HD ** -0.5).then_inc(l1["e"], 1)

            def turned(h):
                act.wait_ge(l1["t"], h + 1)
                nc.scalar.activation(flat(ptx[:]), ps[:, 2, :], ACT.Copy).then_inc(l1["te"], 1)

            def mixed(h):
                act.wait_ge(l1["u"], h + 1)
                if exists(h, h - 1):
                    act.wait_ge(a_used, h + NX)
                nc.scalar.activation(flat(u_hi[:]), flat(ps[:, 3:5, :]), ACT.Copy).then_inc(l1["uhi"], 1)

            def outs(h, u):
                act.wait_ge(a_used, h + NX + 1)
                if exists(h, h - 2):
                    act.wait_ge(b_used, h + NX - 1)
                nc.scalar.activation(ot_hi[:, u, 0, :], ps[:, 5, :], ACT.Identity, bias=vec[:, bass.ds(h + VB, 1)]).then_inc(l1["ohi"], 1)

            def keys(m, u):
                if exists(m, m - 2):
                    act.wait_ge(l1["s"], m - 1)
                nc.scalar.activation(kn[:, u, :], kst[:, bass.ds(m, 1), :].rearrange("p a n -> p (a n)"), ACT.Copy).then_inc(l1["kn"], 1)

            def turn(i, u):
                m = 2 * i + u
                if exists(m, m - 2):
                    turned(m - 2)
                if within(m + 1):
                    keys(m + 1, 1 - u)
                if exists(m, m - 2):
                    if m is not H + 1:
                        hi_part(act, "a", i, NX + u - 1, L1X)
                    elif 6 > 4:
                        hi_part(act, "a", i, NX + u - 1, L1A)
                    mixed(m - 2)
                if within(m):
                    exps(m, u)
                if exists(m, m - 2):
                    if m is not H + 1:
                        hi_part(act, "b", i, NX + u - 1, L1X)
                    outs(m - 2, u)

            keys(0, 0)
            for i in range(2):
                for u in range(2):
                    turn(i, u)
            with act.Fori(2, H // 2 - 1) as i:
                for u in range(2):
                    turn(i, u)
            for i in (H // 2 - 1, H // 2):
                for u in range(2):
                    turn(i, u)

        STEPS1 = 3

        def l1x_dve(dve):
            ln_dve(dve, 3)
            dve.wait_ge(l1["acc0"], 2)
            dve.wait_ge(l1["nqk"], 1)
            for u in range(2):
                proj_dve(dve, u, u)
            with dve.Fori(1, H // 2) as i:
                for u in range(2):
                    proj_dve(dve, 2 * i + u, u)
            dve.wait_ge(l1["sqrt"], 1)
            dve.wait_ge(ln_t, 4)
            nc.vector.reciprocal(rq, sq[:, 1024:1536])
            for p in range(2):
                r = slice(T * p, T * (p + 1))
                last = nc.vector.reciprocal(rk[r].rearrange("p (G e) k -> p G e k", e=2), sq[r, 0:1024].rearrange("p (G q e k) -> p q G e k", G=2, q=2, e=2)[:, p])
            last.then_inc(l1["rk"], 1)
            dve.wait_ge(l1["rk"], 1)

            def scores(m, u):
                c = Count(STEPS1 * m)
                dve.wait_ge(l1["s"], m + 1)
                nc.vector.tensor_tensor(st, ps[:, u, :], rk.rearrange("p g k -> p (g k)"), ALU.mult).then_inc(l1["se"], 1)
                dve.wait_ge(l1["se"], m + 1)
                nc.vector.tensor_reduce(mx[:, 0:4], groups(st, 4), AX.X, ALU.max).then_inc(l1["dve"], 1)
                dve.wait_ge(l1["dve"], c.up())
                nc.vector.tensor_tensor(groups(st, 4), groups(st, 4), wide(mx[:, 0:4], 4, S), ALU.subtract).then_inc(l1["sh"], 1)

            def weights(m, u):
                c = Count(STEPS1 * m + 1)
                dve.wait_ge(l1["e"], m + 1)
                nc.vector.tensor_reduce(sm[:, 0:4], groups(pr[:, u, :], 4), AX.X, ALU.add).then_inc(l1["dve"], 1)
                dve.wait_ge(l1["dve"], c.up())
                nc.vector.reciprocal(rc[:, 0:4], sm[:, 0:4]).then_inc(l1["dve"], 1)
                dve.wait_ge(l1["dve"], c.up())
                nc.vector.tensor_tensor(groups(pr[:, u, :], 4), groups(pr[:, u, :], 4), wide(rc[:, 0:4], 4, S), ALU.mult).then_inc(l1["p"], 1)

            def mixed(h):
                dve.wait_ge(l1["uhi"], h + 1)
                nc.vector.tensor_tensor(flat(u_lo[:]), flat(ps[:, 3:5, :]), flat(u_hi[:]).bitcast(F32), ALU.subtract).then_inc(l1["ulo"], 1)

            def outs(h, u):
                dve.wait_ge(l1["ohi"], h + 1)
                nc.vector.scalar_tensor_tensor(ot_lo[:, u, 0, :], ps[:, 5, :], vec[:, bass.ds(h + VB, 1)], ot_hi[:, u, 0, :].bitcast(F32), ALU.add, ALU.subtract).then_inc(l1["olo"], 1)

            def turn(m, u):
                if within(m):
                    scores(m, u)
                if within(m - 2):
                    mixed(m - 2)
                if within(m):
                    weights(m, u)
                if within(m - 2):
                    outs(m - 2, u)

            for m in range(4):
                turn(m, m % 2)
            with dve.Fori(2, H // 2) as i:
                for u in range(2):
                    turn(2 * i + u, u)
            for m in range(H, H + 2):
                turn(m, m % 2)
            add_y(dve, 2)

        NA = L1A[0]

        def l1a_project(pe, j, u):
            pe.wait_ge(a_split, j + NA + 1)
            for a in range(2):
                if exists(j, j - 1):
                    pe.wait_ge(la["qe"], j)
                for c in range(C2):
                    last = mm3(ps[:, a, :], wa(u, 2 * P * a + c * P, P), (xt_hi[:, c, :], xt_lo[:, c, :]), c == 0, c == 1)
                last.then_inc(la["q"] if a == 0 else a_used, 1)

        def l1a_scores(pe, j):
            pe.wait_ge(la["qe"], j + 1)
            if exists(j, j - 1):
                pe.wait_ge(la["se"], j)
            apart(pe)
            for b in range(B):
                p, g = place(b)
                cols = slice(b * T, (b + 1) * T)
                for a in range(2):
                    o = ps[T * p:T * (p + 1), 3, (4 * a + g) * T:(4 * a + g + 1) * T]
                    nc.tensor.matmul(o, qc[:, a, cols], krot[:, 0, cols], start=True, stop=False)
                    last = nc.tensor.matmul(o, qsn[:, a, cols], krot[:, 1, cols], start=False, stop=True)
            last.then_inc(la["s"], 1)

        def l1a_turn(pe, j, u):
            pe.wait_ge(la["p"], j + 1)
            if exists(j, j - 1):
                pe.wait_ge(la["te"], j)
            for k in range(4):
                last = nc.tensor.transpose(ps[:, 2, k * P:(k + 1) * P], pr[:, u, k * P:(k + 1) * P], ident[:])
            last.then_inc(la["t"], 1)

        def l1a_pv(pe, j, u):
            pe.wait_ge(la["te"], j + 1)
            if exists(j, j - 1):
                pe.wait_ge(la["olo"], j)
            apart(pe)
            for b in range(B):
                p, g = place(b)
                k0 = T * (b % 2)
                for a in range(2):
                    c0 = D * a + (b // 2) * T
                    last = nc.tensor.matmul(ps[:, 4 + b % 2, c0:c0 + T], lat[k0:k0 + T, b // 2, :], dtl[k0:k0 + T, a, g // 2, T * p:T * (p + 1)], start=True, stop=True)
            last.then_inc(la["pv"], 1)

        def l1a_out(pe, j, u, a):
            if a == 0:
                pe.wait_ge(la["olo"], j + 1)
                pe.wait_ge(b_split, j + NA + 1)
            last = y_add(lambda t: (ot_hi[:, u, a, t * P:(t + 1) * P], ot_lo[:, u, a, t * P:(t + 1) * P]), wb(u, a * D, D))
            if a == 1:
                last.then_inc(b_used, 1)

        def l1a_step(pe, j, u):
            l1a_project(pe, j, u)
            if exists(j, j - 2):
                l1a_out(pe, j - 2, u, 0)
            if exists(j, j - 1):
                l1a_turn(pe, j - 1, 1 - u)
            if exists(j, j - 2):
                l1a_out(pe, j - 2, u, 1)
            if exists(j, j - 1):
                l1a_pv(pe, j - 1, 1 - u)
            l1a_scores(pe, j)

        def l1a_pe(pe):
            ln_pe(pe, 4)
            y_start(R_PB)
            pe.wait_ge(ln_lo, 5)
            pe.wait_ge(la["wlo"], 1)
            for c in range(C2):
                last = mm3(ps[:, 0, :], (wl_hi[:, c, :], wl_lo[:, c, :]), (xt_hi[:, c, :], xt_lo[:, c, :]), c == 0, c == 1)
            last.then_inc(la["lt"], 1)
            nc.tensor.matmul(ps[:, 1, :], ones[0:1, :], row[:, R_LB:R_LB + HD].unsqueeze(1).broadcast_to([1, NT, HD]), start=True, stop=False, skip_group_check=True)
            for t in range(NT):
                for c in range(C2):
                    last = mm3(ps[:, 1, t * HD:(t + 1) * HD], xt(c, t * P, P), (wl_hi[:, c, :], wl_lo[:, c, :]), False, t == NT - 1 and c == 1, skip_group_check=True)
            last.then_inc(la["lt"], 1)
            pe.wait_ge(la["lte"], 1)
            nc.tensor.matmul(ps[:, 2, :], rotm[:], lt[:], start=True, stop=True).then_inc(la["rot"], 1)
            pe.wait_ge(la["kr"], 1)
            nc.tensor.matmul(ps[:, 2, :], rotm[:], krot[:, 0, :], start=True, stop=True).then_inc(la["rot"], 1)
            pe.wait_ge(la["late"], 1)
            pe.wait_ge(la["krot"], 1)
            for u in range(2):
                l1a_step(pe, u, u)
            with pe.Fori(1, H // 4) as i:
                for u in range(2):
                    l1a_step(pe, 2 * i + u, u)
            l1a_out(pe, H // 2 - 2, 0, 0)
            l1a_turn(pe, H // 2 - 1, 1)
            l1a_out(pe, H // 2 - 2, 0, 1)
            l1a_pv(pe, H // 2 - 1, 1)
            for a in range(2):
                l1a_out(pe, H // 2 - 1, 1, a)
            y_stop()

        def l1a_pool(pool):
            ln_pool(pool, 4)
            lo_part(pool, "a", 0, NA + 1, L1A)
            lo_parts(pool, L1A, None, 2)

        def banks45f():
            return ps[:, 4:6, :].rearrange("p e (a n) -> p e a n", a=2)

        def l1a_act(act):
            ln_act(act, 4)
            nc.scalar.activation(flat(wl_hi[:]), flat(wl[:]), ACT.Copy).then_inc(la["whi"], 1)
            act.wait_ge(la["lt"], 1)
            nc.scalar.activation(lt[:], ps[:, 0, :], ACT.Identity, bias=vec[:, LB:LB + 1]).then_inc(la["lte"], 1)
            act.wait_ge(la["lt"], 2)
            nc.scalar.activation(lat[:].rearrange("p t d -> p (t d)"), ps[:, 1, :], ACT.Copy).then_inc(la["late"], 1)

            def after(j, u):
                act.wait_ge(la["t"], j + 1)
                nc.scalar.activation(dtl[:].rearrange("p a g n -> p (a g n)"), ps[:, 2, :], ACT.Copy).then_inc(la["te"], 1)
                act.wait_ge(la["pv"], j + 1)
                if exists(j, j - 2):
                    act.wait_ge(b_used, j + NA - 1)
                for a in range(2):
                    last = nc.scalar.activation(by_batch(ot_hi[:, u, a, :]), banks45f()[:, :, a, :].rearrange("p e (b k) -> p e b k", k=T), ACT.Copy)
                last.then_inc(la["ohi"], 1)

            def step(i, u):
                j = 2 * i + u
                if exists(j, j - 1):
                    hi_part(act, "b", i, NA + u - 1, L1A)
                next_part(hi_part, act, i, u, L1A, None)
                if exists(j, j - 1):
                    after(j - 1, 1 - u)
                act.wait_ge(la["sh"], j + 1)
                nc.scalar.activation(pr[:, u, :], st, ACT.Exp, scale=HD ** -0.5).then_inc(la["e"], 1)

            peeled(act, H // 2, step)
            hi_part(act, "b", 0, NA + H // 2 - 1, L1A)
            after(H // 2 - 1, 1)

        STEPSA = 3

        def l1a_dve(dve):
            ln_dve(dve, 4)
            dve.wait_ge(la["whi"], 1)
            nc.vector.tensor_tensor(flat(wl_lo[:]), flat(wl[:]), flat(wl_hi[:]).bitcast(F32), ALU.subtract).then_inc(la["wlo"], 1)
            rc_, rs_ = (rope[:, k, :].unsqueeze(1).broadcast_to([P, B, T]) for k in range(2))

            def by(ap):
                return ap.rearrange("p (b k) -> p b k", k=T)

            dve.wait_ge(la["lte"], 1)
            nc.vector.tensor_tensor(by(lcos[:]), by(lt[:]), rc_, ALU.mult).then_inc(la["dve"], 1)
            dve.wait_ge(la["rot"], 1)
            nc.vector.tensor_tensor(by(lsin[:]), by(ps[:, 2, :]), rs_, ALU.mult).then_inc(la["dve"], 1)
            dve.wait_ge(la["dve"], 2)
            nc.vector.tensor_tensor(krot[:, 0, :], lcos[:], lsin[:], ALU.subtract).then_inc(la["kr"], 1)
            dve.wait_ge(la["rot"], 2)
            nc.vector.tensor_copy(krot[:, 1, :], ps[:, 2, :]).then_inc(la["krot"], 1)

            def queries(j):
                if exists(j, j - 1):
                    dve.wait_ge(la["s"], j)
                for a in range(2):
                    dve.wait_ge(la["q"] if a == 0 else a_used, j + 1 if a == 0 else j + NA + 1)
                    bias = vec[:, bass.ds(2 * j + (DB + a), 1)]
                    nc.vector.scalar_tensor_tensor(by(qc[:, a, :]), by(ps[:, a, :]), bias, rc_, ALU.add, ALU.mult)
                    last = nc.vector.scalar_tensor_tensor(by(qsn[:, a, :]), by(ps[:, a, :]), bias, rs_, ALU.add, ALU.mult)
                last.then_inc(la["qe"], 1)

            def after(j, u):
                dve.wait_ge(la["ohi"], j + 1)
                for a in range(2):
                    last = nc.vector.tensor_tensor(by_batch(ot_lo[:, u, a, :]), banks45f()[:, :, a, :].rearrange("p e (b k) -> p e b k", k=T),
                                                   by_batch(ot_hi[:, u, a, :]).bitcast(F32), ALU.subtract)
                last.then_inc(la["olo"], 1)

            def step(j, u):
                c = Count(2 + STEPSA * j)
                queries(j)
                if exists(j, j - 1):
                    after(j - 1, 1 - u)
                dve.wait_ge(la["s"], j + 1)
                nc.vector.tensor_tensor(groups(st), groups(ps[:, 3, :]), mask[:].unsqueeze(1).broadcast_to([P, 8, T]), ALU.add).then_inc(la["se"], 1)
                dve.wait_ge(la["se"], j + 1)
                nc.vector.tensor_reduce(mx[:], groups(st), AX.X, ALU.max).then_inc(la["dve"], 1)
                dve.wait_ge(la["dve"], c.up())
                nc.vector.tensor_tensor(groups(st), groups(st), wide(mx[:], 8, T), ALU.subtract).then_inc(la["sh"], 1)
                dve.wait_ge(la["e"], j + 1)
                nc.vector.tensor_reduce(sm[:], groups(pr[:, u, :]), AX.X, ALU.add).then_inc(la["dve"], 1)
                dve.wait_ge(la["dve"], c.up())
                nc.vector.reciprocal(rc[:], sm[:]).then_inc(la["dve"], 1)
                dve.wait_ge(la["dve"], c.up())
                assert c.n == STEPSA
                nc.vector.tensor_tensor(groups(pr[:, u, :]), groups(pr[:, u, :]), wide(rc[:], 8, T), ALU.mult).then_inc(la["p"], 1)

            for u in range(2):
                step(u, u)
            with dve.Fori(1, H // 4) as i:
                for u in range(2):
                    step(2 * i + u, u)
            after(H // 2 - 1, 1)
            add_y(dve, 3)

        NF = L1F[0]
        HALF = 64

        def experts_of(m):
            mid = CH1 // 2
            if m == mid:
                return [(0, 0, HALF, False, True), (1, HALF, P, True, False)]
            return [(0, 0, P, m == 0, False)] if m < mid else [(1, 0, P, False, m == CH1 - 1)]

        def l1f_pe(pe):
            ln_pe(pe, 5)
            pe.wait_ge(ln_lo, 6)
            route_pe(pe, 1)
            pe.wait_ge(ff["comb"], 3)

            def down(i, k):
                m, u, pair = 2 * CH1 * i + CH0 + k, k % 2, k // CH1
                pe.wait_ge(ff["hlo"], m + 1)
                pe.wait_ge(b_split, m + (NF - CH0) + 1)
                for e, r0, r1, first, final in experts_of(k % CH1):
                    if first:
                        pe.wait_ge(ff["ev"], 4 * i + 2 * pair + e + (CH0 - 1))
                    last = ffn_down(m, u, 4 + 2 * e, r0, r1, first, final)
                last.then_inc(b_used, 1)

            with pe.Fori(0, 2) as i:
                for k in range(2 * CH1):
                    m = 2 * CH1 * i + CH0 + k
                    ffn_up(pe, m + (NF - CH0), m, k % 2)
                    if k:
                        down(i, k - 1)
                down(i, 2 * CH1 - 1)

        def l1f_pool(pool):
            ln_pool(pool, 5)
            with pool.Fori(0, 2) as i:
                for k in range(2):
                    lo_part(pool, "a", i, NF + k, L1F, 2 * CH1)
                for k in range(2 * CH1):
                    lo_part(pool, "b", i, NF + k, L1F, 2 * CH1)
                    if k < 2 * CH1 - 2:
                        lo_part(pool, "a", i, NF + k + 2, L1F, 2 * CH1)

        def l1f_act(act):
            ln_act(act, 5)
            route_act(act, 1)
            with act.Fori(0, 2) as i:
                for k in range(2):
                    hi_part(act, "a", i, NF + k, L1F, 2 * CH1)
                for k in range(2 * CH1):
                    m = 2 * CH1 * i + CH0 + k
                    ffn_act(act, m, k % 2)
                    hi_part(act, "b", i, NF + k, L1F, 2 * CH1)
                    if k < 2 * CH1 - 2:
                        hi_part(act, "a", i, NF + k + 2, L1F, 2 * CH1)
                    ffn_act_hi(act, m, k % 2, m + (NF - CH0) - 1)

        def l1f_dve(dve):
            ln_dve(dve, 5)
            route_dve(dve, 1)
            dve.wait_ge(ff["comb"], 4)
            with dve.Fori(0, 2) as i:
                for k in range(2 * CH1):
                    m = 2 * CH1 * i + CH0 + k
                    ffn_dve(dve, m + (NF - CH0), m, k % 2, None)
                    if (k - 1) % CH1 == CH1 // 2 or (k and k % CH1 == 0):
                        e = 2 * (k // CH1) if k % CH1 else 2 * (k // CH1) - 1
                        ffn_add(dve, 4 + 2 * (e % 2), 4 * i + e, m + (NF - CH0), 4 * i + e + (CH0 + 1))
                ffn_add(dve, 6, 4 * i + 3, 2 * CH1 * i + 2 * CH1 + NF, 4 * i + 3 + (CH0 + 1))

        block = top.enter_context(nc.Block())

        @block.sync
        def _(sp):
            setup_sync(sp)
            for src, stage in zip((w_l0a, w_l0f, w_l1p, w_l1x, w_l1a, w_l1f)[:6], (L0A, L0F, L1P, L1X, L1A, L1F)):
                load_stage(sp, src, stage)
            sp.wait_ge(ff["ev"], CH0 + E1)
            sp.dma_start(out, x[:]).then_inc(stored, 16)
            sp.wait_ge(stored, 16)

        @block.gpsimd
        def _(pool):
            setup_pool(pool)
            ln_pool(pool, 0)
            l0x_pool(pool)
            l0a_pool(pool)
            l0f_pool(pool)
            l1x_pool(pool)
            l1a_pool(pool)
            l1f_pool(pool)

        @block.scalar
        def _(act):
            l0x_act(act)
            l0a_act(act)
            l0f_act(act)
            l1x_act(act)
            l1a_act(act)
            l1f_act(act)

        @block.vector
        def _(dve):
            l0x_dve(dve)
            l0a_dve(dve)
            l0f_dve(dve)
            l1x_dve(dve)
            l1a_dve(dve)
            l1f_dve(dve)

        @block.tensor
        def _(pe):
            l0x_pe(pe)
            l0a_pe(pe)
            l0f_pe(pe)
            l1x_pe(pe)
            l1a_pe(pe)
            l1f_pe(pe)


def kernel(**inputs):
    import numpy as _np
    import concourse.bacc as _bacc
    from concourse import mybir as _mybir
    from concourse.bass_utils import run_bass_kernel_spmd as _run

    g = {k: _np.ascontiguousarray(v) for k, v in inputs.items()}
    cat = _np.concatenate

    def rows_to_partitions(w):
        return w.reshape(C2, P, -1).transpose(1, 0, 2)

    def by_head(w, width):
        n = w.shape[1] // width
        return w.reshape(C2, P, n, width).transpose(2, 1, 0, 3).reshape(n, P, C2 * width)

    def head_rows(w, n):
        return w.reshape(n, P, D)

    wkv = g["L0_xattn_Wkv"]
    w_x0 = rows_to_partitions(cat([g["L0_xattn_Wq"], wkv, g["L0_xattn_Wp"]], axis=1))
    w_l0a = cat([by_head(g["L0_attn_Wq"], HD), by_head(g["L0_attn_Wk"], HD), by_head(g["L0_attn_Wv"], HD), head_rows(g["L0_attn_Wo"], H)], axis=2)
    gu = g["L0_ffn_w_gate_up"].reshape(E0, C2, P, 2, P).transpose(0, 2, 3, 1, 4).reshape(E0, P, 512)
    sgu = g["L0_ffn_w_sh_gate_up"].reshape(C2, P, 2, 4, P).transpose(3, 1, 2, 0, 4).reshape(4, P, 512)
    w_l0f = cat([cat([gu, g["L0_ffn_w_down"]], axis=2), cat([sgu, head_rows(g["L0_ffn_w_sh_down"], 4)], axis=2)], axis=0)
    w_l1p = cat([by_head(g["L1_xattn_q_w"], HD), by_head(g["L1_xattn_ki_w"], HD)], axis=2)
    w_l1x = cat([by_head(g["L1_xattn_vi_w"], HD), head_rows(g["L1_xattn_o_w"], H)], axis=2)
    wd = g["L1_attn_W_d"].reshape(C2, P, H // 2, 2, HD).transpose(2, 1, 3, 0, 4).reshape(H // 2, P, 512)
    wpr = g["L1_attn_W_proj"].reshape(H // 2, 2, P, D).transpose(0, 2, 1, 3).reshape(H // 2, P, 512)
    w_l1a = cat([wd, wpr], axis=2)
    n1 = 4 * CH1

    def turned_rows(w):
        return w.reshape(n1, P, C2, P).transpose(0, 3, 2, 1).reshape(n1, P, 2 * P)

    w_l1f = cat([turned_rows(g["L1_ffn_w1"]), turned_rows(g["L1_ffn_w3"]), g["L1_ffn_w2"].transpose(0, 2, 1).reshape(n1, P, D)], axis=2)
    gates = _np.stack([rows_to_partitions(g["L0_ffn_w_gate"]), rows_to_partitions(g["L1_ffn_Wg"].T)], axis=1)
    cols = [g[k].reshape(H, P).T for k in ("L1_xattn_q_b", "L1_xattn_ki_b", "L1_xattn_vi_b", "L1_xattn_nq_s", "L1_xattn_nki_s", "L1_attn_b_d")]
    vecs = cat(cols + [g["L1_attn_b_latent"].reshape(1, P).T, g["L0_xattn_bkv"][D:].reshape(C2, P).T], axis=1)
    two = [g["L0_xattn_bq"], g["L0_xattn_bkv"][:D], g["L0_xattn_bp"], g["L1_xattn_o_b"], g["L1_attn_b_proj"], g["L1_attn_b_latent"], g["L0_attn_lambda_init"]]
    rows = cat(two).reshape(1, NROW)
    ident = _np.eye(P, dtype=_np.float32)
    key, query = _np.arange(T)[None, :], _np.arange(P)[:, None] % T
    mask = _np.where(key <= query, 0.0, -3.0e38).astype(_np.float32)
    half = HD // 2
    inv = (_np.float32(10000.0) ** (-_np.arange(half, dtype=_np.float32) / _np.float32(half))).astype(_np.float32)
    ang = (_np.arange(T, dtype=_np.float32)[:, None] * inv[None, :]).astype(_np.float32)
    rope = _np.stack([_np.repeat(_np.cos(ang), 2, axis=1).T, _np.repeat(_np.sin(ang), 2, axis=1).T], axis=1).astype(_np.float32)
    rotm = _np.zeros((P, P), _np.float32)
    rotm[_np.arange(0, P, 2), _np.arange(1, P, 2)] = -1.0
    rotm[_np.arange(1, P, 2), _np.arange(0, P, 2)] = 1.0

    named = {
        "x_in": g["x"].reshape(NT, P, D).transpose(1, 0, 2), "ctx_in": g["ctx_2048"].transpose(1, 0, 2), "w_x0": w_x0, "w_l0a": w_l0a, "w_l0f": w_l0f,
        "w_l1p": w_l1p, "w_l1x": w_l1x, "w_l1a": w_l1a, "w_l1f": w_l1f, "gates": gates, "vecs": vecs, "rows": rows,
        "ident_in": ident, "mask_in": mask, "rope_in": rope, "rotm_in": rotm, "wl_in": rows_to_partitions(g["L1_attn_W_latent"]),
    }
    nc = _bacc.Bacc("TRN2", target_bir_lowering=False, num_devices=1)
    arrays, args = {}, {}
    for name, a in named.items():
        arrays[name] = _np.ascontiguousarray(a)
        args[name] = nc.dram_tensor(name, arrays[name].shape, _mybir.dt.from_np(arrays[name].dtype), kind="ExternalInput").ap()
    out = nc.dram_tensor("x_out", (NT, P, D), F32, kind="ExternalOutput").ap()
    build(nc, out=out.rearrange("t p d -> p t d"), **args)
    r = _run(nc, [arrays], core_ids=[0])
    return r.results[0]["x_out"].reshape(B, T, D)
```

```python
from contextlib import ExitStack

import numpy as np

import concourse.bass as bass
from concourse import mybir

ALU = mybir.AluOpType
ACT = mybir.ActivationFunctionType
AX = mybir.AxisListType
F32 = mybir.dt.float32
F32R = mybir.dt.float32r
BF16 = mybir.dt.bfloat16

P = 128
D = 256
C2 = D // P
B, T = 8, 64
NT = B * T // P
NTOK = B * T
S = 128
NKT = B
H = 16
HD0 = 16
HW = 64
HD = 128
E0, E1 = 8, 8
CH0 = 12
CH1 = 11
ROUND = 12582912.0
LN255 = float(np.log(255.0))
RING = 4
SENT = -3.0e38
WA, WB = 768, 512

L0A = (0, 16, 768, 256)
L0F = (16, 12, 512, 256)
L1P = (28, 16, 256, 256)
L1X = (44, 16, 256, 256)
L1A = (60, 8, 512, 512)
L1F = (68, 44, 512, 256)

QB, KB, VB, NQ, NK, DB = 0, 16, 32, 48, 64, 80
LB, XVB = 96, 97
NVEC = 99
R_BQ, R_BK, R_BP, R_OB, R_PB, R_LB, R_LAM = 0, D, 2 * D, 3 * D, 4 * D, 5 * D, 5 * D + HD
NROW = R_LAM + H


def place(b):
    return (b // 2) % 2, 2 * (b // 4) + b % 2


class Count:

    def __init__(self, base):
        self.base, self.n = base, 0

    def up(self):
        self.n += 1
        return self.base + self.n


def build(nc, x_in, ctx_in, w_x0, w_l0a, w_l0f, w_l1p, w_l1x, w_l1a, w_l1f, gates, vecs, rows, ident_in, mask_in, rope_in, rotm_in, wl_in, out):
    with ExitStack() as top:
        def sem(name):
            return top.enter_context(nc.semaphore(name))

        def sb(name, shape, dt=F32, ctx=top):
            return ctx.enter_context(nc.sbuf_tensor(name, shape, dt))

        ps = top.enter_context(nc.psum_tensor("ps", [P, 8, 512], F32))

        x = sb("x", [P, NT, D])
        xn = sb("xn", [P, NT, D])
        xt_hi = sb("xt_hi", [P, C2, NTOK], F32R)
        xt_lo = sb("xt_lo", [P, C2, NTOK], F32R)
        stats = sb("stats", [P, NT, 6])
        mv = sb("mv", [P, NT, 2])
        vareps = sb("vareps", [P, NT])
        rstd = sb("rstd", [P, NT])
        neghalf = sb("neghalf", [P, NT])
        ident = sb("ident", [P, P])
        ident_bf = sb("ident_bf", [P, P], BF16)
        mask = sb("mask", [P, T])
        rope = sb("rope", [P, 2, T])
        vec = sb("vec", [P, NVEC])
        row = sb("row", [1, NROW])
        ones = sb("ones", [P, P])
        zero = sb("zero", [1, 1])
        rnd = sb("rnd", [P, 1])
        gate = sb("gate", [P, 2, C2, 8])
        gate_hi = sb("gate_hi", [P, 2, C2, 8], F32R)
        gate_lo = sb("gate_lo", [P, 2, C2, 8], F32R)
        raw = sb("raw", [P, 2, 1024])
        wa_hi = sb("wa_hi", [P, 2, WA], F32R)
        wa_lo = sb("wa_lo", [P, 2, WA], F32R)
        wb_hi = sb("wb_hi", [P, 2, WB], F32R)
        wb_lo = sb("wb_lo", [P, 2, WB], F32R)
        ctx = sb("ctx", [P, NKT, D])
        soft = sb("soft", [P, 3, 512])
        st, pr = soft[:, 0, :], soft[:, 1:3, :]
        rms = sb("rms", [P, NKT + NT])
        mx = sb("mx", [P, 8])
        sm = sb("sm", [P, 8])
        rc = sb("rc", [P, 8])
        lam = sb("lam", [P, H])
        mo = ExitStack()
        ex = sb("ex", [P, RING, B * S], ctx=mo)
        mo.close()
        ot_hi = sb("ot_hi", [P, 2, 2, 512], F32R)
        ot_lo = sb("ot_lo", [P, 2, 2, 512], F32R)
        rotm = sb("rotm", [P, P])
        wl = sb("wl", [P, C2, HD])
        wl_hi = sb("wl_hi", [P, C2, HD], F32R)
        wl_lo = sb("wl_lo", [P, C2, HD], F32R)

        loaded = [sem("ctx_loaded"), sem("ident_loaded"), sem("x_loaded"), sem("wkv_loaded"), sem("wqp_loaded"), sem("row_loaded")]
        set_up = sem("set_up")
        passed_pool, passed_pe = sem("passed_pool"), sem("passed_pe")
        ct_t, ct_hi_done, ct_lo_done, wx_split = sem("ct_t"), sem("ct_hi_done"), sem("ct_lo_done"), sem("wx_split")
        consts = sem("consts")
        a_loaded = [sem("a_loaded_0"), sem("a_loaded_1")]
        b_loaded = [sem("b_loaded_0"), sem("b_loaded_1")]
        a_hi, b_hi = sem("a_hi"), sem("b_hi")
        a_split, b_split = sem("a_split"), sem("b_split")
        a_used, b_used = sem("a_used"), sem("b_used")
        ln_step, ln_pow, ln_xn, ln_t, ln_hi, ln_lo = (sem(n) for n in ("ln_step", "ln_pow", "ln_xn", "ln_t", "ln_hi", "ln_lo"))
        x0 = {n: sem("x0_" + n) for n in (
            "wx_hi", "kz", "kb", "kbe", "wk_lo", "mm", "qe", "ke", "ve", "dve", "q1", "q2", "vr", "qrep", "kint", "kd", "k1", "kres", "k2", "krep", "idbf", "vti", "vi_t", "vi",
            "turn", "qt", "kt", "s", "nm", "nb", "e", "rnd_add", "rnd_pool", "rnd_dve", "t", "pt_dve", "pt_act", "pv", "rs", "out", "y", "at_t", "at_hi", "at_lo")}
        l0 = {n: sem("l0_" + n) for n in ("lam", "q", "k", "qe", "ke", "ve", "s", "se", "dve", "sh", "e", "d", "t", "te", "pv", "ohi", "olo")}
        ff = {n: sem("ff_" + n) for n in ("lg", "dve", "shift", "e", "comb", "ghi", "glo", "g", "sg", "h", "hhi", "hlo", "ev")}
        l1 = {n: sem("l1_" + n) for n in ("acc0", "nqk", "sqq", "kst", "qst", "sqk", "acck", "accq", "ms", "var", "rk", "diag", "placed", "qn", "kn", "s", "se", "dve", "sh", "e", "p", "t", "te", "u", "uhi", "ulo", "ohi", "olo")}
        la = {n: sem("la_" + n) for n in ("whi", "wlo", "lt", "lte", "late", "rot", "dve", "kr", "krot", "q", "qe", "s", "se", "sh", "e", "p", "t", "te", "pv", "ohi", "olo")}

        x_ready = sem("x_ready")
        y_done = sem("y_done")
        stored = sem("stored")

        def mm3(o, a, b, start, stop, **kw):
            nc.tensor.matmul(o, a[0], b[0], start=start, stop=False, **kw)
            nc.tensor.matmul(o, a[0], b[1], start=False, stop=False, **kw)
            return nc.tensor.matmul(o, a[1], b[0], start=False, stop=stop, **kw)

        def xt(c, lo, n):
            return xt_hi[:, c, lo:lo + n], xt_lo[:, c, lo:lo + n]

        def wa(u, lo, n):
            return wa_hi[:, u, lo:lo + n], wa_lo[:, u, lo:lo + n]

        def wb(u, lo, n, k0=0, k1=P):
            return wb_hi[k0:k1, u, lo:lo + n], wb_lo[k0:k1, u, lo:lo + n]

        SET_UP = 6

        def apart(eng):
            eng.sem_inc(passed_pool if eng is nc.gpsimd else passed_pe, 1)

        def load_block(sp, n, k, m, src, stage):
            u, a, cols = k % 2, stage[2], stage[2] + stage[3]
            old = not isinstance(n, int) or n >= 2
            if old:
                sp.wait_ge(a_split, n - 1)
                if isinstance(n, int):
                    sp.wait_ge(b_split, n - 1)
            block_of = src[bass.ds(m, 1)].rearrange("a p m -> p (a m)")
            sp.dma_start(raw[:, u, 0:a], block_of[:, 0:a]).then_inc(a_loaded[u], 16)
            if old:
                sp.wait_ge(b_split, n - 1)
            sp.dma_start(raw[:, u, a:cols], block_of[:, a:cols]).then_inc(b_loaded[u], 16)

        def load_stage(sp, src, stage):
            first, count = stage[0], stage[1]
            for u in range(2):
                load_block(sp, first + u, u, u, src, stage)
            with sp.Fori(1, count // 2) as i:
                for u in range(2):
                    load_block(sp, 2 * i + (first + u), u, 2 * i + u, src, stage)

        def hi_part(act, part, i, k, stage, stride=2):
            n, u = stride * i + k, k % 2
            old = not isinstance(n, int) or n >= 2
            cols = slice(0, stage[2]) if part == "a" else slice(stage[2], stage[2] + stage[3])
            dst, loaded_, done, used = (wa_hi, a_loaded, a_hi, a_used) if part == "a" else (wb_hi, b_loaded, b_hi, b_used)
            act.wait_ge(loaded_[u], 16 * ((stride // 2) * i + k // 2) + 16)
            if old:
                act.wait_ge(used, n - 1)
            nc.scalar.activation(dst[:, u, 0:cols.stop - cols.start], raw[:, u, cols], ACT.Copy).then_inc(done, 1)

        def lo_part(pool, part, i, k, stage, stride=2):
            n, u = stride * i + k, k % 2
            cols = slice(0, stage[2]) if part == "a" else slice(stage[2], stage[2] + stage[3])
            hi, lo, ready, done = (wa_hi, wa_lo, a_hi, a_split) if part == "a" else (wb_hi, wb_lo, b_hi, b_split)
            w = cols.stop - cols.start
            pool.wait_ge(ready, n + 1)
            nc.gpsimd.tensor_tensor(lo[:, u, 0:w], raw[:, u, cols], hi[:, u, 0:w].bitcast(F32), ALU.subtract).then_inc(done, 1)

        def next_part(f, eng, i, u, stage, following, lead=1):
            n = 2 * i + u + lead if isinstance(i, int) else 0
            if n < stage[1] or (n == stage[1] and following):
                f(eng, "a", i, stage[0] + u + lead, following if n == stage[1] else stage)

        def peeled(eng, count, step):
            for u in range(2):
                step(0, u)
            with eng.Fori(1, count // 2 - 1) as i:
                for u in range(2):
                    step(i, u)
            for u in range(2):
                step(count // 2 - 1, u)

        def lo_parts(pool, stage, following, lead=1):
            def step(i, u):
                lo_part(pool, "b", i, stage[0] + u, stage)
                next_part(lo_part, pool, i, u, stage, following, lead)

            peeled(pool, stage[1], step)

        LNS = 3

        def ln_dve_stats(dve, n):
            for t in range(NT):
                last = nc.vector.bn_stats(stats[:, t, :], x[:, t, :])
            last.then_inc(ln_step, 1)
            dve.wait_ge(ln_step, LNS * n + 1)
            for t in range(NT):
                last = nc.vector.bn_aggr(mv[:, t, :], stats[:, t, :])
            last.then_inc(ln_step, 1)
            dve.wait_ge(ln_step, LNS * n + 2)
            nc.vector.tensor_scalar(vareps[:], mv[:, :, 1], 1e-5, None, ALU.add).then_inc(ln_step, 1)
            dve.wait_ge(ln_pow, n + 1)
            for t in range(NT):
                last = nc.vector.tensor_scalar(xn[:, t, :], x[:, t, :], mv[:, t, 0:1], rstd[:, t:t + 1], ALU.subtract, ALU.mult)
                if t % 2 == 1:
                    last.then_inc(ln_xn, 1)

        def ln_views(j):
            def of(buf):
                return buf[:, :, 2 * j * P:2 * (j + 1) * P].rearrange("p c (t n) -> p t c n", n=P)

            return ps[:, j, :].rearrange("p (t c n) -> p t c n", t=2, c=C2), of(xt_hi), of(xt_lo)

        def ln_dve_split(dve, n):
            for j in range(2):
                bank, hi, lo = ln_views(j)
                dve.wait_ge(ln_hi, 2 * n + j + 1)
                nc.vector.tensor_tensor(lo, bank, hi.bitcast(F32), ALU.subtract).then_inc(ln_lo, 1)

        def ln_dve(dve, n):
            ln_dve_stats(dve, n)
            ln_dve_split(dve, n)

        def ln_pool(pool, n):
            pool.wait_ge(ln_step, LNS * n + 3)
            nc.gpsimd.tensor_tensor(rstd[:], vareps[:], neghalf[:], ALU.pow).then_inc(ln_pow, 1)

        def ln_pe(pe, n):
            for t in range(NT):
                if t % 2 == 0:
                    pe.wait_ge(ln_xn, 2 * n + t // 2 + 1)
                for c in range(C2):
                    last = nc.tensor.transpose(ps[:, t // 2, ((t % 2) * C2 + c) * P:((t % 2) * C2 + c + 1) * P], xn[:, t, c * P:(c + 1) * P], ident[:])
                if t % 2 == 1:
                    last.then_inc(ln_t, 1)

        def ln_act(act, n):
            for j in range(2):
                bank, hi, _ = ln_views(j)
                act.wait_ge(ln_t, 2 * n + j + 1)
                nc.scalar.activation(hi, bank, ACT.Copy).then_inc(ln_hi, 1)

        def twice(off):
            return row[:, off:off + D].unsqueeze(1).broadcast_to([1, 2, D])

        def y_start(off):
            src = twice(off) if off is not None else zero[:, :].broadcast_to([1, 512])
            for k in range(2):
                nc.tensor.matmul(ps[:, 6 + k, :], ones[0:1, :], src, start=True, stop=False, skip_group_check=True)

        def y_add(o, w, final=False):
            for t in range(NT):
                last = mm3(ps[:, 6 + t // 2, (t % 2) * D:(t % 2 + 1) * D], o(t), w, False, final and t % 2 == 1, skip_group_check=True)
                if final and t == 1:
                    last.then_inc(y_done, 1)
            return last

        def add_y(dve, n, whole):
            for k in range(2):
                dve.wait_ge(*((y_done, n + 1) if k == 0 else whole))
                v = x[:, 2 * k:2 * k + 2, :].rearrange("p t d -> p (t d)")
                nc.vector.tensor_tensor(v, ps[:, 6 + k, :], v, ALU.add).then_inc(x_ready, 1)
            dve.wait_ge(x_ready, 2 * n + 2)

        def flat(ap):
            return ap.rearrange("p a b -> p (a b)")

        mc = ExitStack()
        ct_hi = sb("ct_hi", [P, C2, B * S], F32R, mc)
        ct_lo = sb("ct_lo", [P, C2, B * S], F32R, mc)
        acc = sb("acc", [P, 1536], ctx=mc)
        m0 = ExitStack()
        wx = sb("wx", [P, C2, 1024], ctx=m0)
        wx_hi = sb("wx_hi", [P, C2, 1024], F32R, m0)
        wx_lo = sb("wx_lo", [P, C2, 1024], F32R, m0)
        qf = sb("qf", [P, NT, D], ctx=m0)
        kf = sb("kf", [P, NKT, D], ctx=m0)
        vf = sb("vf", [P, C2, B * S], ctx=m0)
        kres = sb("kres", [P, NKT, D], ctx=m0)
        qs = sb("qs", [P, NT * H], ctx=m0)
        qr = sb("qr", [P, NT * H], ctx=m0)
        ks = sb("ks", [P, NKT * H], ctx=m0)
        kr = sb("kr", [P, NKT * H], ctx=m0)
        vs = sb("vs", [P, C2], ctx=m0)
        vr = sb("vr", [P, C2], ctx=m0)
        q_rep = sb("q_rep", [P, NT, (H + 2) * HW], BF16, m0)
        k_rep = sb("k_rep", [P, NKT, (H + 2) * HW], BF16, m0)
        vti = sb("vti", [P, C2, B * S], BF16, m0)
        vi = sb("vi", [P, NKT, D], BF16, m0)
        qt = sb("qt", [P, 2, NTOK], BF16, m0)
        kt = sb("kt", [P, 2, B * S], BF16, m0)
        ei = flat(kres[:]).bitcast(BF16).rearrange("p (r n) -> p r n", r=RING)
        pt = flat(vf[:]).bitcast(BF16).rearrange("p (r n) -> p r n", r=RING)
        kb = sb("kb", [P, D], ctx=m0)
        nm = sb("nm", [P, 2], ctx=m0)
        nb = sb("nb", [P, 2], ctx=m0)
        sums = sb("sums", [P, 2, 8], ctx=m0)
        rs = sb("rs", [P, 8], ctx=m0)
        m0.close()
        m1 = ExitStack()
        qh = sb("qh", [P, 512], ctx=m1)
        kh = sb("kh", [P, 512], ctx=m1)
        vh = sb("vh", [P, 2, NT, HD], ctx=m1)
        dd = sb("dd", [P, 2, 256], ctx=m1)
        ddt = sb("ddt", [P, 2, P], ctx=m1)
        m1.close()
        m2 = ExitStack()
        lg = sb("lg", [P, NT, 16], ctx=m2)
        top8 = sb("top8", [P, NT, 8], ctx=m2)
        rep = sb("rep", [P, NT, 16], ctx=m2)
        sel = sb("sel", [P, NT, 8], ctx=m2)
        sh = sb("sh", [P, NT, 8], ctx=m2)
        ssum = sb("ssum", [P, NT], ctx=m2)
        comb = sb("comb", [P, CH0, NT], ctx=m2)
        sg = sb("sg", [P, 2, 512], ctx=m2)
        hh = sb("hh", [P, 2, 512], ctx=m2)
        h_hi = sb("h_hi", [P, 2, 512], F32R, m2)
        h_lo = sb("h_lo", [P, 2, 512], F32R, m2)
        m2.close()
        m3 = ExitStack()
        kst = sb("kst", [P, H, B * S], ctx=m3)
        qst = sb("qst", [P, H, NTOK], ctx=m3)
        nqk = sb("nqk", [P, H], ctx=m3)
        m3.close()
        sq = flat(soft[:])
        rq = flat(xn[:, 0:2, :])
        rk = flat(xn[:, 2:4, :]).rearrange("p (g k) -> p g k", g=4)
        m4 = ExitStack()
        qc = sb("qc", [P, B, 2, T], ctx=m4)
        qsn = sb("qsn", [P, B, 2, T], ctx=m4)
        lt = sb("lt", [P, NTOK], ctx=m4)
        lat = sb("lat", [P, NT, HD], ctx=m4)
        krot = sb("krot", [P, 2, NTOK], ctx=m4)
        lcos = sb("lcos", [P, NTOK], ctx=m4)
        lsin = sb("lsin", [P, NTOK], ctx=m4)
        dtl = sb("dtl", [P, NT, P], ctx=m4)
        m4.close()
        mc.close()
        mu = ExitStack()
        qn = sb("qn", [P, 2, NTOK], ctx=mu)
        kn = sb("kn", [P, 2, B * S], ctx=mu)
        ptx = sb("ptx", [P, 4, P], ctx=mu)
        u_hi = sb("u_hi", [P, C2, 512], F32R, mu)
        u_lo = sb("u_lo", [P, C2, 512], F32R, mu)
        mu.close()


        def setup_sync(sp):
            sp.dma_start(ctx[:], ctx_in).then_inc(loaded[0], 16)
            sp.dma_start(ident[:], ident_in).then_inc(loaded[1], 16)
            sp.dma_start(wx[:, :, D:3 * D], w_x0[:, :, D:3 * D]).then_inc(loaded[3], 16)
            sp.dma_start(row[:], rows).then_inc(loaded[5], 16)
            sp.dma_start(x[:], x_in).then_inc(loaded[2], 16)
            for k in (0, 3):
                sp.dma_start(wx[:, :, k * D:(k + 1) * D], w_x0[:, :, k * D:(k + 1) * D]).then_inc(loaded[4], 16)
            for dst, src in ((vec, vecs), (mask, mask_in), (rope, rope_in), (gate, gates), (rotm, rotm_in), (wl, wl_in)):
                sp.dma_start(dst[:], src).then_inc(consts, 16)

        CONSTS = 6 * 16

        def clear_idle(eng, buf, signal):
            heads = buf[:, :, 0:H * HW].rearrange("p t (h w) -> p t h w", w=HW)
            eng.memset(heads[:, :, :, 3 * HD0:HW], 0.0).then_inc(signal, 1)
            eng.memset(buf[:, :, H * HW:(H + 2) * HW], 0.0).then_inc(signal, 1)

        def setup_pool(pool):
            nc.gpsimd.memset(ones[:], 1.0).then_inc(set_up, 1)
            nc.gpsimd.memset(zero[:], 0.0).then_inc(set_up, 1)
            nc.gpsimd.memset(neghalf[:], -0.5).then_inc(set_up, 1)
            nc.gpsimd.memset(rnd[:], ROUND).then_inc(set_up, 1)
            clear_idle(nc.gpsimd, q_rep, set_up)

        def bank_bf(b):
            return ps[:, b, :].bitcast(BF16)

        VBANK = ((6, 8), (2, 4))

        def l0x_pe_before(pe):
            pe.wait_ge(loaded[0], 16)
            pe.wait_ge(loaded[1], 16)
            for c in range(C2):
                for k in range(NKT):
                    last = nc.tensor.transpose(ps[:, 2 + 2 * c + k // 4, (k % 4) * P:(k % 4 + 1) * P], ctx[:, k, c * P:(c + 1) * P], ident[:])
            last.then_inc(ct_t, 1)
            pe.wait_ge(loaded[5], 16)
            pe.wait_ge(set_up, 4)
            nc.tensor.matmul(ps[:, 0, 0:D], ones[0:1, :], row[:, R_BK:R_BK + D], start=True, stop=True).then_inc(x0["kb"], 1)
            pe.wait_ge(x0["wk_lo"], 1)
            pe.wait_ge(ct_lo_done, 1)
            for j in range(2):
                for k in (2 * j, 2 * j + 1):
                    for t in (2 * k, 2 * k + 1):
                        for c in range(C2):
                            last = mm3(ps[:, 2 + k, (t % 2) * D:(t % 2 + 1) * D], (ct_hi[:, c, t * P:(t + 1) * P], ct_lo[:, c, t * P:(t + 1) * P]),
                                       (wx_hi[:, c, D:2 * D], wx_lo[:, c, D:2 * D]), t % 2 == 0 and c == 0, t % 2 == 1 and c == 1, skip_group_check=True)
                last.then_inc(x0["mm"], 1)
            pe.wait_ge(x0["kbe"], 1)
            ln_pe(pe, 0)

            def values(m):
                for j in range(2):
                    for c in range(C2):
                        cols = slice(2 * D + m * P, 2 * D + (m + 1) * P)
                        last = mm3(ps[:, VBANK[m][0] + j, :], (wx_hi[:, c, cols], wx_lo[:, c, cols]),
                                   (ct_hi[:, c, j * 512:(j + 1) * 512], ct_lo[:, c, j * 512:(j + 1) * 512]), c == 0, c == 1)
                last.then_inc(x0["mm"], 1)

            pe.wait_ge(wx_split, 1)
            values(0)
            pe.wait_ge(ln_lo, 2)
            pe.wait_ge(wx_split, 2)
            for k in range(2):
                nc.tensor.matmul(ps[:, k, :], ones[0:1, :], twice(R_BQ), start=True, stop=False, skip_group_check=True)
                for t in (2 * k, 2 * k + 1):
                    for c in range(C2):
                        last = mm3(ps[:, k, (t % 2) * D:(t % 2 + 1) * D], xt(c, t * P, P), (wx_hi[:, c, 0:D], wx_lo[:, c, 0:D]),
                                   False, t % 2 == 1 and c == 1, skip_group_check=True)
            last.then_inc(x0["mm"], 1)
            pe.wait_ge(x0["ke"], 1)
            values(1)
            pe.wait_ge(x0["qrep"], 1)
            pe.wait_ge(x0["krep"], 2)
            pe.wait_ge(x0["qe"], 1)
            pe.wait_ge(x0["ve"], 2)
            pe.wait_ge(x0["idbf"], 1)
            l0x_turn(pe, 0, 0)

        VI_TURN = 3

        def l0x_turn_values(pe):
            pe.wait_ge(x0["vti"], 1)
            for k in range(NKT):
                for c in range(C2):
                    last = nc.tensor.transpose(bank_bf(6 + k // 4)[:, (k % 4) * D + c * P:(k % 4) * D + (c + 1) * P], vti[:, c, k * P:(k + 1) * P], ident_bf[:])
            last.then_inc(x0["vi_t"], 1)
            pe.wait_ge(x0["vi"], 1)

        def l0x_turn(pe, pair, u):
            for t in range(NT):
                nc.tensor.transpose(bank_bf(0)[:, t * P:(t + 1) * P], q_rep[:, t, bass.ds(pair * 2 * HW, P)], ident_bf[:])
            for t in range(NKT):
                last = nc.tensor.transpose(bank_bf(1)[:, t * P:(t + 1) * P], k_rep[:, t, bass.ds(pair * 2 * HW, P)], ident_bf[:])
            last.then_inc(x0["turn"], 1)

        TL, VL, TURN, OUT = 4, 6, 2, 5
        EV_ACT = tuple(r for r in range(16) if r % 8 != 6)
        RND_POOL = (1, 4, 9, 12)

        def shared(i, m, mine, sem_mine, sem_other):
            q, r = divmod(m, 16)
            if r in mine:
                return sem_mine, (i + q) * len(mine) + len([a for a in mine if a <= r])
            return sem_other, (i + q) * (16 - len(mine)) + len([a for a in range(r + 1) if a not in mine])

        def copied(i, m):
            return shared(i, m, EV_ACT, x0["pt_act"], x0["pt_dve"])

        def rounded(i, m):
            return shared(i, m, RND_POOL, x0["rnd_pool"], x0["rnd_dve"])

        def exists(i, n):
            return not isinstance(i, int) or n >= 0

        def l0x_pe_unit(pe, i, m, live=True):
            n, k, a, t = 16 * i + m, m % 8, (m % 8) // 4, m % 4
            pair, u = 2 * i + m // 8, (m // 8) % 2
            if live:
                if k == 0:
                    pe.wait_ge(x0["qt"], pair + 1)
                    pe.wait_ge(x0["kt"], pair + 1)
                if exists(i, n - 2):
                    pe.wait_ge(x0["e"], n - 1)
                for j in range(2):
                    last = nc.tensor.matmul(ps[:, 2 + 2 * (m % 2) + j, :], qt[64 * a:64 * a + 48, u, t * P:(t + 1) * P],
                                            kt[64 * a:64 * a + 48, u, j * 512:(j + 1) * 512], start=True, stop=True)
                last.then_inc(x0["s"], 1)
            if exists(i, n - TL) and (live or m < TL):
                pe.wait_ge(*rounded(i, m - TL))
                if exists(i, n - TL - 2):
                    pe.wait_ge(*copied(i, m - TL - 2))
                for kk in range(NKT):
                    last = nc.tensor.transpose(bank_bf(6 + (m - TL) % 2)[:, kk * P:(kk + 1) * P], ei[:, (m - TL) % RING, kk * P:(kk + 1) * P], ident_bf[:])
                last.then_inc(x0["t"], 1)
            if exists(i, n - VL):
                q, kp = divmod(m - VL, 8)
                if kp == 0 and exists(i, n - VL - 1):
                    pe.wait_ge(x0["out"], 2 * i + q)
                if live and k == TURN + 1:
                    pe.wait_ge(x0["qt"], pair + 2)
                pe.wait_ge(*copied(i, m - VL))
                for kk in range(NKT):
                    last = nc.tensor.matmul(ps[:, 0, 256 + 16 * kp:272 + 16 * kp], pt[:, (m - VL) % RING, kk * P:(kk + 1) * P],
                                            vi[:, kk, bass.ds((2 * i + q) * 32 + (kp // 4) * HD0, HD0)], start=kk == 0, stop=kk == NKT - 1)
                last.then_inc(x0["pv"], 1)
            if live and k == TURN:
                l0x_turn(pe, pair + 1, 1 - u)

        def l0x_pe(pe):
            l0x_pe_before(pe)
            for m in range(16):
                l0x_pe_unit(pe, 0, m)
                if m == VI_TURN:
                    l0x_turn_values(pe)
            with pe.Fori(1, 4) as i:
                for m in range(16):
                    l0x_pe_unit(pe, i, m)
            for m in range(VL):
                l0x_pe_unit(pe, 4, m, live=False)
            pe.wait_ge(x0["out"], 8)
            for c in range(C2):
                for t in range(NT):
                    last = nc.tensor.transpose(ps[:, 2 + c, t * P:(t + 1) * P], xn[:, t, c * P:(c + 1) * P], ident[:])
            last.then_inc(x0["at_t"], 1)
            y_start(R_BP)
            pe.wait_ge(x0["at_lo"], 1)
            for c in range(C2):
                last = y_add(lambda t: xt(c, t * P, P), (wx_hi[:, c, 3 * D:], wx_lo[:, c, 3 * D:]), c == 1)
            last.then_inc(x0["y"], 1)

        def l0x_pool(pool):
            for k, n in ((2, 1), (0, 2), (3, 3)):
                pool.wait_ge(x0["wx_hi"], n)
                cols = slice(k * D, (k + 1) * D)
                nc.gpsimd.tensor_tensor(wx_lo[:, :, cols], wx[:, :, cols], wx_hi[:, :, cols].bitcast(F32), ALU.subtract).then_inc(wx_split, 1)
            qv = qf[:].rearrange("p t (h e) -> p (t h) e", e=HD0)
            pool.wait_ge(x0["q1"], 1)
            nc.gpsimd.tensor_tensor(qv, qv, qr[:].unsqueeze(2).broadcast_to([P, NT * H, HD0]), ALU.mult).then_inc(x0["q2"], 1)
            pool.wait_ge(x0["vr"], 1)
            nc.gpsimd.tensor_tensor(flat(vti[:]), flat(vf[:]), rnd[:, :].broadcast_to([P, C2 * B * S]), ALU.subtract).then_inc(x0["vti"], 1)

            def unit(i, m):
                n, r = 16 * i + m, rounded(i, m)[1]
                pool.wait_ge(x0["e"], n + 1)
                if exists(i, n - RING):
                    pool.wait_ge(x0["t"], n - RING + 1)
                nc.gpsimd.tensor_tensor(ex[:, m % RING, :], ex[:, m % RING, :], rnd[:, :].broadcast_to([P, B * S]), ALU.add).then_inc(x0["rnd_add"], 1)
                pool.wait_ge(x0["rnd_add"], r)
                nc.gpsimd.tensor_tensor(ei[:, m % RING, :], ex[:, m % RING, :], rnd[:, :].broadcast_to([P, B * S]), ALU.subtract).then_inc(x0["rnd_pool"], 1)

            for m in RND_POOL:
                unit(0, m)
            with pool.Fori(1, 4) as i:
                for m in RND_POOL:
                    unit(i, m)

        def l0x_copy_pt(eng, i, m):
            n = 16 * i + m
            act = m % 16 in EV_ACT
            eng.wait_ge(x0["t"], n + 1)
            if exists(i, n - RING):
                eng.wait_ge(x0["pv"], n - RING + 1)
            if act:
                nc.scalar.activation(pt[:, m % RING, :], bank_bf(6 + m % 2), ACT.Copy).then_inc(x0["pt_act"], 1)
            else:
                nc.vector.tensor_copy(pt[:, m % RING, :], bank_bf(6 + m % 2)).then_inc(x0["pt_dve"], 1)

        def l0x_act(act):
            act.wait_ge(loaded[3], 16)
            nc.scalar.activation(wx_hi[:, :, D:3 * D], wx[:, :, D:3 * D], ACT.Copy).then_inc(x0["wx_hi"], 1)
            act.wait_ge(ct_t, 1)
            for c in range(C2):
                last = nc.scalar.activation(ct_hi[:, c, :], flat(ps[:, 2 + 2 * c:4 + 2 * c, :]), ACT.Copy)
            last.then_inc(ct_hi_done, 1)
            act.wait_ge(x0["kb"], 1)
            nc.scalar.activation(kb[:], ps[:, 0, 0:D], ACT.Copy).then_inc(x0["kbe"], 1)
            act.wait_ge(loaded[4], 32)
            for k in (0, 3):
                nc.scalar.activation(wx_hi[:, :, k * D:(k + 1) * D], wx[:, :, k * D:(k + 1) * D], ACT.Copy).then_inc(x0["wx_hi"], 1)
            ln_act(act, 0)

            def values(c):
                act.wait_ge(x0["mm"], (3, 5)[c])
                nc.scalar.activation(vf[:, c, :], flat(ps[:, VBANK[c][0]:VBANK[c][1], :]), ACT.Identity, bias=vec[:, XVB + c:XVB + c + 1]).then_inc(x0["ve"], 1)

            def key_part(r, j, src):
                dst = k_rep[:, 4 * j:4 * j + 4, 0:H * HW].rearrange("p t (h w) -> p t h w", w=HW)[:, :, :, r * HD0:(r + 1) * HD0]
                nc.scalar.activation(dst, src[:, 4 * j:4 * j + 4, :].rearrange("p t (h e) -> p t h e", e=HD0), ACT.Copy).then_inc(x0["k1"] if r == 0 else x0["k2"], 1)

            act.wait_ge(consts, CONSTS)
            values(0)
            act.wait_ge(x0["mm"], 4)
            nc.scalar.activation(flat(qf[:]), flat(ps[:, 0:2, :]), ACT.Copy, scale=0.25).then_inc(x0["qe"], 1)
            for j in range(2):
                act.wait_ge(x0["kd"], j + 1)
                key_part(0, j, kf)
            values(1)
            for j in range(2):
                act.wait_ge(x0["kres"], j + 1)
                key_part(1, j, kres)

            def turned(pair, u):
                act.wait_ge(x0["turn"], pair + 1)
                nc.scalar.activation(qt[:, u, :], bank_bf(0)[:, 0:NTOK], ACT.Copy).then_inc(x0["qt"], 1)

            def unit(i, m, live=True):
                n, k, pair, u = 16 * i + m, m % 8, 2 * i + m // 8, (m // 8) % 2
                if live:
                    act.wait_ge(x0["nb"], n + 1)
                    if exists(i, n - RING):
                        act.wait_ge(*rounded(i, m - RING))
                    if k == 0 and exists(i, n - 16):
                        act.wait_ge(x0["out"], pair - 1)
                    col = (m % 4) * H + (m % 8) // 4
                    nc.scalar.activation(ex[:, m % RING, :], flat(ps[:, 2 + 2 * (m % 2):4 + 2 * (m % 2), :]), ACT.Exp, bias=nb[:, m % 2:m % 2 + 1],
                                         scale=qs[:, bass.ds(2 * pair + col, 1)], accum_out=sums[:, u, k:k + 1]).then_inc(x0["e"], 1)
                if live and k == TURN:
                    turned(pair + 1, 1 - u)
                if (m - TL) % 16 in EV_ACT and exists(i, n - TL) and (live or m < TL):
                    l0x_copy_pt(act, i, m - TL)

            turned(0, 0)
            for m in range(16):
                unit(0, m)
            with act.Fori(1, 4) as i:
                for m in range(16):
                    unit(i, m)
            for m in range(TL):
                unit(4, m, live=False)
            act.wait_ge(x0["at_t"], 1)
            for c in range(C2):
                last = nc.scalar.activation(xt_hi[:, c, :], ps[:, 2 + c, :], ACT.Copy, scale=vs[:, c:c + 1])
            last.then_inc(x0["at_hi"], 1)

        def l0x_dve(dve):
            c = Count(0)
            step = x0["dve"]
            clear_idle(nc.vector, k_rep, x0["kz"])
            dve.wait_ge(loaded[1], 16)
            nc.vector.tensor_copy(ident_bf[:], ident[:]).then_inc(x0["idbf"], 1)
            dve.wait_ge(x0["wx_hi"], 1)
            nc.vector.tensor_tensor(wx_lo[:, :, D:2 * D], wx[:, :, D:2 * D], wx_hi[:, :, D:2 * D].bitcast(F32), ALU.subtract).then_inc(x0["wk_lo"], 1)
            dve.wait_ge(ct_hi_done, 1)
            for k in range(C2):
                last = nc.vector.tensor_tensor(ct_lo[:, k, :], flat(ps[:, 2 + 2 * k:4 + 2 * k, :]), ct_hi[:, k, :].bitcast(F32), ALU.subtract)
            last.then_inc(ct_lo_done, 1)
            dve.wait_ge(loaded[2], 16)
            dve.wait_ge(set_up, SET_UP)
            ln_dve_stats(dve, 0)

            def amax(src, s):
                nc.vector.tensor_reduce(s, src, AX.X, ALU.max, apply_absolute_value=True).then_inc(step, 1)
                c.up()

            def scale_of(s, r, sem_done):
                dve.wait_ge(step, c.base + c.n)
                nc.vector.tensor_scalar(s, s, 1.0 / 127.0, 1e-8, ALU.mult, ALU.max).then_inc(step, 1)
                dve.wait_ge(step, c.up())
                nc.vector.reciprocal(r, s).then_inc(sem_done, 1)
                if sem_done is step:
                    dve.wait_ge(step, c.up())

            def heads(ap, j):
                return ap[:, 4 * j:4 * j + 4, :].rearrange("p t (h e) -> p (t h) e", e=HD0)

            def per_head(ap, j):
                return ap[:, 4 * H * j:4 * H * (j + 1)].unsqueeze(2).broadcast_to([P, 4 * H, HD0])

            for j in range(2):
                dve.wait_ge(x0["mm"], j + 1)
                dve.wait_ge(x0["kbe"], 1)
                nc.vector.tensor_tensor(kf[:, 4 * j:4 * j + 4, :], ps[:, 2 + 2 * j:4 + 2 * j, :].rearrange("p b (t d) -> p (b t) d", d=D),
                                        kb[:].unsqueeze(1).broadcast_to([P, 4, D]), ALU.add).then_inc(x0["ke"], 1)
                if j == 0:
                    ln_dve_split(dve, 0)
                dve.wait_ge(x0["ke"], j + 1)
                amax(heads(kf, j), ks[:, 4 * H * j:4 * H * (j + 1)])
            scale_of(ks[:], kr[:], step)
            for j in range(2):
                nc.vector.tensor_tensor(heads(kf, j), heads(kf, j), per_head(kr, j), ALU.mult).then_inc(step, 1)
                c.up()
            for j in range(2):
                dve.wait_ge(step, c.n - 1 + j)
                kj = kf[:, 4 * j:4 * j + 4, :].rearrange("p t d -> p (t d)")
                nc.vector.tensor_scalar(kj, kj, ROUND, ROUND, ALU.add, ALU.subtract).then_inc(x0["kint"], 1)
            for j in range(2):
                dve.wait_ge(x0["kint"], j + 1)
                nc.vector.tensor_tensor(heads(kf, j), heads(kf, j), per_head(ks, j), ALU.mult).then_inc(x0["kd"], 1)
            qv = qf[:].rearrange("p t (h e) -> p (t h) e", e=HD0)
            dve.wait_ge(x0["qe"], 1)
            amax(qv, qs[:])
            scale_of(qs[:], qr[:], x0["q1"])

            def key_part(r, j):
                return k_rep[:, 4 * j:4 * j + 4, 0:H * HW].rearrange("p t (h w) -> p t h w", w=HW)[:, :, :, r * HD0:(r + 1) * HD0]

            def by_tile(ap, j):
                return ap[:, 4 * j:4 * j + 4, :].rearrange("p t (h e) -> p t h e", e=HD0)

            for j in range(2):
                dve.wait_ge(x0["kd"], j + 1)
                dve.wait_ge(x0["k1"], j + 1)
                nc.vector.tensor_tensor(by_tile(kres, j), by_tile(kf, j), key_part(0, j), ALU.subtract).then_inc(x0["kres"], 1)
            dve.wait_ge(x0["q2"], 1)
            for r in range(3):
                for t in range(NT):
                    dst = q_rep[:, t, 0:H * HW].rearrange("p (h w) -> p h w", w=HW)[:, :, r * HD0:(r + 1) * HD0]
                    last = nc.vector.tensor_scalar(dst, qf[:, t, :].rearrange("p (h e) -> p h e", e=HD0), ROUND, ROUND, ALU.add, ALU.subtract)
            last.then_inc(x0["qrep"], 1)
            for j in range(2):
                dve.wait_ge(x0["kres"], j + 1)
                dve.wait_ge(x0["k2"], j + 1)
                nc.vector.tensor_tensor(key_part(2, j), by_tile(kres, j), key_part(1, j), ALU.subtract).then_inc(x0["krep"], 1)
            dve.wait_ge(x0["ve"], 2)
            amax(vf[:], vs[:])
            scale_of(vs[:], vr[:], step)
            for k in range(C2):
                last = nc.vector.tensor_scalar(vf[:, k, :], vf[:, k, :], vr[:, k:k + 1], ROUND, ALU.mult, ALU.add)
            last.then_inc(x0["vr"], 1)

            def turned(pair, u):
                dve.wait_ge(x0["turn"], pair + 1)
                nc.vector.tensor_copy(kt[:, u, :], bank_bf(1)).then_inc(x0["kt"], 1)

            def outputs(pair, u):
                dve.wait_ge(x0["pv"], 8 * pair + 8)
                nc.vector.reciprocal(rs[:], sums[:, u, :]).then_inc(x0["rs"], 1)
                dve.wait_ge(x0["rs"], pair + 1)
                for a in range(2):
                    last = nc.vector.tensor_tensor(xn[:, :, bass.ds(32 * pair + HD0 * a, HD0)], ps[:, 0, 256 + 64 * a:320 + 64 * a].rearrange("p (t e) -> p t e", t=NT),
                                                   rs[:, 4 * a:4 * a + 4].unsqueeze(2).broadcast_to([P, NT, HD0]), ALU.mult)
                last.then_inc(x0["out"], 1)

            def unit(i, m, live=True):
                n, k, pair, u = 16 * i + m, m % 8, 2 * i + m // 8, (m // 8) % 2
                if live:
                    dve.wait_ge(x0["s"], n + 1)
                    nc.vector.tensor_reduce(nm[:, m % 2:m % 2 + 1], flat(ps[:, 2 + 2 * (m % 2):4 + 2 * (m % 2), :]), AX.X, ALU.max, negate=True).then_inc(x0["nm"], 1)
                    dve.wait_ge(x0["nm"], n + 1)
                    if exists(i, n - 2):
                        dve.wait_ge(x0["e"], n - 1)
                    col = (m % 4) * H + (m % 8) // 4
                    nc.vector.tensor_scalar(nb[:, m % 2:m % 2 + 1], nm[:, m % 2:m % 2 + 1], qs[:, bass.ds(2 * pair + col, 1)], LN255, ALU.mult, ALU.add).then_inc(x0["nb"], 1)
                if k == OUT and exists(i, n - 8):
                    outputs(pair - 1, 1 - u)
                if (m - 1) % 16 not in RND_POOL and exists(i, n - 1) and (live or m < 1):
                    dve.wait_ge(x0["e"], n)
                    if exists(i, n - 1 - RING):
                        dve.wait_ge(x0["t"], n - RING)
                    nc.vector.tensor_scalar(ei[:, (m - 1) % RING, :], ex[:, (m - 1) % RING, :], ROUND, ROUND, ALU.add, ALU.subtract).then_inc(x0["rnd_dve"], 1)
                if (m - TL) % 16 not in EV_ACT and exists(i, n - TL) and (live or m < TL):
                    l0x_copy_pt(dve, i, m - TL)
                if live and k == TURN:
                    turned(pair + 1, 1 - u)

            turned(0, 0)
            for m in range(16):
                unit(0, m)
                if m == VI_TURN:
                    dve.wait_ge(x0["vi_t"], 1)
                    nc.vector.tensor_copy(vi[:].rearrange("p k d -> p (k d)"), flat(ps[:, 6:8, :]).bitcast(BF16)).then_inc(x0["vi"], 1)
            with dve.Fori(1, 4) as i:
                for m in range(16):
                    unit(i, m)
            for m in range(OUT + 1):
                unit(4, m, live=False)
            dve.wait_ge(x0["at_hi"], 1)
            for k in range(C2):
                last = nc.vector.scalar_tensor_tensor(xt_lo[:, k, :], ps[:, 2 + k, :], vs[:, k:k + 1], xt_hi[:, k, :].bitcast(F32), ALU.mult, ALU.subtract)
            last.then_inc(x0["at_lo"], 1)
            add_y(dve, 0, (x0["y"], 1))

        N1 = L0A[0]

        def by_batch(ap):
            return ap.rearrange("p (b e k) -> p e b k", e=2, k=T)

        def banks45():
            return ps[:, 4:6, 0:256].rearrange("p e (b k) -> p e b k", k=T)

        def l0a_project(pe, h, u):
            n = h + N1
            pe.wait_ge(a_split, n + 1)
            for k, name in enumerate(("q", "k")):
                if exists(h, h - 1):
                    pe.wait_ge(l0["se"], h)
                for c in range(C2):
                    last = mm3(ps[:, k, :], wa(u, 2 * P * k + c * P, P), (xt_hi[:, c, :], xt_lo[:, c, :]), c == 0, c == 1)
                last.then_inc(l0[name], 1)
            if exists(h, h - 1):
                pe.wait_ge(l0["ve"], h)
            for t in range(NT):
                for c in range(C2):
                    last = mm3(ps[:, 2, t * P:(t + 1) * P], xt(c, t * P, P), wa(u, 4 * P + c * P, P), c == 0, c == 1)
            last.then_inc(a_used, 1)

        def l0a_turn(pe, h, u):
            pe.wait_ge(l0["d"], h + 1)
            if exists(h, h - 1):
                pe.wait_ge(l0["te"], h)
            for g in range(2):
                last = nc.tensor.transpose(ps[:, 3, g * P:(g + 1) * P], dd[:, u, g * P:(g + 1) * P], ident[:])
            last.then_inc(l0["t"], 1)

        def l0a_pv(pe, h, u):
            pe.wait_ge(l0["te"], h + 1)
            if exists(h, h - 1):
                pe.wait_ge(l0["olo"], h)
            apart(pe)
            for b in range(B):
                p, g = place(b)
                k0 = T * (b % 2)
                last = nc.tensor.matmul(ps[:, 4 + b % 2, (b // 2) * T:(b // 2 + 1) * T], vh[k0:k0 + T, u, b // 2, :], ddt[k0:k0 + T, g // 2, T * p:T * (p + 1)], start=True, stop=True)
            last.then_inc(l0["pv"], 1)

        def l0a_scores(pe, h, u):
            pe.wait_ge(l0["qe"], h + 1)
            pe.wait_ge(l0["ke"], h + 1)
            apart(pe)
            for b in range(B):
                p, g = place(b)
                for f in range(2):
                    r = slice(T * f, T * f + T)
                    last = nc.tensor.matmul(ps[T * p:T * (p + 1), f, g * T:(g + 1) * T], qh[r, b * T:(b + 1) * T], kh[r, b * T:(b + 1) * T], start=True, stop=True)
            last.then_inc(l0["s"], 1)

        def l0a_out(pe, h, u, final=False):
            pe.wait_ge(l0["olo"], h + 1)
            pe.wait_ge(b_split, h + N1 + 1)
            y_add(lambda t: (ot_hi[:, u, 0, t * P:(t + 1) * P], ot_lo[:, u, 0, t * P:(t + 1) * P]), wb(u, 0, D), final).then_inc(b_used, 1)

        def l0a_pe_head(pe, h, u):
            l0a_project(pe, h, u)
            if exists(h, h - 1):
                l0a_turn(pe, h - 1, 1 - u)
            l0a_scores(pe, h, u)
            if exists(h, h - 2):
                l0a_out(pe, h - 2, u)
            if exists(h, h - 1):
                l0a_pv(pe, h - 1, 1 - u)

        def l0a_pe(pe):
            ln_pe(pe, 1)
            pe.wait_ge(x_ready, 2)
            y_start(None)
            pe.wait_ge(consts, CONSTS)
            lam_mm = nc.tensor.matmul(ps[:, 3, 0:H], ones[0:1, :], row[:, R_LAM:R_LAM + H], start=True, stop=True)
            lam_mm.then_inc(l0["lam"], 1)
            pe.wait_ge(l0["lam"], 2)
            pe.wait_ge(ln_lo, 4)
            for u in range(2):
                l0a_pe_head(pe, u, u)
            with pe.Fori(1, H // 2) as i:
                for u in range(2):
                    l0a_pe_head(pe, 2 * i + u, u)
            l0a_turn(pe, H - 1, 1)
            l0a_out(pe, H - 2, 0)
            l0a_pv(pe, H - 1, 1)
            l0a_out(pe, H - 1, 1, final=True)

        def l0a_pool(pool):
            lo_part(pool, "a", 0, L0A[0], L0A)
            ln_pool(pool, 1)
            lo_part(pool, "a", 0, L0A[0] + 1, L0A)
            lo_parts(pool, L0A, L0F, 2)

        def l0a_act(act):
            hi_part(act, "a", 0, L0A[0], L0A)
            ln_act(act, 1)
            act.wait_ge(l0["lam"], 1)
            nc.scalar.activation(lam[:], ps[:, 3, 0:H], ACT.Exp, scale=-1.0).then_inc(l0["lam"], 1)

            def turned(h):
                act.wait_ge(l0["t"], h + 1)
                nc.scalar.activation(flat(ddt[:]), ps[:, 3, 0:2 * P], ACT.Copy).then_inc(l0["te"], 1)

            def after(h, u):
                act.wait_ge(l0["pv"], h + 1)
                if exists(h, h - 2):
                    act.wait_ge(b_used, h + N1 - 1)
                nc.scalar.activation(by_batch(ot_hi[:, u, 0, :]), banks45(), ACT.Copy).then_inc(l0["ohi"], 1)

            def head(i, u):
                h = 2 * i + u
                act.wait_ge(l0["q"], h + 1)
                if exists(h, h - 1):
                    act.wait_ge(l0["s"], h)
                nc.scalar.activation(qh[:], ps[:, 0, :], ACT.Copy).then_inc(l0["qe"], 1)
                act.wait_ge(l0["k"], h + 1)
                nc.scalar.activation(kh[:], ps[:, 1, :], ACT.Copy).then_inc(l0["ke"], 1)
                if exists(h, h - 1):
                    hi_part(act, "b", i, N1 + u - 1, L0A)
                next_part(hi_part, act, i, u, L0A, None)
                if exists(h, h - 1):
                    turned(h - 1)
                act.wait_ge(l0["sh"], h + 1)
                nc.scalar.activation(pr[:, u, :], st, ACT.Exp, scale=T ** -0.5).then_inc(l0["e"], 1)
                if exists(h, h - 1):
                    after(h - 1, 1 - u)

            for u in range(2):
                head(0, u)
            with act.Fori(1, H // 2 - 1) as i:
                for u in range(2):
                    head(i, u)
            for u in range(2):
                head(H // 2 - 1, u)
            if 6 > 1:
                hi_part(act, "a", 0, N1 + H, L0F)
            hi_part(act, "b", 0, N1 + H - 1, L0A)
            turned(H - 1)
            after(H - 1, 1)

        STEPS0 = 5

        def groups(ap, n=8):
            return ap.rearrange("p (g k) -> p g k", g=n)

        def wide(ap, n, k):
            return ap.unsqueeze(2).broadcast_to([P, n, k])

        def l0a_dve(dve):
            ln_dve(dve, 1)
            c = Count(0)
            dve.wait_ge(l0["lam"], 2)
            for k in range(3):
                if k == 0:
                    nc.vector.tensor_scalar(lam[:], lam[:], 1.0, None, ALU.add).then_inc(l0["dve"], 1)
                elif k == 1:
                    nc.vector.reciprocal(lam[:], lam[:]).then_inc(l0["dve"], 1)
                else:
                    nc.vector.tensor_scalar(lam[:], lam[:], -1.0, None, ALU.mult).then_inc(l0["dve"], 1)
                dve.wait_ge(l0["dve"], c.up())

            def after(h, u):
                dve.wait_ge(l0["ohi"], h + 1)
                nc.vector.tensor_tensor(by_batch(ot_lo[:, u, 0, :]), banks45(), by_batch(ot_hi[:, u, 0, :]).bitcast(F32), ALU.subtract).then_inc(l0["olo"], 1)

            def head(h, u):
                c = Count(3 + STEPS0 * h)
                dve.wait_ge(a_used, h + N1 + 1)
                if exists(h, h - 2):
                    dve.wait_ge(l0["pv"], h - 1)
                nc.vector.tensor_copy(vh[:, u, :, :].rearrange("p t d -> p (t d)"), ps[:, 2, :]).then_inc(l0["ve"], 1)
                dve.wait_ge(l0["s"], h + 1)
                nc.vector.tensor_tensor(st.rearrange("p (f g k) -> p f g k", f=2, g=4), ps[:, 0:2, 0:256].rearrange("p f (g k) -> p f g k", g=4),
                                        mask[:].unsqueeze(1).unsqueeze(1).broadcast_to([P, 2, 4, T]), ALU.add).then_inc(l0["se"], 1)
                dve.wait_ge(l0["se"], h + 1)
                nc.vector.tensor_reduce(mx[:], groups(st), AX.X, ALU.max).then_inc(l0["dve"], 1)
                dve.wait_ge(l0["dve"], c.up())
                nc.vector.tensor_tensor(groups(st), groups(st), wide(mx[:], 8, T), ALU.subtract).then_inc(l0["sh"], 1)
                dve.wait_ge(l0["e"], h + 1)
                nc.vector.tensor_reduce(sm[:], groups(pr[:, u, :]), AX.X, ALU.add).then_inc(l0["dve"], 1)
                dve.wait_ge(l0["dve"], c.up())
                nc.vector.reciprocal(rc[:], sm[:]).then_inc(l0["dve"], 1)
                dve.wait_ge(l0["dve"], c.up())
                nc.vector.tensor_scalar(rc[:, 4:8], rc[:, 4:8], lam[:, bass.ds(h, 1)], None, ALU.mult).then_inc(l0["dve"], 1)
                dve.wait_ge(l0["dve"], c.up())
                nc.vector.tensor_tensor(groups(pr[:, u, :]), groups(pr[:, u, :]), wide(rc[:], 8, T), ALU.mult).then_inc(l0["dve"], 1)
                dve.wait_ge(l0["dve"], c.up())
                assert c.n == STEPS0
                nc.vector.tensor_tensor(dd[:, u, :], pr[:, u, 0:256], pr[:, u, 256:512], ALU.add).then_inc(l0["d"], 1)
                if exists(h, h - 1):
                    after(h - 1, 1 - u)

            for u in range(2):
                head(u, u)
            with dve.Fori(1, H // 2) as i:
                for u in range(2):
                    head(2 * i + u, u)
            after(H - 1, 1)
            add_y(dve, 1, (b_used, N1 + H))

        RSTEPS = 7

        def route_pe(pe, k):
            for t in range(NT):
                for c in range(C2):
                    last = mm3(ps[:, 6, 8 * t:8 * t + 8], xt(c, t * P, P), (gate_hi[:, k, c, :], gate_lo[:, k, c, :]), c == 0, c == 1)
            last.then_inc(ff["lg"], 1)

        def route_act(act, k):
            if k == 0:
                act.wait_ge(consts, CONSTS)
                nc.scalar.activation(gate_hi[:].rearrange("p a b e -> p (a b e)"), gate[:].rearrange("p a b e -> p (a b e)"), ACT.Copy).then_inc(ff["ghi"], 1)
            act.wait_ge(ff["shift"], k + 1)
            nc.scalar.activation(sh[:], sh[:], ACT.Exp).then_inc(ff["e"], 1)

        def route_dve(dve, k):
            c = Count(RSTEPS * k)
            step = ff["dve"]
            dve.wait_ge(ff["lg"], k + 1)
            nc.vector.memset(lg[:, :, 8:16], SENT)
            nc.vector.tensor_copy(lg[:, :, 0:8], ps[:, 6, 0:8 * NT].rearrange("p (t e) -> p t e", t=NT)).then_inc(step, 1)
            dve.wait_ge(step, c.up())
            for t in range(NT):
                last = nc.vector.max(top8[:, t, :], lg[:, t, :])
            last.then_inc(step, 1)
            dve.wait_ge(step, c.up())
            nc.vector.tensor_tensor(sh[:], lg[:, :, 0:8], top8[:, :, 0:1].broadcast_to([P, NT, 8]), ALU.subtract).then_inc(ff["shift"], 1)
            nc.vector.memset(top8[:, :, 2:8], SENT).then_inc(step, 1)
            dve.wait_ge(step, c.up())
            for t in range(NT):
                last = nc.vector.match_replace(rep[:, t, :], top8[:, t, :], lg[:, t, :], -SENT)
            last.then_inc(step, 1)
            dve.wait_ge(step, c.up())
            nc.vector.tensor_tensor(sel[:], rep[:, :, 0:8], lg[:, :, 0:8], ALU.not_equal).then_inc(step, 1)
            dve.wait_ge(step, c.up())
            dve.wait_ge(ff["e"], k + 1)
            nc.vector.tensor_tensor(sel[:], sel[:], sh[:], ALU.mult).then_inc(step, 1)
            dve.wait_ge(step, c.up())
            nc.vector.tensor_reduce(ssum[:], sel[:], AX.X, ALU.add).then_inc(step, 1)
            dve.wait_ge(step, c.up())
            assert c.n == RSTEPS
            nc.vector.reciprocal(ssum[:], ssum[:]).then_inc(ff["comb"], 1)
            dve.wait_ge(ff["comb"], 2 * k + 1)
            nc.vector.tensor_tensor(comb[:, 0:8, :].rearrange("p e t -> p t e"), sel[:], wide(ssum[:], NT, 8), ALU.mult).then_inc(ff["comb"], 1)

        def ffn_up(pe, n, m, u):
            pe.wait_ge(a_split, n + 1)
            if exists(m, m - 2):
                pe.wait_ge(ff["h"], m - 1)
            for k in range(2):
                for c in range(C2):
                    last = mm3(ps[:, 2 * u + k, :], wa(u, 2 * P * k + c * P, P), (xt_hi[:, c, :], xt_lo[:, c, :]), c == 0, c == 1)
                last.then_inc(ff["g"] if k == 0 else a_used, 1)

        def ffn_down(m, u, bank, r0, r1, first, final):
            for t in range(NT):
                o = (h_hi[r0:r1, u, t * P:(t + 1) * P], h_lo[r0:r1, u, t * P:(t + 1) * P])
                last = mm3(ps[:, bank + t // 2, (t % 2) * D:(t % 2 + 1) * D], o, wb(u, 0, D, r0, r1),
                           first and t % 2 == 0, final and t % 2 == 1, skip_group_check=True)
            return last

        def ffn_act(act, m, u):
            act.wait_ge(ff["g"], m + 1)
            if exists(m, m - 2):
                act.wait_ge(ff["h"], m - 1)
            nc.scalar.activation(sg[:, u, :], ps[:, 2 * u, :], ACT.Silu).then_inc(ff["sg"], 1)

        def ffn_act_hi(act, m, u, nb_used):
            act.wait_ge(ff["h"], m + 1)
            if nb_used is not None:
                act.wait_ge(b_used, nb_used)
            nc.scalar.activation(h_hi[:, u, :], hh[:, u, :], ACT.Copy).then_inc(ff["hhi"], 1)

        def ffn_dve(dve, n, m, u, old):
            dve.wait_ge(ff["sg"], m + 1)
            dve.wait_ge(a_used, n + 1)
            if exists(m, m - 2):
                dve.wait_ge(ff["hlo"], m - 1)
            nc.vector.tensor_tensor(hh[:, u, :], sg[:, u, :], ps[:, 2 * u + 1, :], ALU.mult).then_inc(ff["h"], 1)
            dve.wait_ge(ff["hhi"], m + 1)
            nc.vector.tensor_tensor(h_lo[:, u, :], hh[:, u, :], h_hi[:, u, :].bitcast(F32), ALU.subtract).then_inc(ff["hlo"], 1)

        def ffn_add(dve, bank, expert, used, xstep):
            dve.wait_ge(b_used, used)
            for t in range(NT):
                last = nc.vector.scalar_tensor_tensor(x[:, t, :], ps[:, bank + t // 2, (t % 2) * D:(t % 2 + 1) * D],
                                                      comb[:, bass.ds(expert, 1), t], x[:, t, :], ALU.mult, ALU.add)
            last.then_inc(ff["ev"], 1)
            dve.wait_ge(ff["ev"], xstep)

        N2 = L0F[0]

        def l0f_pe(pe):
            ln_pe(pe, 2)
            pe.wait_ge(ff["glo"], 1)
            pe.wait_ge(ln_lo, 6)
            route_pe(pe, 0)

            def down(m, u):
                pe.wait_ge(ff["hlo"], m + 1)
                pe.wait_ge(b_split, m + N2 + 1)
                if exists(m, m - 2):
                    pe.wait_ge(ff["ev"], m - 1)
                ffn_down(m, u, 4 + 2 * u, 0, P, True, True).then_inc(b_used, 1)

            def chunk(m, u):
                ffn_up(pe, m + N2, m, u)
                if exists(m, m - 1):
                    down(m - 1, 1 - u)

            for u in range(2):
                chunk(u, u)
            with pe.Fori(1, CH0 // 2) as i:
                for u in range(2):
                    chunk(2 * i + u, u)
            down(CH0 - 1, 1)

        def l0f_pool(pool):
            ln_pool(pool, 2)
            lo_part(pool, "a", 0, N2 + 1, L0F)
            lo_parts(pool, L0F, L1P, 2)

        def l0f_act(act):
            hi_part(act, "a", 0, N2 + 1, L0F)
            ln_act(act, 2)
            route_act(act, 0)

            def chunk(i, u):
                m = 2 * i + u
                ffn_act(act, m, u)
                hi_part(act, "b", i, N2 + u, L0F)
                next_part(hi_part, act, i, u, L0F, L1P, 2)
                ffn_act_hi(act, m, u, m + N2 - 1 if exists(m, m - 2) else None)

            peeled(act, CH0, chunk)

        def l0f_dve(dve):
            ln_dve_stats(dve, 2)
            dve.wait_ge(ff["ghi"], 1)
            nc.vector.tensor_tensor(gate_lo[:].rearrange("p a b e -> p (a b e)"), gate[:].rearrange("p a b e -> p (a b e)"),
                                    gate_hi[:].rearrange("p a b e -> p (a b e)").bitcast(F32), ALU.subtract).then_inc(ff["glo"], 1)
            ln_dve_split(dve, 2)
            nc.vector.memset(comb[:, 8:12, :], 1.0)
            route_dve(dve, 0)
            dve.wait_ge(ff["comb"], 2)

            def chunk(m, u):
                ffn_dve(dve, m + N2, m, u, None)
                if exists(m, m - 1):
                    ffn_add(dve, 4 + 2 * (1 - u), m - 1, m + N2, m)

            for u in range(2):
                chunk(u, u)
            with dve.Fori(1, CH0 // 2) as i:
                for u in range(2):
                    chunk(2 * i + u, u)
            ffn_add(dve, 6, CH0 - 1, CH0 + N2, CH0)

        NP, NX = L1P[0], L1X[0]

        def proj_pe(pe, m, u):
            n = m + NP
            pe.wait_ge(a_split, n + 1)
            if exists(m, m - 2):
                pe.wait_ge(l1["qst"], m - 1)
            for c in range(C2):
                last = mm3(ps[:, 4 + u, :], wa(u, c * P, P), (xt_hi[:, c, :], xt_lo[:, c, :]), c == 0, c == 1)
            last.then_inc(a_used, 1)
            pe.wait_ge(b_split, n + 1)
            if exists(m, m - 2):
                pe.wait_ge(l1["kst"], m - 1)
            for j in range(2):
                for c in range(C2):
                    last = mm3(ps[:, 2 * u + j, :], wb(u, c * P, P), (ct_hi[:, c, j * 512:(j + 1) * 512], ct_lo[:, c, j * 512:(j + 1) * 512]), c == 0, c == 1)
            last.then_inc(b_used, 1)

        def proj_keys(act, m):
            act.wait_ge(l1["kst"], m + 1)
            if exists(m, m - 1):
                act.wait_ge(l1["acck"], m)
            nc.scalar.activation(sq[:, 0:1024], kst[:, bass.ds(m, 1), :].rearrange("p a n -> p (a n)"), ACT.Square).then_inc(l1["sqk"], 1)

        def proj_act(act, i, u):
            m = 2 * i + u
            for part in "ab":
                hi_part(act, part, i, NP + u + 1, L1P)
            act.wait_ge(a_used, m + NP + 1)
            if exists(m, m - 1):
                act.wait_ge(l1["accq"], m)
            nc.scalar.activation(sq[:, 1024:1536], ps[:, 4 + u, :], ACT.Square, bias=vec[:, bass.ds(m + QB, 1)]).then_inc(l1["sqq"], 1)
            if exists(m, m - 1):
                proj_keys(act, m - 1)

        def proj_acc(dve, m):
            dve.wait_ge(l1["sqk"], m + 1)
            nc.vector.tensor_tensor(acc[:, 0:1024], acc[:, 0:1024], sq[:, 0:1024], ALU.add).then_inc(l1["acck"], 1)
            dve.wait_ge(l1["acck"], m + 1)

        def proj_dve(dve, m, u):
            dve.wait_ge(l1["sqq"], m + 1)
            nc.vector.tensor_scalar(qst[:, bass.ds(m, 1), :].rearrange("p a n -> p (a n)"), ps[:, 4 + u, :], vec[:, bass.ds(m + QB, 1)], nqk[:, bass.ds(m, 1)],
                                    ALU.add, ALU.mult).then_inc(l1["qst"], 1)
            if exists(m, m - 1):
                proj_acc(dve, m - 1)
            dve.wait_ge(b_used, m + NP + 1)
            nc.vector.tensor_scalar(kst[:, bass.ds(m, 1), :].rearrange("p a n -> p (a n)"), flat(ps[:, 2 * u:2 * u + 2, :]), vec[:, bass.ds(m + KB, 1)], None, ALU.add).then_inc(l1["kst"], 1)

        def key_scores(pe, m, u):
            pe.wait_ge(l1["qn"], m + 1)
            pe.wait_ge(l1["kn"], m + 1)
            if exists(m, m - 2):
                pe.wait_ge(l1["se"], m - 1)
            apart(pe)
            for b in range(B):
                p, g = place(b)
                last = nc.tensor.matmul(ps[T * p:T * (p + 1), u, g * S:(g + 1) * S], qn[:, u, b * T:(b + 1) * T], kn[:, u, b * S:(b + 1) * S], start=True, stop=True)
            last.then_inc(l1["s"], 1)

        def turn_x(pe, h, u):
            pe.wait_ge(l1["p"], h + 1)
            if exists(h, h - 1):
                pe.wait_ge(l1["te"], h)
            for g in range(4):
                last = nc.tensor.transpose(ps[:, 2, g * P:(g + 1) * P], pr[:, u, g * P:(g + 1) * P], ident[:])
            last.then_inc(l1["t"], 1)

        def mix_ctx(pe, h):
            pe.wait_ge(l1["te"], h + 1)
            if exists(h, h - 1):
                pe.wait_ge(l1["ulo"], h)
            apart(pe)
            for c in range(C2):
                for b in range(B):
                    p, g = place(b)
                    last = nc.tensor.matmul(ps[:, 3 + c, b * T:(b + 1) * T], ctx[:, b, c * P:(c + 1) * P], ptx[:, g, T * p:T * (p + 1)], start=True, stop=True)
            last.then_inc(l1["u"], 1)

        def values_x(pe, h, u):
            pe.wait_ge(l1["ulo"], h + 1)
            pe.wait_ge(a_split, h + NX + 1)
            if exists(h, h - 1):
                pe.wait_ge(l1["olo"], h)
            for c in range(C2):
                last = mm3(ps[:, 5, :], wa(u, c * P, P), (u_hi[:, c, :], u_lo[:, c, :]), c == 0, c == 1)
            last.then_inc(a_used, 1)

        def out_x(pe, h, u):
            pe.wait_ge(l1["olo"], h + 1)
            pe.wait_ge(b_split, h + NX + 1)
            y_add(lambda t: (ot_hi[:, u, 0, t * P:(t + 1) * P], ot_lo[:, u, 0, t * P:(t + 1) * P]), wb(u, 0, D), h is H - 1).then_inc(b_used, 1)

        def within(m):
            return not isinstance(m, int) or 0 <= m < H

        def l1x_pe(pe):
            ln_pe(pe, 3)
            pe.wait_ge(ln_lo, 8)
            for u in range(2):
                proj_pe(pe, u, u)
            with pe.Fori(1, H // 2) as i:
                for u in range(2):
                    proj_pe(pe, 2 * i + u, u)
            y_start(R_OB)
            pe.wait_ge(l1["accq"], H)
            pe.wait_ge(l1["acck"], H)
            pe.wait_ge(l1["qst"], H)
            for t in range(NKT + NT):
                last = nc.tensor.matmul(ps[:, 2, t:t + 1], acc[:, t * P:(t + 1) * P], ones[:, 0:1], start=True, stop=True)
            last.then_inc(l1["ms"], 1)
            pe.wait_ge(l1["diag"], 1)
            for k in range(3):
                nc.tensor.matmul(ps[:, 2 + k, :], ones[:, :], acc[:, k * 512:(k + 1) * 512], start=True, stop=True).then_inc(l1["ms"], 1)
            pe.wait_ge(l1["rk"], 1)
            pe.wait_ge(l1["placed"], 1)

            def turn(m, u):
                if within(m - 2):
                    turn_x(pe, m - 2, u)
                if within(m):
                    key_scores(pe, m, u)
                if within(m - 3):
                    values_x(pe, m - 3, 1 - u)
                if within(m - 2):
                    mix_ctx(pe, m - 2)
                if within(m - 4):
                    out_x(pe, m - 4, u)

            for m in range(4):
                turn(m, m % 2)
            with pe.Fori(2, H // 2) as i:
                for u in range(2):
                    turn(2 * i + u, u)
            for m in range(H, H + 4):
                turn(m, m % 2)

        def split_x(f, eng, i, u):
            m = 2 * i + u
            if within(m - 2) and exists(m, m - 3):
                f(eng, "a", i, NX + u - 2, L1X)
            elif m is H + 2 and 6 > 4:
                f(eng, "a", i, NX + u - 2, L1A)
            if within(m - 3) and exists(m, m - 4):
                f(eng, "b", i, NX + u - 3, L1X)

        def l1x_pool(pool):
            ln_pool(pool, 3)
            lo_part(pool, "b", 0, NP, L1P)
            nc.gpsimd.memset(acc[:], 0.0).then_inc(l1["acc0"], 1)
            nc.gpsimd.tensor_tensor(nqk[:], vec[:, NQ:NQ + H], vec[:, NK:NK + H], ALU.mult).then_inc(l1["nqk"], 1)

            def proj(i, u):
                m = 2 * i + u
                for part in "ab":
                    lo_part(pool, part, i, NP + u + 1, L1P)
                pool.wait_ge(l1["sqq"], m + 1)
                nc.gpsimd.tensor_tensor(acc[:, 1024:1536], acc[:, 1024:1536], sq[:, 1024:1536], ALU.add).then_inc(l1["accq"], 1)
                pool.wait_ge(l1["accq"], m + 1)

            pool.wait_ge(l1["acc0"], 1)
            for u in range(2):
                proj(0, u)
            with pool.Fori(1, H // 2) as i:
                for u in range(2):
                    proj(i, u)
            pool.wait_ge(l1["var"], 1)
            nc.gpsimd.tensor_tensor(rms[:], rms[:], neghalf[:, 0:1].broadcast_to([P, NKT + NT]), ALU.pow).then_inc(l1["var"], 1)
            pool.wait_ge(l1["rk"], 1)

            def head(m, u):
                if exists(m, m - 2):
                    pool.wait_ge(l1["s"], m - 1)
                nc.gpsimd.tensor_tensor(qn[:, u, :], qst[:, bass.ds(m, 1), :].rearrange("p a n -> p (a n)"), rq, ALU.mult).then_inc(l1["qn"], 1)

            def turn(i, u):
                m = 2 * i + u
                if within(m):
                    head(m, u)
                split_x(lo_part, pool, i, u)

            for i in range(2):
                for u in range(2):
                    turn(i, u)
            with pool.Fori(2, H // 2) as i:
                for u in range(2):
                    turn(i, u)
            for u in range(3):
                turn(H // 2, u)

        def l1x_act(act):
            ln_act(act, 3)
            hi_part(act, "b", 0, NP, L1P)
            for u in range(2):
                proj_act(act, 0, u)
            with act.Fori(1, H // 2) as i:
                for u in range(2):
                    proj_act(act, i, u)
            proj_keys(act, H - 1)

            act.wait_ge(l1["ms"], 4)
            nc.scalar.activation(rq, ps[:, 4, :], ACT.Copy).then_inc(l1["rk"], 1)

            def exps(m, u):
                act.wait_ge(l1["sh"], m + 1)
                if exists(m, m - 2):
                    act.wait_ge(l1["t"], m - 1)
                nc.scalar.activation(pr[:, u, :], st, ACT.Exp, scale=HD ** -0.5).then_inc(l1["e"], 1)

            def turned(h):
                act.wait_ge(l1["t"], h + 1)
                nc.scalar.activation(flat(ptx[:]), ps[:, 2, :], ACT.Copy).then_inc(l1["te"], 1)

            def mixed(h):
                act.wait_ge(l1["u"], h + 1)
                if exists(h, h - 1):
                    act.wait_ge(a_used, h + NX)
                nc.scalar.activation(flat(u_hi[:]), flat(ps[:, 3:5, :]), ACT.Copy).then_inc(l1["uhi"], 1)

            def outs(h, u):
                act.wait_ge(a_used, h + NX + 1)
                if exists(h, h - 2):
                    act.wait_ge(b_used, h + NX - 1)
                nc.scalar.activation(ot_hi[:, u, 0, :], ps[:, 5, :], ACT.Identity, bias=vec[:, bass.ds(h + VB, 1)]).then_inc(l1["ohi"], 1)

            def keys(m, u):
                if exists(m, m - 2):
                    act.wait_ge(l1["s"], m - 1)
                nc.scalar.activation(kn[:, u, :], kst[:, bass.ds(m, 1), :].rearrange("p a n -> p (a n)"), ACT.Copy).then_inc(l1["kn"], 1)

            def turn(i, k):
                m, u = 2 * i + k, k % 2
                if within(m - 2):
                    turned(m - 2)
                if within(m + 1):
                    keys(m + 1, 1 - u)
                split_x(hi_part, act, i, k)
                if within(m - 3):
                    outs(m - 3, 1 - u)
                if within(m):
                    exps(m, u)
                if within(m - 2):
                    mixed(m - 2)

            keys(0, 0)
            for i in range(2):
                for u in range(2):
                    turn(i, u)
            with act.Fori(2, H // 2 - 1) as i:
                for u in range(2):
                    turn(i, u)
            for u in range(5):
                turn(H // 2 - 1, u)

        STEPS1 = 3

        def l1x_dve(dve):
            ln_dve(dve, 3)
            dve.wait_ge(l1["acc0"], 1)
            dve.wait_ge(l1["nqk"], 1)
            for u in range(2):
                proj_dve(dve, u, u)
            with dve.Fori(1, H // 2) as i:
                for u in range(2):
                    proj_dve(dve, 2 * i + u, u)
            proj_acc(dve, H - 1)
            dve.wait_ge(l1["ms"], 1)
            nc.vector.tensor_scalar(rms[:], ps[:, 2, 0:NKT + NT], 1.0 / (H * HD), 1e-6, ALU.mult, ALU.add).then_inc(l1["var"], 1)
            dve.wait_ge(l1["var"], 2)
            nc.vector.tensor_tensor(acc[:].rearrange("p (t n) -> p t n", n=P), ident[:].unsqueeze(1).broadcast_to([P, NKT + NT, P]),
                                    rms[:].unsqueeze(2).broadcast_to([P, NKT + NT, P]), ALU.mult).then_inc(l1["diag"], 1)
            dve.wait_ge(l1["ms"], 3)
            for p in range(2):
                r = slice(T * p, T * (p + 1))
                last = nc.vector.tensor_copy(rk[r].rearrange("p (G e) k -> p G e k", e=2), ps[r, 2:4, :].rearrange("p G (q e k) -> p q G e k", q=2, e=2)[:, p])
            last.then_inc(l1["placed"], 1)
            dve.wait_ge(l1["placed"], 1)

            def scores(m, u):
                c = Count(STEPS1 * m)
                dve.wait_ge(l1["s"], m + 1)
                nc.vector.tensor_tensor(st, ps[:, u, :], rk.rearrange("p g k -> p (g k)"), ALU.mult).then_inc(l1["se"], 1)
                dve.wait_ge(l1["se"], m + 1)
                nc.vector.tensor_reduce(mx[:, 0:4], groups(st, 4), AX.X, ALU.max).then_inc(l1["dve"], 1)
                dve.wait_ge(l1["dve"], c.up())
                nc.vector.tensor_tensor(groups(st, 4), groups(st, 4), wide(mx[:, 0:4], 4, S), ALU.subtract).then_inc(l1["sh"], 1)

            def weights(m, u):
                c = Count(STEPS1 * m + 1)
                dve.wait_ge(l1["e"], m + 1)
                nc.vector.tensor_reduce(sm[:, 0:4], groups(pr[:, u, :], 4), AX.X, ALU.add).then_inc(l1["dve"], 1)
                dve.wait_ge(l1["dve"], c.up())
                nc.vector.reciprocal(rc[:, 0:4], sm[:, 0:4]).then_inc(l1["dve"], 1)
                dve.wait_ge(l1["dve"], c.up())
                nc.vector.tensor_tensor(groups(pr[:, u, :], 4), groups(pr[:, u, :], 4), wide(rc[:, 0:4], 4, S), ALU.mult).then_inc(l1["p"], 1)

            def mixed(h):
                dve.wait_ge(l1["uhi"], h + 1)
                nc.vector.tensor_tensor(flat(u_lo[:]), flat(ps[:, 3:5, :]), flat(u_hi[:]).bitcast(F32), ALU.subtract).then_inc(l1["ulo"], 1)

            def outs(h, u):
                dve.wait_ge(l1["ohi"], h + 1)
                nc.vector.scalar_tensor_tensor(ot_lo[:, u, 0, :], ps[:, 5, :], vec[:, bass.ds(h + VB, 1)], ot_hi[:, u, 0, :].bitcast(F32), ALU.add, ALU.subtract).then_inc(l1["olo"], 1)

            def turn(m, u):
                if within(m):
                    scores(m, u)
                if within(m - 3):
                    outs(m - 3, 1 - u)
                if within(m):
                    weights(m, u)
                if within(m - 2):
                    mixed(m - 2)

            for m in range(4):
                turn(m, m % 2)
            with dve.Fori(2, H // 2) as i:
                for u in range(2):
                    turn(2 * i + u, u)
            for m in range(H, H + 3):
                turn(m, m % 2)
            add_y(dve, 2, (b_used, NX + H))

        NA = L1A[0]

        def l1a_project(pe, j, u):
            pe.wait_ge(a_split, j + NA + 1)
            for a in range(2):
                if exists(j, j - 1):
                    pe.wait_ge(la["qe"], j)
                for c in range(C2):
                    last = mm3(ps[:, a, :], wa(u, 2 * P * a + c * P, P), (xt_hi[:, c, :], xt_lo[:, c, :]), c == 0, c == 1)
                last.then_inc(la["q"] if a == 0 else a_used, 1)

        def l1a_scores(pe, j):
            pe.wait_ge(la["qe"], j + 1)
            if exists(j, j - 1):
                pe.wait_ge(la["se"], j)
            apart(pe)
            for b in range(B):
                cols = slice(b * T, (b + 1) * T)
                nc.tensor.matmul(ps[:, 3, cols], qc[:, b, :, :].rearrange("p a k -> p (a k)"), krot[:, 0, cols], start=True, stop=False)
                last = nc.tensor.matmul(ps[:, 3, cols], qsn[:, b, :, :].rearrange("p a k -> p (a k)"), krot[:, 1, cols], start=False, stop=True)
            last.then_inc(la["s"], 1)

        def l1a_turn(pe, j, u):
            pe.wait_ge(la["p"], j + 1)
            if exists(j, j - 1):
                pe.wait_ge(la["te"], j)
            for k in range(NT):
                last = nc.tensor.transpose(ps[:, 2, k * P:(k + 1) * P], pr[:, u, k * P:(k + 1) * P], ident[:])
            last.then_inc(la["t"], 1)

        def l1a_pv(pe, j, u):
            pe.wait_ge(la["te"], j + 1)
            if exists(j, j - 1):
                pe.wait_ge(la["olo"], j)
            apart(pe)
            for b in range(B):
                k0 = T * (b % 2)
                last = nc.tensor.matmul(ps[:, 4 + b % 2, (b // 2) * P:(b // 2 + 1) * P], lat[k0:k0 + T, b // 2, :], dtl[k0:k0 + T, b // 2, :], start=True, stop=True)
            last.then_inc(la["pv"], 1)

        def l1a_out(pe, j, u, a, final=False):
            if a == 0:
                pe.wait_ge(la["olo"], j + 1)
                pe.wait_ge(b_split, j + NA + 1)
            last = y_add(lambda t: (ot_hi[:, u, a, t * P:(t + 1) * P], ot_lo[:, u, a, t * P:(t + 1) * P]), wb(u, a * D, D), final)
            if a == 1:
                last.then_inc(b_used, 1)

        def l1a_step(pe, j, u):
            l1a_project(pe, j, u)
            if exists(j, j - 2):
                l1a_out(pe, j - 2, u, 0)
            if exists(j, j - 1):
                l1a_turn(pe, j - 1, 1 - u)
            if exists(j, j - 2):
                l1a_out(pe, j - 2, u, 1)
            if exists(j, j - 1):
                l1a_pv(pe, j - 1, 1 - u)
            l1a_scores(pe, j)

        def l1a_pe(pe):
            ln_pe(pe, 4)
            y_start(R_PB)
            pe.wait_ge(ln_lo, 10)
            pe.wait_ge(la["wlo"], 1)
            for c in range(C2):
                last = mm3(ps[:, 0, :], (wl_hi[:, c, :], wl_lo[:, c, :]), (xt_hi[:, c, :], xt_lo[:, c, :]), c == 0, c == 1)
            last.then_inc(la["lt"], 1)
            nc.tensor.matmul(ps[:, 1, :], ones[0:1, :], row[:, R_LB:R_LB + HD].unsqueeze(1).broadcast_to([1, NT, HD]), start=True, stop=False, skip_group_check=True)
            for t in range(NT):
                for c in range(C2):
                    last = mm3(ps[:, 1, t * HD:(t + 1) * HD], xt(c, t * P, P), (wl_hi[:, c, :], wl_lo[:, c, :]), False, t == NT - 1 and c == 1, skip_group_check=True)
            last.then_inc(la["lt"], 1)
            pe.wait_ge(la["lte"], 1)
            nc.tensor.matmul(ps[:, 2, :], rotm[:], lt[:], start=True, stop=True).then_inc(la["rot"], 1)
            pe.wait_ge(la["kr"], 1)
            nc.tensor.matmul(ps[:, 2, :], rotm[:], krot[:, 0, :], start=True, stop=True).then_inc(la["rot"], 1)
            pe.wait_ge(la["late"], 1)
            pe.wait_ge(la["krot"], 1)
            for u in range(2):
                l1a_step(pe, u, u)
            with pe.Fori(1, H // 4) as i:
                for u in range(2):
                    l1a_step(pe, 2 * i + u, u)
            l1a_out(pe, H // 2 - 2, 0, 0)
            l1a_turn(pe, H // 2 - 1, 1)
            l1a_out(pe, H // 2 - 2, 0, 1)
            l1a_pv(pe, H // 2 - 1, 1)
            for a in range(2):
                l1a_out(pe, H // 2 - 1, 1, a, final=a == 1)

        def l1a_pool(pool):
            ln_pool(pool, 4)
            lo_part(pool, "a", 0, NA + 1, L1A)
            lo_parts(pool, L1A, None, 2)

        def banks45f(a):
            return ps[:, 4:6, :].rearrange("p e (b a k) -> p a e b k", a=2, k=T)[:, a]

        def l1a_act(act):
            ln_act(act, 4)
            nc.scalar.activation(flat(wl_hi[:]), flat(wl[:]), ACT.Copy).then_inc(la["whi"], 1)
            act.wait_ge(la["lt"], 1)
            nc.scalar.activation(lt[:], ps[:, 0, :], ACT.Identity, bias=vec[:, LB:LB + 1]).then_inc(la["lte"], 1)
            act.wait_ge(la["lt"], 2)
            nc.scalar.activation(lat[:].rearrange("p t d -> p (t d)"), ps[:, 1, :], ACT.Copy).then_inc(la["late"], 1)

            def after(j, u):
                act.wait_ge(la["t"], j + 1)
                nc.scalar.activation(flat(dtl[:]), ps[:, 2, :], ACT.Copy).then_inc(la["te"], 1)
                act.wait_ge(la["pv"], j + 1)
                if exists(j, j - 2):
                    act.wait_ge(b_used, j + NA - 1)
                for a in range(2):
                    last = nc.scalar.activation(by_batch(ot_hi[:, u, a, :]), banks45f(a), ACT.Copy)
                last.then_inc(la["ohi"], 1)

            def step(i, u):
                j = 2 * i + u
                if exists(j, j - 1):
                    hi_part(act, "b", i, NA + u - 1, L1A)
                next_part(hi_part, act, i, u, L1A, None)
                if exists(j, j - 1):
                    after(j - 1, 1 - u)
                act.wait_ge(la["sh"], j + 1)
                nc.scalar.activation(pr[:, u, :], st, ACT.Exp, scale=HD ** -0.5).then_inc(la["e"], 1)

            peeled(act, H // 2, step)
            hi_part(act, "b", 0, NA + H // 2 - 1, L1A)
            after(H // 2 - 1, 1)

        STEPSA = 3

        def l1a_dve(dve):
            ln_dve(dve, 4)
            dve.wait_ge(la["whi"], 1)
            nc.vector.tensor_tensor(flat(wl_lo[:]), flat(wl[:]), flat(wl_hi[:]).bitcast(F32), ALU.subtract).then_inc(la["wlo"], 1)
            rc_, rs_ = (rope[:, k, :].unsqueeze(1).broadcast_to([P, B, T]) for k in range(2))

            def by(ap):
                return ap.rearrange("p (b k) -> p b k", k=T)

            dve.wait_ge(la["lte"], 1)
            nc.vector.tensor_tensor(by(lcos[:]), by(lt[:]), rc_, ALU.mult).then_inc(la["dve"], 1)
            dve.wait_ge(la["rot"], 1)
            nc.vector.tensor_tensor(by(lsin[:]), by(ps[:, 2, :]), rs_, ALU.mult).then_inc(la["dve"], 1)
            dve.wait_ge(la["dve"], 2)
            nc.vector.tensor_tensor(krot[:, 0, :], lcos[:], lsin[:], ALU.subtract).then_inc(la["kr"], 1)
            dve.wait_ge(la["rot"], 2)
            nc.vector.tensor_copy(krot[:, 1, :], ps[:, 2, :]).then_inc(la["krot"], 1)

            def queries(j):
                if exists(j, j - 1):
                    dve.wait_ge(la["s"], j)
                for a in range(2):
                    dve.wait_ge(la["q"] if a == 0 else a_used, j + 1 if a == 0 else j + NA + 1)
                    bias = vec[:, bass.ds(2 * j + (DB + a), 1)]
                    nc.vector.scalar_tensor_tensor(qc[:, :, a, :], by(ps[:, a, :]), bias, rc_, ALU.add, ALU.mult)
                    last = nc.vector.scalar_tensor_tensor(qsn[:, :, a, :], by(ps[:, a, :]), bias, rs_, ALU.add, ALU.mult)
                last.then_inc(la["qe"], 1)

            def after(j, u):
                dve.wait_ge(la["ohi"], j + 1)
                for a in range(2):
                    last = nc.vector.tensor_tensor(by_batch(ot_lo[:, u, a, :]), banks45f(a),
                                                   by_batch(ot_hi[:, u, a, :]).bitcast(F32), ALU.subtract)
                last.then_inc(la["olo"], 1)

            def step(j, u):
                c = Count(2 + STEPSA * j)
                queries(j)
                if exists(j, j - 1):
                    after(j - 1, 1 - u)
                dve.wait_ge(la["s"], j + 1)
                nc.vector.tensor_tensor(groups(st), groups(ps[:, 3, :]), mask[:].unsqueeze(1).broadcast_to([P, 8, T]), ALU.add).then_inc(la["se"], 1)
                dve.wait_ge(la["se"], j + 1)
                nc.vector.tensor_reduce(mx[:], groups(st), AX.X, ALU.max).then_inc(la["dve"], 1)
                dve.wait_ge(la["dve"], c.up())
                nc.vector.tensor_tensor(groups(st), groups(st), wide(mx[:], 8, T), ALU.subtract).then_inc(la["sh"], 1)
                dve.wait_ge(la["e"], j + 1)
                nc.vector.tensor_reduce(sm[:], groups(pr[:, u, :]), AX.X, ALU.add).then_inc(la["dve"], 1)
                dve.wait_ge(la["dve"], c.up())
                nc.vector.reciprocal(rc[:], sm[:]).then_inc(la["dve"], 1)
                dve.wait_ge(la["dve"], c.up())
                assert c.n == STEPSA
                nc.vector.tensor_tensor(groups(pr[:, u, :]), groups(pr[:, u, :]), wide(rc[:], 8, T), ALU.mult).then_inc(la["p"], 1)

            for u in range(2):
                step(u, u)
            with dve.Fori(1, H // 4) as i:
                for u in range(2):
                    step(2 * i + u, u)
            after(H // 2 - 1, 1)
            add_y(dve, 3, (b_used, NA + H // 2))

        NF = L1F[0]
        HALF = 64

        def experts_of(m):
            mid = CH1 // 2
            if m == mid:
                return [(0, 0, HALF, False, True), (1, HALF, P, True, False)]
            return [(0, 0, P, m == 0, False)] if m < mid else [(1, 0, P, False, m == CH1 - 1)]

        def l1f_pe(pe):
            ln_pe(pe, 5)
            pe.wait_ge(ln_lo, 12)
            route_pe(pe, 1)

            def down(i, k):
                m, u, pair = 2 * CH1 * i + CH0 + k, k % 2, k // CH1
                pe.wait_ge(ff["hlo"], m + 1)
                pe.wait_ge(b_split, m + (NF - CH0) + 1)
                for e, r0, r1, first, final in experts_of(k % CH1):
                    if first:
                        pe.wait_ge(ff["ev"], 4 * i + 2 * pair + e + (CH0 - 1))
                    last = ffn_down(m, u, 4 + 2 * e, r0, r1, first, final)
                last.then_inc(b_used, 1)

            with pe.Fori(0, 2) as i:
                for k in range(2 * CH1):
                    m = 2 * CH1 * i + CH0 + k
                    ffn_up(pe, m + (NF - CH0), m, k % 2)
                    if k:
                        down(i, k - 1)
                down(i, 2 * CH1 - 1)

        def l1f_pool(pool):
            ln_pool(pool, 5)
            with pool.Fori(0, 2) as i:
                for k in range(2):
                    lo_part(pool, "a", i, NF + k, L1F, 2 * CH1)
                for k in range(2 * CH1):
                    lo_part(pool, "b", i, NF + k, L1F, 2 * CH1)
                    if k < 2 * CH1 - 2:
                        lo_part(pool, "a", i, NF + k + 2, L1F, 2 * CH1)

        def l1f_act(act):
            ln_act(act, 5)
            route_act(act, 1)
            with act.Fori(0, 2) as i:
                for k in range(2):
                    hi_part(act, "a", i, NF + k, L1F, 2 * CH1)
                for k in range(2 * CH1):
                    m = 2 * CH1 * i + CH0 + k
                    ffn_act(act, m, k % 2)
                    hi_part(act, "b", i, NF + k, L1F, 2 * CH1)
                    if k < 2 * CH1 - 2:
                        hi_part(act, "a", i, NF + k + 2, L1F, 2 * CH1)
                    ffn_act_hi(act, m, k % 2, m + (NF - CH0) - 1)

        def l1f_dve(dve):
            ln_dve(dve, 5)
            route_dve(dve, 1)
            dve.wait_ge(ff["comb"], 4)
            with dve.Fori(0, 2) as i:
                for k in range(2 * CH1):
                    m = 2 * CH1 * i + CH0 + k
                    ffn_dve(dve, m + (NF - CH0), m, k % 2, None)
                    if (k - 1) % CH1 == CH1 // 2 or (k and k % CH1 == 0):
                        e = 2 * (k // CH1) if k % CH1 else 2 * (k // CH1) - 1
                        ffn_add(dve, 4 + 2 * (e % 2), 4 * i + e, m + (NF - CH0), 4 * i + e + (CH0 + 1))
                ffn_add(dve, 6, 4 * i + 3, 2 * CH1 * i + 2 * CH1 + NF, 4 * i + 3 + (CH0 + 1))

        block = top.enter_context(nc.Block())

        @block.sync
        def _(sp):
            setup_sync(sp)
            for src, stage in zip((w_l0a, w_l0f, w_l1p, w_l1x, w_l1a, w_l1f)[:6], (L0A, L0F, L1P, L1X, L1A, L1F)):
                load_stage(sp, src, stage)
            sp.wait_ge(ff["ev"], CH0 + E1)
            sp.dma_start(out, x[:]).then_inc(stored, 16)
            sp.wait_ge(stored, 16)

        @block.gpsimd
        def _(pool):
            setup_pool(pool)
            ln_pool(pool, 0)
            l0x_pool(pool)
            l0a_pool(pool)
            l0f_pool(pool)
            l1x_pool(pool)
            l1a_pool(pool)
            l1f_pool(pool)

        @block.scalar
        def _(act):
            l0x_act(act)
            l0a_act(act)
            l0f_act(act)
            l1x_act(act)
            l1a_act(act)
            l1f_act(act)

        @block.vector
        def _(dve):
            l0x_dve(dve)
            l0a_dve(dve)
            l0f_dve(dve)
            l1x_dve(dve)
            l1a_dve(dve)
            l1f_dve(dve)

        @block.tensor
        def _(pe):
            l0x_pe(pe)
            l0a_pe(pe)
            l0f_pe(pe)
            l1x_pe(pe)
            l1a_pe(pe)
            l1f_pe(pe)


def kernel(**inputs):
    import numpy as _np
    import concourse.bacc as _bacc
    from concourse import mybir as _mybir
    from concourse.bass_utils import run_bass_kernel_spmd as _run

    g = {k: _np.ascontiguousarray(v) for k, v in inputs.items()}
    cat = _np.concatenate

    def rows_to_partitions(w):
        return w.reshape(C2, P, -1).transpose(1, 0, 2)

    def by_head(w, width):
        n = w.shape[1] // width
        return w.reshape(C2, P, n, width).transpose(2, 1, 0, 3).reshape(n, P, C2 * width)

    def head_rows(w, n):
        return w.reshape(n, P, D)

    wkv = g["L0_xattn_Wkv"]
    w_x0 = rows_to_partitions(cat([g["L0_xattn_Wq"], wkv, g["L0_xattn_Wp"]], axis=1))
    w_l0a = cat([by_head(g["L0_attn_Wq"], HD), by_head(g["L0_attn_Wk"], HD), by_head(g["L0_attn_Wv"], HD), head_rows(g["L0_attn_Wo"], H)], axis=2)
    gu = g["L0_ffn_w_gate_up"].reshape(E0, C2, P, 2, P).transpose(0, 2, 3, 1, 4).reshape(E0, P, 512)
    sgu = g["L0_ffn_w_sh_gate_up"].reshape(C2, P, 2, 4, P).transpose(3, 1, 2, 0, 4).reshape(4, P, 512)
    w_l0f = cat([cat([gu, g["L0_ffn_w_down"]], axis=2), cat([sgu, head_rows(g["L0_ffn_w_sh_down"], 4)], axis=2)], axis=0)
    w_l1p = cat([by_head(g["L1_xattn_q_w"], HD), by_head(g["L1_xattn_ki_w"], HD)], axis=2)
    w_l1x = cat([by_head(g["L1_xattn_vi_w"], HD), head_rows(g["L1_xattn_o_w"], H)], axis=2)
    wd = g["L1_attn_W_d"].reshape(C2, P, H // 2, 2, HD).transpose(2, 1, 3, 0, 4).reshape(H // 2, P, 512)
    wpr = g["L1_attn_W_proj"].reshape(H // 2, 2, P, D).transpose(0, 2, 1, 3).reshape(H // 2, P, 512)
    w_l1a = cat([wd, wpr], axis=2)
    n1 = 4 * CH1

    def turned_rows(w):
        return w.reshape(n1, P, C2, P).transpose(0, 3, 2, 1).reshape(n1, P, 2 * P)

    w_l1f = cat([turned_rows(g["L1_ffn_w1"]), turned_rows(g["L1_ffn_w3"]), g["L1_ffn_w2"].transpose(0, 2, 1).reshape(n1, P, D)], axis=2)
    gates = _np.stack([rows_to_partitions(g["L0_ffn_w_gate"]), rows_to_partitions(g["L1_ffn_Wg"].T)], axis=1)
    cols = [g[k].reshape(H, P).T for k in ("L1_xattn_q_b", "L1_xattn_ki_b", "L1_xattn_vi_b", "L1_xattn_nq_s", "L1_xattn_nki_s", "L1_attn_b_d")]
    vecs = cat(cols + [g["L1_attn_b_latent"].reshape(1, P).T, g["L0_xattn_bkv"][D:].reshape(C2, P).T], axis=1)
    two = [g["L0_xattn_bq"], g["L0_xattn_bkv"][:D], g["L0_xattn_bp"], g["L1_xattn_o_b"], g["L1_attn_b_proj"], g["L1_attn_b_latent"], g["L0_attn_lambda_init"]]
    rows = cat(two).reshape(1, NROW)
    ident = _np.eye(P, dtype=_np.float32)
    key, query = _np.arange(T)[None, :], _np.arange(P)[:, None] % T
    mask = _np.where(key <= query, 0.0, -3.0e38).astype(_np.float32)
    half = HD // 2
    inv = (_np.float32(10000.0) ** (-_np.arange(half, dtype=_np.float32) / _np.float32(half))).astype(_np.float32)
    ang = (_np.arange(T, dtype=_np.float32)[:, None] * inv[None, :]).astype(_np.float32)
    rope = _np.stack([_np.repeat(_np.cos(ang), 2, axis=1).T, _np.repeat(_np.sin(ang), 2, axis=1).T], axis=1).astype(_np.float32)
    rotm = _np.zeros((P, P), _np.float32)
    rotm[_np.arange(0, P, 2), _np.arange(1, P, 2)] = -1.0
    rotm[_np.arange(1, P, 2), _np.arange(0, P, 2)] = 1.0

    named = {
        "x_in": g["x"].reshape(NT, P, D).transpose(1, 0, 2), "ctx_in": g["ctx_2048"].transpose(1, 0, 2), "w_x0": w_x0, "w_l0a": w_l0a, "w_l0f": w_l0f,
        "w_l1p": w_l1p, "w_l1x": w_l1x, "w_l1a": w_l1a, "w_l1f": w_l1f, "gates": gates, "vecs": vecs, "rows": rows,
        "ident_in": ident, "mask_in": mask, "rope_in": rope, "rotm_in": rotm, "wl_in": rows_to_partitions(g["L1_attn_W_latent"]),
    }
    nc = _bacc.Bacc("TRN2", target_bir_lowering=False, num_devices=1)
    arrays, args = {}, {}
    for name, a in named.items():
        arrays[name] = _np.ascontiguousarray(a)
        args[name] = nc.dram_tensor(name, arrays[name].shape, _mybir.dt.from_np(arrays[name].dtype), kind="ExternalInput").ap()
    out = nc.dram_tensor("x_out", (NT, P, D), F32, kind="ExternalOutput").ap()
    build(nc, out=out.rearrange("t p d -> p t d"), **args)
    r = _run(nc, [arrays], core_ids=[0])
    return r.results[0]["x_out"].reshape(B, T, D)
```
